# Optimizing a Trainium2 kernel written in Bass

```python
import numpy as np
import jax
import jax.numpy as jnp

def _softmax(x, axis=-1):
    return jax.nn.softmax(x, axis=axis)

def _gelu(x):
    return jax.nn.gelu(x, approximate=True)

def _silu(x):
    return jax.nn.silu(x)

def _sigmoid(x):
    return jax.nn.sigmoid(x)

def _layernorm(x, axis=-1, eps=1e-05):
    m = jnp.mean(x, axis=axis, keepdims=True)
    v = jnp.var(x, axis=axis, keepdims=True)
    return (x - m) / jnp.sqrt(v + eps)

def _scatter_add(tgt, idx, src, axis=0):
    return tgt.at[idx].add(src)

def _segment_sum(src, seg, n):
    return jax.ops.segment_sum(src, seg, n)
kernel_name = 'mk_recurrent_d4_jaxref_r8_e2b9bb'

def setup_inputs(seed: int=0):
    np.random.seed(seed)
    _w = jnp.asarray

    def _L0_attn_setup():
        import jax, jax.numpy as jnp
        import numpy as np
        NUM_HEADS = 8
        ROPE_BASE = 10000.0

        def _rope(x):
            b, n, c = x.shape
            k_max = c // 2
            theta = 1.0 / ROPE_BASE ** (jnp.arange(k_max, dtype=jnp.float32) / k_max)
            angles = jnp.arange(n, dtype=jnp.float32)[:, None] * theta
            cos = jnp.cos(angles)
            sin = jnp.sin(angles)
            xr = x[..., 0::2]
            xi = x[..., 1::2]
            pr = cos * xr - sin * xi
            pi = cos * xi + sin * xr
            return jnp.concatenate([pr, pi], axis=-1)
        key = jax.random.key(seed)
        ks = jax.random.split(key, 5)
        b, n, c = (4, 512, 128)
        x = jax.random.normal(ks[0], (b, n, c), dtype=jnp.float32)
        qk_w = jax.random.normal(ks[1], (c, 2 * c), dtype=jnp.float32) * (1.0 / np.sqrt(c))
        qk_b = jnp.zeros((2 * c,), dtype=jnp.float32)
        lepe_w = jax.random.normal(ks[2], (3, c, c), dtype=jnp.float32) * (1.0 / np.sqrt(3 * c))
        lepe_b = jnp.zeros((c,), dtype=jnp.float32)
        return {'x': x, 'qk_w': qk_w, 'qk_b': qk_b, 'lepe_w': lepe_w, 'lepe_b': lepe_b}
    _L0_attn_in = _L0_attn_setup()

    def _L0_ffn_setup():
        import jax, jax.numpy as jnp
        import numpy as np
        H = 16
        E = 8
        EPS = 1e-05

        def _layernorm(x, g, b):
            mu = jnp.mean(x, axis=-1, keepdims=True)
            var = jnp.mean(jnp.square(x - mu), axis=-1, keepdims=True)
            return (x - mu) * jax.lax.rsqrt(var + EPS) * g + b
        key = jax.random.key(seed)
        T, B, C = (128, 8, 128)
        ks = jax.random.split(key, 12)
        s = 0.02
        return {'x': jax.random.normal(ks[0], (T, B, C), jnp.float32), 'in_proj_w': jax.random.normal(ks[1], (3 * C, C), jnp.float32) * s, 'in_proj_b': jnp.zeros((3 * C,), jnp.float32), 'out_w': jax.random.normal(ks[2], (C, C), jnp.float32) * s, 'out_b': jnp.zeros((C,), jnp.float32), 'ln1_g': jnp.ones((C,), jnp.float32), 'ln1_b': jnp.zeros((C,), jnp.float32), 'router_w': jax.random.normal(ks[3], (E, C), jnp.float32) * s, 'router_b': jnp.zeros((E,), jnp.float32), 'w1': jax.random.normal(ks[4], (E, C, C), jnp.float32) * s, 'b1': jnp.zeros((E, C), jnp.float32), 'w2': jax.random.normal(ks[5], (E, C, C), jnp.float32) * s, 'b2': jnp.zeros((E, C), jnp.float32), 'ln2_g': jnp.ones((C,), jnp.float32), 'ln2_b': jnp.zeros((C,), jnp.float32)}
    _L0_ffn_in = _L0_ffn_setup()

    def _L1_attn_setup():
        import jax, jax.numpy as jnp
        import numpy as np
        DIM = 128
        QK = 128
        HID = 256
        B, N = (4, 256)
        EPS = 1e-05
        key = jax.random.key(seed)
        ks = jax.random.split(key, 8)
        std = 0.02
        return {'x': jax.random.normal(ks[0], (B, N, DIM), jnp.float32), 'ln_scale': jnp.ones((DIM,), jnp.float32), 'ln_bias': jnp.zeros((DIM,), jnp.float32), 'W_hidden': jax.random.normal(ks[1], (DIM, 2 * HID), jnp.float32) * std, 'b_hidden': jnp.zeros((2 * HID,), jnp.float32), 'W_qk': jax.random.normal(ks[2], (DIM, QK), jnp.float32) * std, 'b_qk': jnp.zeros((QK,), jnp.float32), 'os_weight': jax.random.normal(ks[3], (2, QK), jnp.float32) * std, 'os_bias': jnp.zeros((2, QK), jnp.float32), 'W_out': jax.random.normal(ks[4], (HID, DIM), jnp.float32) * std, 'b_out': jnp.zeros((DIM,), jnp.float32)}
    _L1_attn_in = _L1_attn_setup()

    def _L1_ffn_setup():
        import math
        import jax, jax.numpy as jnp
        import numpy as np
        E = 8
        TOPK = 2
        CF = 1.25
        EPS = 1e-05
        NEG = -1e+30

        def _layer_norm(x, gamma, beta):
            mu = jnp.mean(x, axis=-1, keepdims=True)
            var = jnp.mean((x - mu) ** 2, axis=-1, keepdims=True)
            return (x - mu) * jax.lax.rsqrt(var + EPS) * gamma + beta
        key = jax.random.key(seed)
        ks = jax.random.split(key, 8)
        B, S, H, F = (4, 256, 128, 512)
        hidden_states = jax.random.normal(ks[0], (B, S, H), jnp.float32)
        token_mask = jnp.ones((B, S), jnp.int32)
        Wr = jax.random.normal(ks[1], (H, E), jnp.float32) * 0.001
        br = jnp.zeros((E,), jnp.float32)
        W1 = jax.random.normal(ks[2], (E, H, F), jnp.float32) * (1.0 / np.sqrt(H))
        b1 = jax.random.normal(ks[3], (E, F), jnp.float32) * 0.01
        W2 = jax.random.normal(ks[4], (E, F, H), jnp.float32) * (1.0 / np.sqrt(F))
        b2 = jax.random.normal(ks[5], (E, H), jnp.float32) * 0.01
        gamma = jnp.ones((H,), jnp.float32)
        beta = jnp.zeros((H,), jnp.float32)
        return {'hidden_states': hidden_states, 'Wr': Wr, 'br': br, 'W1': W1, 'b1': b1, 'W2': W2, 'b2': b2, 'gamma': gamma, 'beta': beta, 'token_mask': token_mask}
    _L1_ffn_in = _L1_ffn_setup()

    def _L2_attn_setup():
        import jax, jax.numpy as jnp
        import numpy as np
        import math
        HEAD_SIZE = 64

        def rotate_every_two(x):
            x1 = x[..., ::2]
            x2 = x[..., 1::2]
            return jnp.stack((-x2, x1), axis=-1).reshape(x.shape)

        def rope_table(seq_len, dtype=jnp.float32):
            pos = jnp.arange(seq_len, dtype=jnp.float32)
            inv = 10000.0 ** (jnp.arange(0, HEAD_SIZE, 2, dtype=jnp.float32) / HEAD_SIZE)
            radians = pos[:, None] / inv
            sincos = jnp.stack((jnp.sin(radians), jnp.cos(radians)), axis=-1).reshape(seq_len, -1)
            t = jnp.repeat(sincos, 2, axis=-1)
            return t.astype(dtype)
        key = jax.random.key(seed)
        ks = jax.random.split(key, 7)
        B, S, H = (2, 512, 128)
        sd = 1.0 / math.sqrt(H)
        return {'hidden_states': jax.random.normal(ks[0], (B, S, H), dtype=jnp.float32), 'Wq': jax.random.normal(ks[1], (H, H), dtype=jnp.float32) * sd, 'bq': jax.random.normal(ks[2], (H,), dtype=jnp.float32) * sd, 'Wk': jax.random.normal(ks[3], (H, H), dtype=jnp.float32) * sd, 'bk': jax.random.normal(ks[4], (H,), dtype=jnp.float32) * sd, 'Wv': jax.random.normal(ks[5], (H, H), dtype=jnp.float32) * sd, 'bv': jax.random.normal(ks[6], (H,), dtype=jnp.float32) * sd}
    _L2_attn_in = _L2_attn_setup()

    def _L2_ffn_setup():
        import jax, jax.numpy as jnp
        import numpy as np
        from jax import lax
        T, B, I, M, O = (32, 64, 128, 128, 128)

        def _xavier(key, shape):
            fan_out, fan_in = shape
            limit = float(np.sqrt(6.0 / (fan_in + fan_out)))
            return jax.random.uniform(key, shape, jnp.float32, -limit, limit)
        key = jax.random.key(seed)
        ks = jax.random.split(key, 9)
        x = jax.random.normal(ks[0], (T, B, I), jnp.float32)
        return {'x': x, 'wf': _xavier(ks[1], (M, I)), 'uf': _xavier(ks[2], (M, M)), 'bf': jnp.zeros((M,), jnp.float32), 'wi': _xavier(ks[3], (M, I)), 'ui': _xavier(ks[4], (M, M)), 'bi': jnp.zeros((M,), jnp.float32), 'wc': _xavier(ks[5], (M, I)), 'uc': _xavier(ks[6], (M, M)), 'bc': jnp.zeros((M,), jnp.float32), 'wo': _xavier(ks[7], (O, I)), 'uo': _xavier(ks[8], (O, M)), 'bo': jnp.zeros((O,), jnp.float32), 'in_c': jnp.zeros((M,), jnp.float32)}
    _L2_ffn_in = _L2_ffn_setup()

    def _L3_attn_setup():
        import jax, jax.numpy as jnp
        import numpy as np
        B, L, D, H, E, F, STEPS, TOPK = (2, 128, 128, 16, 8, 256, 3, 2)
        HD = D // H

        def layernorm(x, g, b, eps=1e-05):
            m = jnp.mean(x, -1, keepdims=True)
            v = jnp.var(x, -1, keepdims=True)
            return (x - m) * jax.lax.rsqrt(v + eps) * g + b

        def gated_attention(x, Wqkv, Wout, Wgate):
            b, l, d = x.shape
            qkv = (x @ Wqkv).reshape(b, l, 3, H, HD)
            q, k, v = [jnp.moveaxis(qkv[:, :, i], 1, 2) for i in range(3)]
            attn = jax.nn.softmax(jnp.einsum('bhqd,bhkd->bhqk', q, k) * HD ** (-0.5), axis=-1)
            out = jnp.einsum('bhqk,bhkd->bhqd', attn, v)
            out = jnp.moveaxis(out, 1, 2).reshape(b, l, d)
            return out @ Wout * jax.nn.sigmoid(x @ Wgate)

        def ssm(x, Win, cw, cb, Wout):
            xz = x @ Win
            xs, z = jnp.split(xz, 2, axis=-1)
            xt = jnp.swapaxes(xs, 1, 2)
            y = jax.lax.conv_general_dilated(xt, cw, window_strides=(1,), padding=[(3, 0)], dimension_numbers=('NCH', 'OIH', 'NCH'), feature_group_count=D) + cb[None, :, None]
            xc = jax.nn.silu(jnp.swapaxes(y, 1, 2))
            return xc * jax.nn.sigmoid(z) @ Wout

        def moe(x, Wg, W1, W2, W3):
            b, l, d = x.shape
            flat = x.reshape(-1, d)
            probs = jax.nn.softmax(flat @ Wg, axis=-1)
            topp, topi = jax.lax.top_k(probs, TOPK)
            topp = topp / (jnp.sum(topp, -1, keepdims=True) + 1e-08)
            T = flat.shape[0]
            cw = jnp.zeros((T, E), flat.dtype).at[jnp.arange(T)[:, None], topi].add(topp)
            out = jnp.zeros_like(flat)
            for e in range(E):
                h = jax.nn.silu(flat @ W1[e]) * (flat @ W3[e])
                out = out + cw[:, e:e + 1] * (h @ W2[e])
            return out.reshape(b, l, d)
        key = jax.random.key(seed)
        ks = jax.random.split(key, 16)

        def n(k, shape, scale=0.02):
            return jax.random.normal(k, shape, jnp.float32) * scale
        return dict(x=jax.random.normal(ks[0], (B, L, D), jnp.float32), Wr=n(ks[1], (D, 2)), br=jnp.zeros((2,), jnp.float32), step_bias=jnp.zeros((STEPS,), jnp.float32), ln1_g=jnp.ones((D,), jnp.float32), ln1_b=jnp.zeros((D,), jnp.float32), ln2_g=jnp.ones((D,), jnp.float32), ln2_b=jnp.zeros((D,), jnp.float32), ls1=jnp.full((D,), 1e-05, jnp.float32), ls2=jnp.full((D,), 1e-05, jnp.float32), Wqkv=n(ks[2], (D, 3 * D)), Wout=n(ks[3], (D, D)), Wgate=n(ks[4], (D, D)), Win_ssm=n(ks[5], (D, 2 * D)), conv_w=n(ks[6], (D, 1, 4)), conv_b=jnp.zeros((D,), jnp.float32), Wout_ssm=n(ks[7], (D, D)), Wg=n(ks[8], (D, E)), W1=n(ks[9], (E, D, F)), W2=n(ks[10], (E, F, D)), W3=n(ks[11], (E, D, F)))
    _L3_attn_in = _L3_attn_setup()

    def _L3_ffn_setup():
        import jax, jax.numpy as jnp
        import numpy as np
        B, S, D = (1, 256, 128)
        I = 256
        E = 8
        K = 2
        LIMIT = 7.0
        ALPHA = 1.702
        EPS = 1e-05

        def _swiglu(h):
            x_glu = jnp.minimum(h[..., ::2], LIMIT)
            x_lin = jnp.clip(h[..., 1::2], -LIMIT, LIMIT)
            return x_glu * jax.nn.sigmoid(ALPHA * x_glu) * (x_lin + 1.0)

        def _moe(t, gate_w, gate_b, mlp1_w, mlp1_b, mlp2_w, mlp2_b):
            T = t.shape[0]
            logits = t @ gate_w + gate_b
            top_v, top_i = jax.lax.top_k(logits, K)
            probs = jax.nn.softmax(top_v, axis=-1)
            w = jnp.zeros((T, E), t.dtype).at[jnp.arange(T)[:, None], top_i].set(probs)

            def body(acc, ew):
                w1, b1, w2, b2, we = ew
                h = _swiglu(t @ w1 + b1)
                y = h @ w2 + b2
                return (acc + we[:, None] * y, None)
            acc0 = jnp.zeros((T, t.shape[1]), t.dtype)
            acc, _ = jax.lax.scan(body, acc0, (mlp1_w, mlp1_b, mlp2_w, mlp2_b, w.T))
            return acc
        key = jax.random.key(seed)
        ks = jax.random.split(key, 4)
        s = 0.02
        return {'x': jax.random.normal(ks[0], (B, S, D), jnp.float32), 'norm_scale': jnp.ones((D,), jnp.float32), 'gate_w': jax.random.normal(ks[1], (D, E), jnp.float32) * s, 'gate_b': jnp.zeros((E,), jnp.float32), 'mlp1_w': jax.random.normal(ks[2], (E, D, 2 * I), jnp.float32) * s, 'mlp1_b': jnp.zeros((E, 2 * I), jnp.float32), 'mlp2_w': jax.random.normal(ks[3], (E, I, D), jnp.float32) * s, 'mlp2_b': jnp.zeros((E, D), jnp.float32)}
    _L3_ffn_in = _L3_ffn_setup()
    _d = {'L0_attn_x': _L0_attn_in['x'], 'L0_attn_qk_w': _L0_attn_in['qk_w'], 'L0_attn_qk_b': _L0_attn_in['qk_b'], 'L0_attn_lepe_w': _L0_attn_in['lepe_w'], 'L0_attn_lepe_b': _L0_attn_in['lepe_b'], 'L0_ffn_in_proj_w': _L0_ffn_in['in_proj_w'], 'L0_ffn_in_proj_b': _L0_ffn_in['in_proj_b'], 'L0_ffn_out_w': _L0_ffn_in['out_w'], 'L0_ffn_out_b': _L0_ffn_in['out_b'], 'L0_ffn_ln1_g': _L0_ffn_in['ln1_g'], 'L0_ffn_ln1_b': _L0_ffn_in['ln1_b'], 'L0_ffn_router_w': _L0_ffn_in['router_w'], 'L0_ffn_router_b': _L0_ffn_in['router_b'], 'L0_ffn_w1': _L0_ffn_in['w1'], 'L0_ffn_b1': _L0_ffn_in['b1'], 'L0_ffn_w2': _L0_ffn_in['w2'], 'L0_ffn_b2': _L0_ffn_in['b2'], 'L0_ffn_ln2_g': _L0_ffn_in['ln2_g'], 'L0_ffn_ln2_b': _L0_ffn_in['ln2_b'], 'L1_attn_ln_scale': _L1_attn_in['ln_scale'], 'L1_attn_ln_bias': _L1_attn_in['ln_bias'], 'L1_attn_W_hidden': _L1_attn_in['W_hidden'], 'L1_attn_b_hidden': _L1_attn_in['b_hidden'], 'L1_attn_W_qk': _L1_attn_in['W_qk'], 'L1_attn_b_qk': _L1_attn_in['b_qk'], 'L1_attn_os_weight': _L1_attn_in['os_weight'], 'L1_attn_os_bias': _L1_attn_in['os_bias'], 'L1_attn_W_out': _L1_attn_in['W_out'], 'L1_attn_b_out': _L1_attn_in['b_out'], 'L1_ffn_Wr': _L1_ffn_in['Wr'], 'L1_ffn_br': _L1_ffn_in['br'], 'L1_ffn_W1': _L1_ffn_in['W1'], 'L1_ffn_b1': _L1_ffn_in['b1'], 'L1_ffn_W2': _L1_ffn_in['W2'], 'L1_ffn_b2': _L1_ffn_in['b2'], 'L1_ffn_gamma': _L1_ffn_in['gamma'], 'L1_ffn_beta': _L1_ffn_in['beta'], 'L1_ffn_token_mask': _L1_ffn_in['token_mask'], 'L2_attn_Wq': _L2_attn_in['Wq'], 'L2_attn_bq': _L2_attn_in['bq'], 'L2_attn_Wk': _L2_attn_in['Wk'], 'L2_attn_bk': _L2_attn_in['bk'], 'L2_attn_Wv': _L2_attn_in['Wv'], 'L2_attn_bv': _L2_attn_in['bv'], 'L2_ffn_wf': _L2_ffn_in['wf'], 'L2_ffn_uf': _L2_ffn_in['uf'], 'L2_ffn_bf': _L2_ffn_in['bf'], 'L2_ffn_wi': _L2_ffn_in['wi'], 'L2_ffn_ui': _L2_ffn_in['ui'], 'L2_ffn_bi': _L2_ffn_in['bi'], 'L2_ffn_wc': _L2_ffn_in['wc'], 'L2_ffn_uc': _L2_ffn_in['uc'], 'L2_ffn_bc': _L2_ffn_in['bc'], 'L2_ffn_wo': _L2_ffn_in['wo'], 'L2_ffn_uo': _L2_ffn_in['uo'], 'L2_ffn_bo': _L2_ffn_in['bo'], 'L2_ffn_in_c': _L2_ffn_in['in_c'], 'L3_attn_Wr': _L3_attn_in['Wr'], 'L3_attn_br': _L3_attn_in['br'], 'L3_attn_step_bias': _L3_attn_in['step_bias'], 'L3_attn_ln1_g': _L3_attn_in['ln1_g'], 'L3_attn_ln1_b': _L3_attn_in['ln1_b'], 'L3_attn_ln2_g': _L3_attn_in['ln2_g'], 'L3_attn_ln2_b': _L3_attn_in['ln2_b'], 'L3_attn_ls1': _L3_attn_in['ls1'], 'L3_attn_ls2': _L3_attn_in['ls2'], 'L3_attn_Wqkv': _L3_attn_in['Wqkv'], 'L3_attn_Wout': _L3_attn_in['Wout'], 'L3_attn_Wgate': _L3_attn_in['Wgate'], 'L3_attn_Win_ssm': _L3_attn_in['Win_ssm'], 'L3_attn_conv_w': _L3_attn_in['conv_w'], 'L3_attn_conv_b': _L3_attn_in['conv_b'], 'L3_attn_Wout_ssm': _L3_attn_in['Wout_ssm'], 'L3_attn_Wg': _L3_attn_in['Wg'], 'L3_attn_W1': _L3_attn_in['W1'], 'L3_attn_W2': _L3_attn_in['W2'], 'L3_attn_W3': _L3_attn_in['W3'], 'L3_ffn_norm_scale': _L3_ffn_in['norm_scale'], 'L3_ffn_gate_w': _L3_ffn_in['gate_w'], 'L3_ffn_gate_b': _L3_ffn_in['gate_b'], 'L3_ffn_mlp1_w': _L3_ffn_in['mlp1_w'], 'L3_ffn_mlp1_b': _L3_ffn_in['mlp1_b'], 'L3_ffn_mlp2_w': _L3_ffn_in['mlp2_w'], 'L3_ffn_mlp2_b': _L3_ffn_in['mlp2_b']}
    _x0 = _d['L0_attn_x']
    _d['L0_attn_x'] = jax.random.normal(jax.random.fold_in(jax.random.key(seed), 1), (8, 256, 128), dtype=_x0.dtype)
    del _x0
    return _d

def reference(L0_attn_x, L0_attn_qk_w, L0_attn_qk_b, L0_attn_lepe_w, L0_attn_lepe_b, L0_ffn_in_proj_w, L0_ffn_in_proj_b, L0_ffn_out_w, L0_ffn_out_b, L0_ffn_ln1_g, L0_ffn_ln1_b, L0_ffn_router_w, L0_ffn_router_b, L0_ffn_w1, L0_ffn_b1, L0_ffn_w2, L0_ffn_b2, L0_ffn_ln2_g, L0_ffn_ln2_b, L1_attn_ln_scale, L1_attn_ln_bias, L1_attn_W_hidden, L1_attn_b_hidden, L1_attn_W_qk, L1_attn_b_qk, L1_attn_os_weight, L1_attn_os_bias, L1_attn_W_out, L1_attn_b_out, L1_ffn_Wr, L1_ffn_br, L1_ffn_W1, L1_ffn_b1, L1_ffn_W2, L1_ffn_b2, L1_ffn_gamma, L1_ffn_beta, L1_ffn_token_mask, L2_attn_Wq, L2_attn_bq, L2_attn_Wk, L2_attn_bk, L2_attn_Wv, L2_attn_bv, L2_ffn_wf, L2_ffn_uf, L2_ffn_bf, L2_ffn_wi, L2_ffn_ui, L2_ffn_bi, L2_ffn_wc, L2_ffn_uc, L2_ffn_bc, L2_ffn_wo, L2_ffn_uo, L2_ffn_bo, L2_ffn_in_c, L3_attn_Wr, L3_attn_br, L3_attn_step_bias, L3_attn_ln1_g, L3_attn_ln1_b, L3_attn_ln2_g, L3_attn_ln2_b, L3_attn_ls1, L3_attn_ls2, L3_attn_Wqkv, L3_attn_Wout, L3_attn_Wgate, L3_attn_Win_ssm, L3_attn_conv_w, L3_attn_conv_b, L3_attn_Wout_ssm, L3_attn_Wg, L3_attn_W1, L3_attn_W2, L3_attn_W3, L3_ffn_norm_scale, L3_ffn_gate_w, L3_ffn_gate_b, L3_ffn_mlp1_w, L3_ffn_mlp1_b, L3_ffn_mlp2_w, L3_ffn_mlp2_b):

    def _L0_attn_ref(x, qk_w, qk_b, lepe_w, lepe_b):
        import jax, jax.numpy as jnp
        import numpy as np
        NUM_HEADS = 8
        ROPE_BASE = 10000.0

        def _rope(x):
            b, n, c = x.shape
            k_max = c // 2
            theta = 1.0 / ROPE_BASE ** (jnp.arange(k_max, dtype=jnp.float32) / k_max)
            angles = jnp.arange(n, dtype=jnp.float32)[:, None] * theta
            cos = jnp.cos(angles)
            sin = jnp.sin(angles)
            xr = x[..., 0::2]
            xi = x[..., 1::2]
            pr = cos * xr - sin * xi
            pi = cos * xi + sin * xr
            return jnp.concatenate([pr, pi], axis=-1)
        b, n, c = x.shape
        h = NUM_HEADS
        d = c // h
        qk = x @ qk_w + qk_b
        q, k = jnp.split(qk, 2, axis=-1)
        q = jax.nn.elu(q) + 1.0
        k = jax.nn.elu(k) + 1.0
        q_rope = _rope(q)
        k_rope = _rope(k)

        def to_heads(t):
            return t.reshape(b, n, h, d).transpose(0, 2, 1, 3)
        qh = to_heads(q)
        kh = to_heads(k)
        qr = to_heads(q_rope)
        kr = to_heads(k_rope)
        vh = to_heads(x)
        k_mean = jnp.mean(kh, axis=2, keepdims=True)
        z = 1.0 / (jnp.einsum('bhnd,bhmd->bhnm', qh, k_mean) + 1e-06)
        kv = jnp.einsum('bhnd,bhne->bhde', kr, vh) * (1.0 / jnp.sqrt(jnp.float32(n)))
        out = jnp.einsum('bhnd,bhde->bhne', qr, kv) * z
        out = out.transpose(0, 2, 1, 3).reshape(b, n, c)
        lepe = jax.lax.conv_general_dilated(x, lepe_w, window_strides=(1,), padding='SAME', dimension_numbers=('NWC', 'WIO', 'NWC')) + lepe_b
        return out + lepe

    def _L0_ffn_ref(x, in_proj_w, in_proj_b, out_w, out_b, ln1_g, ln1_b, router_w, router_b, w1, b1, w2, b2, ln2_g, ln2_b):
        import jax, jax.numpy as jnp
        import numpy as np
        H = 16
        E = 8
        EPS = 1e-05

        def _layernorm(x, g, b):
            mu = jnp.mean(x, axis=-1, keepdims=True)
            var = jnp.mean(jnp.square(x - mu), axis=-1, keepdims=True)
            return (x - mu) * jax.lax.rsqrt(var + EPS) * g + b
        T, B, C = x.shape
        D = C // H
        qkv = x @ in_proj_w.T + in_proj_b
        q, k, v = jnp.split(qkv, 3, axis=-1)
        q = q.reshape(T, B, H, D)
        k = k.reshape(T, B, H, D)
        v = v.reshape(T, B, H, D)
        scale = 1.0 / np.sqrt(D).astype(np.float32)
        scores = jnp.einsum('tbhd,sbhd->bhts', q, k) * scale
        attn = jax.nn.softmax(scores, axis=-1)
        ctx = jnp.einsum('bhts,sbhd->tbhd', attn, v).reshape(T, B, C)
        attn_out = ctx @ out_w.T + out_b
        h = _layernorm(x + attn_out, ln1_g, ln1_b)
        flat = h.reshape(-1, C)
        logits = flat @ router_w.T + router_b
        probs = jax.nn.softmax(logits, axis=-1)
        _, top_i = jax.lax.top_k(probs, 2)
        assign = jnp.max(top_i, axis=-1)
        out = jnp.zeros_like(flat)
        for e in range(E):
            he = jax.nn.gelu(flat @ w1[e].T + b1[e], approximate=False)
            oe = he @ w2[e].T + b2[e]
            out = jnp.where((assign == e)[:, None], oe, out)
        moe_out = out.reshape(T, B, C)
        return _layernorm(h + moe_out, ln2_g, ln2_b)

    def _L1_attn_ref(x, ln_scale, ln_bias, W_hidden, b_hidden, W_qk, b_qk, os_weight, os_bias, W_out, b_out):
        import jax, jax.numpy as jnp
        import numpy as np
        DIM = 128
        QK = 128
        HID = 256
        B, N = (4, 256)
        EPS = 1e-05
        n = x.shape[1]
        mu = jnp.mean(x, axis=-1, keepdims=True)
        var = jnp.mean(jnp.square(x - mu), axis=-1, keepdims=True)
        xn = (x - mu) / jnp.sqrt(var + EPS) * ln_scale + ln_bias
        hid = jax.nn.silu(xn @ W_hidden + b_hidden)
        v, gate = (hid[..., :HID], hid[..., HID:])
        qk = jax.nn.silu(xn @ W_qk + b_qk)
        qk2 = qk[..., None, :] * os_weight + os_bias
        q, k = (qk2[..., 0, :], qk2[..., 1, :])
        sim = jnp.einsum('bid,bjd->bij', q, k) / n
        attn = jnp.square(jax.nn.relu(sim))
        out = jnp.einsum('bij,bjd->bid', attn, v)
        out = out * gate
        return out @ W_out + b_out

    def _L1_ffn_ref(hidden_states, Wr, br, W1, b1, W2, b2, gamma, beta, token_mask):
        import math
        import jax, jax.numpy as jnp
        import numpy as np
        E = 8
        TOPK = 2
        CF = 1.25
        EPS = 1e-05
        NEG = -1e+30

        def _layer_norm(x, gamma, beta):
            mu = jnp.mean(x, axis=-1, keepdims=True)
            var = jnp.mean((x - mu) ** 2, axis=-1, keepdims=True)
            return (x - mu) * jax.lax.rsqrt(var + EPS) * gamma + beta
        B, S, H = hidden_states.shape
        x = hidden_states.reshape(-1, H)
        N = x.shape[0]
        logits = x @ Wr + br
        top_vals, top_idx = jax.lax.top_k(logits, TOPK)
        w = jax.nn.softmax(top_vals, axis=-1)
        flat_idx = top_idx.reshape(-1)
        flat_tok = jnp.repeat(jnp.arange(N), TOPK)
        w_flat = w.reshape(-1)
        cap = max(int(math.ceil(N / E * CF)), 1)
        key_mat = jnp.where(flat_idx[None, :] == jnp.arange(E)[:, None], w_flat[None, :], NEG)
        kv, ki = jax.lax.top_k(key_mat, cap)
        valid = kv > NEG / 2
        tok = flat_tok[ki]
        gate = jnp.where(valid, w_flat[ki], 0.0)
        xe = x[tok]
        h1 = jnp.einsum('ech,ehf->ecf', xe, W1) + b1[:, None, :]
        h1 = jax.nn.gelu(h1, approximate=False)
        y = jnp.einsum('ecf,efh->ech', h1, W2) + b2[:, None, :]
        out = jnp.zeros_like(x).at[tok.reshape(-1)].add((y * gate[..., None]).reshape(-1, H))
        out = out.reshape(B, S, H) + hidden_states
        return _layer_norm(out, gamma, beta)

    def _L2_attn_ref(hidden_states, Wq, bq, Wk, bk, Wv, bv):
        import jax, jax.numpy as jnp
        import numpy as np
        import math
        HEAD_SIZE = 64

        def rotate_every_two(x):
            x1 = x[..., ::2]
            x2 = x[..., 1::2]
            return jnp.stack((-x2, x1), axis=-1).reshape(x.shape)

        def rope_table(seq_len, dtype=jnp.float32):
            pos = jnp.arange(seq_len, dtype=jnp.float32)
            inv = 10000.0 ** (jnp.arange(0, HEAD_SIZE, 2, dtype=jnp.float32) / HEAD_SIZE)
            radians = pos[:, None] / inv
            sincos = jnp.stack((jnp.sin(radians), jnp.cos(radians)), axis=-1).reshape(seq_len, -1)
            t = jnp.repeat(sincos, 2, axis=-1)
            return t.astype(dtype)
        B, S, H = hidden_states.shape
        t = rope_table(S, hidden_states.dtype)
        q = hidden_states @ Wq.T + bq
        k = hidden_states @ Wk.T + bk
        v = hidden_states @ Wv.T + bv
        q = q * t + rotate_every_two(q) * t
        k = k * t + rotate_every_two(k) * t
        scale = math.sqrt(HEAD_SIZE)
        scores = jnp.einsum('bsh,bth->bst', q, k) / scale
        probs = jax.nn.softmax(scores, axis=-1)
        out = jnp.einsum('bst,bth->bsh', probs, v)
        return out

    def _L2_ffn_ref(x, wf, uf, bf, wi, ui, bi, wc, uc, bc, wo, uo, bo, in_c):
        import jax, jax.numpy as jnp
        import numpy as np
        from jax import lax
        T, B, I, M, O = (32, 64, 128, 128, 128)

        def _xavier(key, shape):
            fan_out, fan_in = shape
            limit = float(np.sqrt(6.0 / (fan_in + fan_out)))
            return jax.random.uniform(key, shape, jnp.float32, -limit, limit)
        batch = x.shape[1]
        c0 = jnp.broadcast_to(in_c, (batch, in_c.shape[0]))

        def step(c, xt):
            ft = jax.nn.sigmoid(xt @ wf.T + c @ uf.T + bf)
            it = jax.nn.sigmoid(xt @ wi.T + c @ ui.T + bi)
            gt = jnp.tanh(xt @ wc.T + c @ uc.T + bc)
            c = ft * c + it * gt
            return (c, None)
        c_final, _ = lax.scan(step, c0, x)
        h = jnp.tanh(jnp.einsum('tbi,oi->tbo', x, wo) + c_final @ uo.T + bo)
        return h

    def _L3_attn_ref(x, Wr, br, step_bias, ln1_g, ln1_b, ln2_g, ln2_b, ls1, ls2, Wqkv, Wout, Wgate, Win_ssm, conv_w, conv_b, Wout_ssm, Wg, W1, W2, W3):
        import jax, jax.numpy as jnp
        import numpy as np
        B, L, D, H, E, F, STEPS, TOPK = (2, 128, 128, 16, 8, 256, 3, 2)
        HD = D // H

        def layernorm(x, g, b, eps=1e-05):
            m = jnp.mean(x, -1, keepdims=True)
            v = jnp.var(x, -1, keepdims=True)
            return (x - m) * jax.lax.rsqrt(v + eps) * g + b

        def gated_attention(x, Wqkv, Wout, Wgate):
            b, l, d = x.shape
            qkv = (x @ Wqkv).reshape(b, l, 3, H, HD)
            q, k, v = [jnp.moveaxis(qkv[:, :, i], 1, 2) for i in range(3)]
            attn = jax.nn.softmax(jnp.einsum('bhqd,bhkd->bhqk', q, k) * HD ** (-0.5), axis=-1)
            out = jnp.einsum('bhqk,bhkd->bhqd', attn, v)
            out = jnp.moveaxis(out, 1, 2).reshape(b, l, d)
            return out @ Wout * jax.nn.sigmoid(x @ Wgate)

        def ssm(x, Win, cw, cb, Wout):
            xz = x @ Win
            xs, z = jnp.split(xz, 2, axis=-1)
            xt = jnp.swapaxes(xs, 1, 2)
            y = jax.lax.conv_general_dilated(xt, cw, window_strides=(1,), padding=[(3, 0)], dimension_numbers=('NCH', 'OIH', 'NCH'), feature_group_count=D) + cb[None, :, None]
            xc = jax.nn.silu(jnp.swapaxes(y, 1, 2))
            return xc * jax.nn.sigmoid(z) @ Wout

        def moe(x, Wg, W1, W2, W3):
            b, l, d = x.shape
            flat = x.reshape(-1, d)
            probs = jax.nn.softmax(flat @ Wg, axis=-1)
            topp, topi = jax.lax.top_k(probs, TOPK)
            topp = topp / (jnp.sum(topp, -1, keepdims=True) + 1e-08)
            T = flat.shape[0]
            cw = jnp.zeros((T, E), flat.dtype).at[jnp.arange(T)[:, None], topi].add(topp)
            out = jnp.zeros_like(flat)
            for e in range(E):
                h = jax.nn.silu(flat @ W1[e]) * (flat @ W3[e])
                out = out + cw[:, e:e + 1] * (h @ W2[e])
            return out.reshape(b, l, d)
        accumulated = jnp.zeros_like(x)
        remainder = jnp.ones(x.shape[:2] + (1,), x.dtype)
        for step in range(STEPS):
            normed = layernorm(x, ln1_g, ln1_b)
            r = normed @ Wr + br
            alpha = jax.nn.sigmoid(r[..., 0:1])
            halt = jax.nn.sigmoid(r[..., 1:2] + step_bias[step])
            ssm_out = ssm(normed, Win_ssm, conv_w, conv_b, Wout_ssm)
            attn_out = gated_attention(normed, Wqkv, Wout, Wgate)
            blended = ls1 * ((1 - alpha) * ssm_out + alpha * attn_out)
            moe_out = moe(layernorm(x + blended, ln2_g, ln2_b), Wg, W1, W2, W3)
            step_output = x + blended + ls2 * moe_out
            weight = remainder if step == STEPS - 1 else halt * remainder
            accumulated = accumulated + weight * step_output
            remainder = jnp.clip(remainder - weight, 0.0, None)
        return accumulated + x

    def _L3_ffn_ref(x, norm_scale, gate_w, gate_b, mlp1_w, mlp1_b, mlp2_w, mlp2_b):
        import jax, jax.numpy as jnp
        import numpy as np
        B, S, D = (1, 256, 128)
        I = 256
        E = 8
        K = 2
        LIMIT = 7.0
        ALPHA = 1.702
        EPS = 1e-05

        def _swiglu(h):
            x_glu = jnp.minimum(h[..., ::2], LIMIT)
            x_lin = jnp.clip(h[..., 1::2], -LIMIT, LIMIT)
            return x_glu * jax.nn.sigmoid(ALPHA * x_glu) * (x_lin + 1.0)

        def _moe(t, gate_w, gate_b, mlp1_w, mlp1_b, mlp2_w, mlp2_b):
            T = t.shape[0]
            logits = t @ gate_w + gate_b
            top_v, top_i = jax.lax.top_k(logits, K)
            probs = jax.nn.softmax(top_v, axis=-1)
            w = jnp.zeros((T, E), t.dtype).at[jnp.arange(T)[:, None], top_i].set(probs)

            def body(acc, ew):
                w1, b1, w2, b2, we = ew
                h = _swiglu(t @ w1 + b1)
                y = h @ w2 + b2
                return (acc + we[:, None] * y, None)
            acc0 = jnp.zeros((T, t.shape[1]), t.dtype)
            acc, _ = jax.lax.scan(body, acc0, (mlp1_w, mlp1_b, mlp2_w, mlp2_b, w.T))
            return acc
        Bx, Sx, Dx = x.shape
        ms = jnp.mean(x * x, axis=-1, keepdims=True)
        t = (x * jax.lax.rsqrt(ms + EPS) * norm_scale).reshape(Bx * Sx, Dx)
        y = _moe(t, gate_w, gate_b, mlp1_w, mlp1_b, mlp2_w, mlp2_b)
        return x + y.reshape(Bx, Sx, Dx)
    x = L0_attn_x
    xn = _layernorm(x, axis=-1)
    s = _L0_attn_ref(xn, L0_attn_qk_w, L0_attn_qk_b, L0_attn_lepe_w, L0_attn_lepe_b)
    g = _silu(_L0_ffn_ref(xn, L0_ffn_in_proj_w, L0_ffn_in_proj_b, L0_ffn_out_w, L0_ffn_out_b, L0_ffn_ln1_g, L0_ffn_ln1_b, L0_ffn_router_w, L0_ffn_router_b, L0_ffn_w1, L0_ffn_b1, L0_ffn_w2, L0_ffn_b2, L0_ffn_ln2_g, L0_ffn_ln2_b))
    x = x + s * g
    xn = _layernorm(x, axis=-1)
    s = _L1_attn_ref(xn, L1_attn_ln_scale, L1_attn_ln_bias, L1_attn_W_hidden, L1_attn_b_hidden, L1_attn_W_qk, L1_attn_b_qk, L1_attn_os_weight, L1_attn_os_bias, L1_attn_W_out, L1_attn_b_out)
    g = _silu(_L1_ffn_ref(xn, L1_ffn_Wr, L1_ffn_br, L1_ffn_W1, L1_ffn_b1, L1_ffn_W2, L1_ffn_b2, L1_ffn_gamma, L1_ffn_beta, L1_ffn_token_mask))
    x = x + s * g
    xn = _layernorm(x, axis=-1)
    s = _L2_attn_ref(xn, L2_attn_Wq, L2_attn_bq, L2_attn_Wk, L2_attn_bk, L2_attn_Wv, L2_attn_bv)
    g = _silu(_L2_ffn_ref(xn, L2_ffn_wf, L2_ffn_uf, L2_ffn_bf, L2_ffn_wi, L2_ffn_ui, L2_ffn_bi, L2_ffn_wc, L2_ffn_uc, L2_ffn_bc, L2_ffn_wo, L2_ffn_uo, L2_ffn_bo, L2_ffn_in_c))
    x = x + s * g
    xn = _layernorm(x, axis=-1)
    s = _L3_attn_ref(xn, L3_attn_Wr, L3_attn_br, L3_attn_step_bias, L3_attn_ln1_g, L3_attn_ln1_b, L3_attn_ln2_g, L3_attn_ln2_b, L3_attn_ls1, L3_attn_ls2, L3_attn_Wqkv, L3_attn_Wout, L3_attn_Wgate, L3_attn_Win_ssm, L3_attn_conv_w, L3_attn_conv_b, L3_attn_Wout_ssm, L3_attn_Wg, L3_attn_W1, L3_attn_W2, L3_attn_W3)
    g = _silu(_L3_ffn_ref(xn, L3_ffn_norm_scale, L3_ffn_gate_w, L3_ffn_gate_b, L3_ffn_mlp1_w, L3_ffn_mlp1_b, L3_ffn_mlp2_w, L3_ffn_mlp2_b))
    x = x + s * g
    return x

_drawn_inputs = setup_inputs


def setup_inputs(seed=0):
    import zlib

    import numpy as np

    out = dict(_drawn_inputs(seed))
    spreads = {'L0_attn_qk_b': (0.0, 0.303),
     'L0_attn_lepe_b': (0.0, 0.1),
     'L0_ffn_in_proj_b': (0.0, 0.381),
     'L0_ffn_out_b': (0.0, 0.1),
     'L0_ffn_ln1_g': (1.0, 0.2),
     'L0_ffn_ln1_b': (0.0, 0.1),
     'L0_ffn_router_b': (0.0, 0.1),
     'L0_ffn_b1': (0.0, 0.8),
     'L0_ffn_b2': (0.0, 0.1),
     'L0_ffn_ln2_g': (1.0, 0.2),
     'L0_ffn_ln2_b': (0.0, 0.1),
     'L1_attn_ln_scale': (1.0, 0.6),
     'L1_attn_ln_bias': (0.0, 0.8),
     'L1_attn_b_hidden': (0.0, 0.8),
     'L1_attn_b_qk': (0.0, 0.8),
     'L1_attn_os_bias': (0.0, 0.8),
     'L1_attn_b_out': (0.0, 0.1),
     'L1_ffn_br': (0.0, 0.516),
     'L1_ffn_gamma': (1.0, 0.6),
     'L1_ffn_beta': (0.0, 0.8),
     'L2_ffn_bf': (0.0, 0.8),
     'L2_ffn_bi': (0.0, 0.8),
     'L2_ffn_bc': (0.0, 0.8),
     'L2_ffn_bo': (0.0, 0.8),
     'L2_ffn_in_c': (0.0, 0.8),
     'L3_attn_br': (0.0, 2.0),
     'L3_attn_step_bias': (0.0, 2.0),
     'L3_attn_ln1_g': (1.0, 0.6),
     'L3_attn_ln1_b': (0.0, 2.0),
     'L3_attn_ln2_g': (1.0, 0.6),
     'L3_attn_ln2_b': (0.0, 2.0),
     'L3_attn_ls1': (9.999999747378752e-06, 0.6),
     'L3_attn_ls2': (9.999999747378752e-06, 0.6),
     'L3_attn_conv_b': (0.0, 2.0),
     'L3_ffn_norm_scale': (1.0, 0.6),
     'L3_ffn_gate_b': (0.0, 0.608),
     'L3_ffn_mlp1_b': (0.0, 0.8),
     'L3_ffn_mlp2_b': (0.0, 0.443)}
    factors = {'L0_ffn_in_proj_w': 3.202,
     'L0_ffn_w1': 2.778,
     'L1_attn_W_hidden': 8.0,
     'L1_attn_W_qk': 8.0,
     'L1_attn_os_weight': 8.0,
     'L1_attn_W_out': 8.0,
     'L1_ffn_Wr': 6.207,
     'L1_ffn_W1': 6.845,
     'L1_ffn_b1': 8.0,
     'L1_ffn_W2': 6.075,
     'L1_ffn_b2': 21.361,
     'L2_attn_bq': 8.0,
     'L2_attn_bk': 8.0,
     'L2_attn_bv': 3.855,
     'L2_ffn_wf': 8.0,
     'L2_ffn_uf': 8.0,
     'L2_ffn_wi': 6.427,
     'L2_ffn_ui': 8.0,
     'L2_ffn_wc': 2.793,
     'L2_ffn_uc': 5.051,
     'L2_ffn_uo': 2.811,
     'L3_attn_Wr': 200.0,
     'L3_attn_Wqkv': 200.0,
     'L3_attn_Wout': 200.0,
     'L3_attn_Wgate': 200.0,
     'L3_attn_Win_ssm': 200.0,
     'L3_attn_conv_w': 200.0,
     'L3_attn_Wout_ssm': 200.0,
     'L3_attn_Wg': 64.0,
     'L3_attn_W1': 64.0,
     'L3_attn_W2': 64.0,
     'L3_attn_W3': 64.0,
     'L3_ffn_gate_w': 3.422,
     'L3_ffn_mlp1_w': 7.243,
     'L3_ffn_mlp2_w': 6.672}
    for name, (base, spread) in spreads.items():
        noise = np.random.default_rng([zlib.crc32(name.encode()), seed]).standard_normal(out[name].shape)
        drawn = base * np.exp(spread * noise) if base else spread * noise
        out[name] = jnp.asarray(drawn.astype(out[name].dtype))
    for name, factor in factors.items():
        out[name] = (out[name] * factor).astype(out[name].dtype)
    return out
```

```python
import numpy as np
import concourse.bass as bass
from concourse import mybir
from concourse.alu_op_type import AluOpType as ALU

F32 = mybir.dt.float32
BF16 = mybir.dt.bfloat16
I32 = mybir.dt.int32
U32 = mybir.dt.uint32
ACT = mybir.ActivationFunctionType
AX = mybir.AxisListType.X

P = 128
C = 128
NB, NS = 8, 256
NT = NB * NS // P
TOK = NB * NS
E = 8
EPS = 1e-5
PAD = 1000


class Token:

    def __init__(self, src, off, loop, back=0):
        self.src, self.off, self.loop, self.back = src, off, loop, back


class Loop:

    def __init__(self, count):
        self.count, self.i, self.base, self.per, self.marks = count, 0, {}, {}, {}

    def mark(self, name, tok):
        self.marks[name] = tok
        return tok

    def prev(self, name, back=1):
        t = self.marks.get(name)
        return None if t is None else Token(t.src, t.off, self, back)


class Source:

    def __init__(self, prog, name, step):
        self.prog, self.step, self.n, self.pad = prog, step, 0, PAD
        self.sem = prog.nc.alloc_semaphore(name)
        prog.sources.append(self)

    def took(self):
        self.n += self.step
        lp = self.prog.loop
        return Token(self, self.n if lp is None else self.n - lp.base.get(self, 0), lp)

    def value(self, t):
        lp = t.loop
        if lp is None:
            return self.pad + t.off
        k = lp.per.get(self, 0)
        if lp is self.prog.loop:
            return lp.i * k + (self.pad + lp.base.get(self, 0) + t.off - k * t.back)
        return self.pad + lp.base.get(self, 0) + (lp.count - 1) * k + t.off


class Engine(Source):
    def __init__(self, prog, name, eng):
        super().__init__(prog, "done_" + name, 1)
        self.eng = eng
        self.seen = {}

    def wait(self, toks):
        for t in toks:
            if t is None or self.prog.dry:
                continue
            key = (t.src, t.loop if t.loop is self.prog.loop else None)
            rank = (-t.back, t.off) if key[1] is not None else (0, t.src.value(t))
            if key in self.seen and self.seen[key] >= rank:
                continue
            self.seen[key] = rank
            self.eng.wait_ge(t.src.sem, t.src.value(t))

    def put(self, build, w=(), inc=True):
        self.wait(w)
        if not self.prog.dry:
            ins = build()
            if inc:
                ins.then_inc(self.sem, 1)
        return self.took() if inc else None

    def now(self):
        lp = self.prog.loop
        return Token(self, self.n if lp is None else self.n - lp.base.get(self, 0), lp)

    def tt(self, out, a, b, op, w=()):
        return self.put(lambda: self.eng.tensor_tensor(out, a, b, op), w)

    def ts(self, out, a, s1, s2=None, op0=ALU.mult, op1=None, w=()):
        if op1 is None:
            return self.put(lambda: self.eng.tensor_scalar(out, a, s1, None, op0), w)
        return self.put(lambda: self.eng.tensor_scalar(out, a, s1, s2, op0, op1), w)

    def stt(self, out, a, s, b, op0, op1, w=(), acc=None):
        return self.put(lambda: self.eng.scalar_tensor_tensor(out=out, in0=a, scalar=s, in1=b, op0=op0, op1=op1,
                                                              accum_out=acc), w)

    def cp(self, out, a, w=()):
        return self.put(lambda: self.eng.tensor_copy(out, a), w)

    def red(self, out, a, op, w=()):
        return self.put(lambda: self.eng.tensor_reduce(out, a, AX, op), w)

    def rcp(self, out, a, w=()):
        return self.put(lambda: self.eng.reciprocal(out, a), w)

    def fill(self, out, val, w=()):
        return self.put(lambda: self.eng.memset(out, val), w)

    def act(self, out, a, func, w=(), bias=0.0, scale=1.0, acc=None):
        return self.put(lambda: self.eng.activation(out, a, func, bias=bias, scale=scale, accum_out=acc), w)

    def mm(self, out, lhsT, rhs, first=True, last=True, w=(), inc=None, shared=False):
        inc = last if inc is None else inc
        return self.put(lambda: self.eng.matmul(out, lhsT, rhs, start=first, stop=last, skip_group_check=shared), w, inc)

    def tr(self, out, a, ident, w=(), inc=True):
        return self.put(lambda: self.eng.transpose(out, a, ident), w, inc)

    def dma(self, out, a, ch, w=()):
        self.wait(w)
        if not self.prog.dry:
            self.eng.dma_start(out, a).then_inc(ch.sem, 16)
        return ch.took()

    def scatter_rows(self, table, idx, rows, ch, w=()):
        self.wait(w)
        if not self.prog.dry:
            self.eng.indirect_dma_start(table, bass.IndirectOffsetOnAxis(ap=idx, axis=0), rows, None).then_inc(ch.sem, 16)
        return ch.took()

    def gather_rows(self, rows, table, idx, ch, w=()):
        self.wait(w)
        if not self.prog.dry:
            self.eng.indirect_dma_start(rows, None, table, bass.IndirectOffsetOnAxis(ap=idx, axis=0)).then_inc(ch.sem, 16)
        return ch.took()


class Program:

    def __init__(self, nc):
        self.nc, self.sources, self.loop, self.dry = nc, [], None, False
        self.pe = Engine(self, "pe", nc.tensor)
        self.dve = Engine(self, "dve", nc.vector)
        self.act = Engine(self, "act", nc.scalar)
        self.pool = Engine(self, "pool", nc.gpsimd)
        self.sp = Engine(self, "sp", nc.sync)
        self.engines = [self.pe, self.dve, self.act, self.pool, self.sp]
        for e in self.engines:
            e.eng.sem_inc(e.sem, PAD)
        self.n_sb = 0

    def channel(self, name, issuer):
        ch = Source(self, name, 16)
        if issuer is self.pool:
            ch.pad = 0
        else:
            issuer.eng.sem_inc(ch.sem, PAD)
        return ch

    def run_loop(self, count, body):
        lp = Loop(count)
        lp.base = {s: s.n for s in self.sources}
        kept = {s: s.n for s in self.sources}
        self.loop, self.dry = lp, True
        body(0, lp)
        lp.per = {s: s.n - kept[s] for s in self.sources}
        for s in self.sources:
            s.n = kept[s]
        self.dry = False
        for e in self.engines:
            e.seen = {}
        with self.nc.Fori(0, count) as i:
            lp.i = i
            body(i, lp)
        lp.i = 0
        self.loop = None
        for s in self.sources:
            s.n = kept[s] + count * lp.per[s]
        for e in self.engines:
            e.seen = {}

    def sbuf(self, name, shape, dt=F32):
        return self.nc.alloc_sbuf_tensor(name, shape, dt)


class Banks:

    def __init__(self, prog, nc):
        self.prog = prog
        self.ps = nc.alloc_psum_tensor("banks", [P, 8 * 512], F32)
        self.k, self.free, self.local = 0, [[] for _ in range(8)], set()

    def take(self, width=512):
        i = self.k % 8
        self.k += 1
        lp = self.prog.loop
        w = self.free[i]
        if lp is not None and i not in self.local:
            w = [lp.prev(f"bank{i}.{n}") for n in range(2)]
        return i, self.ps[:, i * 512:i * 512 + width], w

    def give(self, i, *toks):
        self.free[i] = list(toks)
        lp = self.prog.loop
        if lp is not None:
            self.local.add(i)
            for n, t in enumerate(toks):
                lp.mark(f"bank{i}.{n}", t)

    def run_loop(self, count, body):
        self.prog.pe.wait([t for f in self.free for t in f])

        def whole(i, lp):
            self.k, self.local = 0, set()
            self.free = [[] for _ in range(8)]
            body(i, lp)

        self.prog.run_loop(count, whole)
        self.k = 0


def grow(ap, n):
    return ap.unsqueeze(1).broadcast_to((ap.shape[0], n, ap.shape[1]))


def grow_in(ap, n):
    return ap.unsqueeze(2).broadcast_to((ap.shape[0], ap.shape[1], n))


class Pack:

    def __init__(self, fields):
        self.at, n = {}, 0
        for name, width in fields:
            self.at[name] = (n, n + width)
            n += width
        self.width = n

    def on(self, tensor, start=0):
        self.tensor, self.start = tensor, start
        return self

    def __getitem__(self, name):
        a, b = self.at[name]
        return self.tensor[:, self.start + a:self.start + b]


CONSTS = [("ident", 128), ("ones", 128), ("before", 128), ("swap", 128), ("heads", 8), ("kv_mask", 128),
          ("rope_cos", 256), ("rope_sin", 256), ("rot2", 128), ("rope2", 256), ("iota8", 8), ("iota384", 8),
          ("tile_start", 40), ("tile_third", 40), ("scan_mask", 128), ("one_row8", 1), ("bits", 30)]
W0 = [("q", 128), ("k", 128), ("lepe", 384), ("qkv", 384), ("out", 128), ("router", 8), ("q_b", 1), ("k_b", 1),
      ("w1", 1024), ("w2", 1024)]
R0 = [("lepe_b", 128), ("qkv_b", 384), ("out_b", 128), ("ln1_g", 128), ("ln1_b", 128), ("ln2_g", 128),
      ("ln2_b", 128), ("router_b", 8), ("b1", 1024), ("b2", 1024)]
W1 = [("hidden", 512), ("qk", 128), ("out", 256), ("router", 8), ("ln_g", 1), ("ln_b", 1), ("qk_b", 1),
      ("osw", 2), ("osb", 2), ("w1", 4096), ("w2", 4096)]
R1 = [("hidden_b", 512), ("out_b", 128), ("router_b", 8), ("gamma", 128), ("beta", 128), ("b1", 4096), ("b2", 1024)]
W2 = [("wq", 128), ("wk", 128), ("wv", 128), ("wf", 128), ("wi", 128), ("wc", 128), ("uf", 128), ("ui", 128),
      ("uc", 128), ("wo", 128), ("uo", 128), ("bq", 1), ("bk", 1), ("bf", 1), ("bi", 1), ("bc", 1), ("c0", 1)]
R2 = [("bv", 128), ("bo", 128)]
W3 = [("q", 512), ("k", 512), ("v", 128), ("gate", 128), ("ssm", 256), ("ssm_out", 128), ("attn_out", 128),
      ("halt", 2), ("router", 8), ("gate_w", 8), ("ln_g", 1), ("ln_b", 1), ("conv_w", 4), ("conv_b", 1),
      ("w13", 4096), ("w2", 2048), ("mlp1", 4096), ("mlp2", 2048)]
R3 = [("ln2_g", 128), ("ln2_b", 128), ("ls1", 128), ("ls2", 128), ("halt_b", 2), ("step_b", 3), ("norm", 128),
      ("gate_b", 8), ("mlp1_b", 4096), ("mlp2_b", 1024)]


class Net:

    def __init__(self, nc, ins):
        self.nc = nc
        p = self.p = Program(nc)
        self.pe, self.dve, self.act, self.pool, self.sp = p.engines
        self.banks = Banks(p, nc)
        self.ins = ins
        sb = p.sbuf
        self.x = sb("x", [P, NT, C])
        self.xn = sb("xn", [P, NT, C])
        self.xT = sb("xT", [P, NB, NS + 2])
        self.s = sb("s", [P, NT, C])
        self.g = sb("g", [P, NT, C])
        self.t1 = sb("t1", [P, NT, C])
        self.t2 = self.g
        self.tT = sb("tT", [P, TOK])
        self.work = sb("work", [P, 10496])
        self.arena = self.work[:, 0:4352]
        self.qkv = self.work[:, 4352:10496].rearrange("p (t c) -> p t c", c=3 * C)
        self.c = Pack(CONSTS).on(sb("consts", [P, Pack(CONSTS).width]))
        w0, r0, w1, r1, w2, r2, w3, r3 = (Pack(f) for f in (W0, R0, W1, R1, W2, R2, W3, R3))
        room = max(w0.width + r0.width + w1.width + r1.width, w3.width + r3.width)
        wts = sb("weights", [P, room])
        self.w0, self.r0 = w0.on(wts, 0), r0.on(wts, w0.width)
        a = w0.width + r0.width
        self.w1, self.r1 = w1.on(wts, a), r1.on(wts, a + w1.width)
        self.w3, self.r3 = w3.on(wts, 0), r3.on(wts, w3.width)
        w2s = sb("weights2", [P, w2.width + r2.width])
        self.w2, self.r2 = w2.on(w2s, 0), r2.on(w2s, w2.width)
        self.stats = sb("stats", [P, NT, 6])
        self.v = [sb(f"small{i}", [P, NT]) for i in range(13)]
        self.k8 = [sb(f"byexpert{i}", [P, NT, E]) for i in range(8)]
        self.e8 = [sb(f"experts{i}", [P, E]) for i in range(6)]
        self.gates = sb("gates", [P, 2, NT])
        self.idx = sb("idx", [P, 4, NT], I32)
        self.tile_e = sb("tile_e", [1, 40], I32)
        self.tile_f = sb("tile_f", [1, 40, E])
        self.tile_n = sb("tile_n", [1, 40])
        self.ei = sb("ei", [P, E], I32)
        self.vi = sb("vi", [P, NT], I32)
        self.U = 4
        U = self.U
        at = [0]

        def part(n):
            at[0] += n
            return self.work[:, at[0] - n:at[0]]

        self.hs = [part(C) for _ in range(U)]
        self.hT = [part(C) for _ in range(U)]
        self.hm = [part(512) for _ in range(U)]
        self.ha = [part(512) for _ in range(U)]
        self.aT = [part(512) for _ in range(U)]
        self.y = [part(C) for _ in range(U)]
        self.ch_in = [p.channel(f"ch_in{u}", self.sp) for u in range(U)]
        self.ch_out = [p.channel(f"ch_out{u}", self.act) for u in range(U)]
        self.ch_row = p.channel("ch_row", self.pool)
        self.ch_out_x = p.channel("ch_out_x", self.sp)

    def load(self, eng, pack, name, w=(), rows=False):
        ch = self.p.channel("ch_" + name, eng)
        dst = pack.tensor[:, pack.start:pack.start + pack.width]
        src = self.ins[name]
        if rows:
            src = src.broadcast_to((P, pack.width))
        return eng.dma(dst, src, ch, w)

    def rsqrt(self, out, v, w):
        d, t = self.dve, self.v[10]
        k = d.ts(self.vi[:, :], v.bitcast(I32), 1, op0=ALU.logical_shift_right, w=w)
        k = d.ts(out.bitcast(I32), self.vi[:, :], -1.0, float(0x5F3759DF), ALU.mult, ALU.add, w=[k])
        for _ in range(3):
            k = d.tt(t[:, :], out, out, ALU.mult, w=[k])
            k = d.stt(t[:, :], t[:, :], -0.5, v, ALU.mult, ALU.mult, w=[k])
            k = d.stt(out, t[:, :], 1.5, out, ALU.add, ALU.mult, w=[k])
        return k

    def layernorm(self, src, dst, w, gain=None, bias=None):
        d, st = self.dve, self.stats
        diff, both, q, var, rstd, nmr = (self.v[i][:, :] for i in range(6))
        for t in range(NT):
            k = d.put(lambda: d.eng.bn_stats(st[:, t, :], src[:, t, :]), w(t))
        k1 = d.tt(diff, st[:, :, 1], st[:, :, 4], ALU.subtract, w=[k])
        k2 = d.tt(both, st[:, :, 1], st[:, :, 4], ALU.add, w=[k])
        k3 = d.tt(q, st[:, :, 2], st[:, :, 5], ALU.add, w=[k])
        k4 = d.tt(diff, diff, diff, ALU.mult, w=[k1])
        k5 = d.ts(q, q, 1.0 / C, EPS, ALU.mult, ALU.add, w=[k3])
        k6 = d.stt(var, diff, 0.25, q, ALU.mult, ALU.add, w=[k4, k5])
        k7 = self.rsqrt(rstd, var, [k6])
        k8 = d.stt(nmr, both, -0.5, rstd, ALU.mult, ALU.mult, w=[k7])
        for t in range(NT):
            k = d.ts(dst[:, t, :], src[:, t, :], rstd[:, t:t + 1], nmr[:, t:t + 1], ALU.mult, ALU.add, w=[k8])
        if gain is not None:
            k = d.tt(dst[:, :, :], dst[:, :, :], grow(gain, NT), ALU.mult, w=[k])
            k = d.tt(dst[:, :, :], dst[:, :, :], grow(bias, NT), ALU.add, w=[k])
        return k

    def transposed(self, src, dst4, w, gain=None, bias=None, w_dst=()):
        out = []
        for q in range(4):
            i, ps, wb = self.banks.take()
            for r in range(4):
                k = self.pe.tr(ps[:, r * 128:(r + 1) * 128], src[:, 4 * q + r, :], self.c["ident"],
                               w=list(w) + wb, inc=(r == 3))
            d = dst4(q)
            a = ps if len(d.shape) == 2 else ps.rearrange("p (b n) -> p b n", n=NS)
            if gain is not None:
                k = self.act.act(d, a, ACT.Identity, bias=bias, scale=gain, w=[k] + list(w_dst))
            else:
                eng = self.act if q % 2 else self.dve
                k = eng.act(d, a, ACT.Copy, w=[k] + list(w_dst)) if eng is self.act else eng.cp(d, a, w=[k] + list(w_dst))
            self.banks.give(i, k)
            out.append(k)
        return out

    def xT_tile(self, t):
        return self.xT[:, t // 2, 1 + 128 * (t % 2):129 + 128 * (t % 2)]

    def logits(self, tileT, weight, bias, out, w):
        n = weight.shape[1]
        i, ps, wb = self.banks.take()
        for t in range(NT):
            k = self.pe.mm(ps[:, t * n:(t + 1) * n], tileT(t), weight, w=list(w) + wb, inc=(t == NT - 1))
        k = self.dve.tt(out, ps[:, 0:NT * n].rearrange("p (t n) -> p t n", n=n), grow(bias, NT), ALU.add, w=[k])
        self.banks.give(i, k)
        return k

    def top2(self, lg, w):
        d = self.dve
        io = grow(self.c["iota8"], NT)
        m = [self.v[6][:, :], self.v[7][:, :]]
        oh = [self.k8[1], self.k8[2]]
        u, low, l2 = self.k8[3][:, :, :], self.v[8][:, :], self.k8[4][:, :, :]
        cur, k = lg, None
        for n in range(2):
            k = d.red(m[n], cur, ALU.max, w=list(w) if k is None else [k])
            k = d.tt(u, cur, grow_in(m[n], E), ALU.is_equal, w=[k])
            k = d.stt(u, u, -8.0, io, ALU.mult, ALU.add, w=[k])
            k = d.red(low, u, ALU.min, w=[k])
            k = d.tt(oh[n][:, :, :], u, grow_in(low, E), ALU.is_equal, w=[k])
            if n == 0:
                k = d.stt(l2, oh[0][:, :, :], -3.0e38, lg, ALU.mult, ALU.add, w=[k])
                cur = l2
        return oh, m, k

    def prefix(self, a, out, incl, w):
        d = self.dve
        i, ps, wb = self.banks.take()
        flat = a[:, :, :].rearrange("p t e -> p (t e)")
        self.pe.mm(ps[:, 0:128], self.c["before"], flat, w=list(w) + wb, inc=False)
        k = self.pe.mm(ps[:, 128:256], self.c["ones"], flat)
        tot = self.k8[5][:, :, :].rearrange("p t e -> p (t e)")
        tot3 = tot.rearrange("p (e t) -> p e t", t=NT)
        k = d.cp(tot3, ps[:, 128:256].rearrange("p (t e) -> p e t", e=E), w=[k])
        k = d.put(lambda: d.eng.tensor_tensor_scan(incl, self.c["scan_mask"], tot, 0.0, ALU.mult, ALU.add), [k])
        k = d.tt(tot, incl, tot, ALU.subtract, w=[k])
        k = d.tt(out, ps[:, 0:128].rearrange("p (t e) -> p t e", e=E),
                 tot.rearrange("p (e t) -> p t e", t=NT), ALU.add, w=[k])
        self.banks.give(i, k)
        return k

    def place(self, oh, D, out, w):
        d = self.dve
        u = self.k8[3][:, :, :]
        k = d.tt(u, oh, D, ALU.mult, w=w)
        return d.red(out, u, ALU.add, w=[k])

    def slots(self, ohs, w):
        d = self.dve
        a, k = ohs[0], None
        if len(ohs) == 2:
            a = self.k8[4]
            k = d.tt(a[:, :, :], ohs[0][:, :, :], ohs[1][:, :, :], ALU.add, w=w)
        D, incl = self.k8[6], self.k8[7][:, :, :].rearrange("p t e -> p (t e)")
        k = self.prefix(a, D[:, :, :], incl, list(w) + [k])
        cnt = incl.rearrange("p (e t) -> p e t", t=NT)[:, :, NT - 1]
        rounded, end, base = (self.e8[i][:, :] for i in range(3))
        k = d.ts(self.ei[:, :], cnt, 127.0, op0=ALU.add, w=[k])
        k = d.ts(self.ei[:, :], self.ei[:, :], 7, 7, ALU.logical_shift_right, ALU.logical_shift_left, w=[k])
        k = d.cp(rounded, self.ei[:, :], w=[k])
        k = d.put(lambda: d.eng.tensor_tensor_scan(end, self.c["ones"][:, 0:E], rounded, 0.0, ALU.mult, ALU.add), [k])
        k = d.tt(base, end, rounded, ALU.subtract, w=[k])
        kd = d.tt(D[:, :, :], D[:, :, :], grow(base, NT), ALU.add, w=[k])
        tf = self.tile_f[:, :, :]
        k = d.tt(tf, end[0:1, :].unsqueeze(1).broadcast_to((1, 40, E)),
                 self.c["tile_start"][0:1, :].unsqueeze(2).broadcast_to((1, 40, E)), ALU.is_le, w=[k])
        k = d.red(self.tile_n[:, :], tf, ALU.add, w=[k])
        kt = d.ts(self.tile_e[:, :], self.tile_n[:, :], float(E - 1), op0=ALU.min, w=[k])
        for n, oh in enumerate(ohs):
            k = self.place(oh[:, :, :], D[:, :, :], self.v[9][:, :], [kd, kt])
            k = d.cp(self.idx[:, n, :], self.v[9][:, :], w=[k])
        return k, kt

    def experts(self, xs, ys, ntile, kt, w, mid, F, NF, wa, wb_, b1=None, b2=None, yscale=1.0):
        pe, d, act, sp = self.pe, self.dve, self.act, self.sp
        U = self.U
        pe.wait([t for f in self.banks.free for t in f])
        for e in self.p.engines:
            e.wait(w)

        def bank(i, n=512, at=0):
            return self.banks.ps[:, i * 512 + at:i * 512 + at + n]

        def body(i, lp):
            ex_pe, ex_dve, T = {}, {}, {}

            def expert(u):
                if self.p.dry:
                    ex_pe[u] = ex_dve[u] = 0
                    return
                src = self.tile_e[0:1, bass.ds(i * U + u, 1)]
                ex_pe[u] = pe.eng.value_load(src, min_val=0, max_val=E - 1)
                if b1 is not None or b2 is not None:
                    ex_dve[u] = d.eng.value_load(src, min_val=0, max_val=E - 1)

            def A(u):
                T["in", u] = lp.mark(f"in{u}", sp.dma(self.hs[u][:, :], xs[bass.ds((i * U + u) * P, P), :],
                                                      self.ch_in[u], w=[lp.prev(f"tr{u}")]))

            def A2(u):
                k = pe.tr(bank(2 * u, 128), self.hs[u][:, :], self.c["ident"],
                          w=[T["in", u], lp.prev(f"y{u}")])
                lp.mark(f"tr{u}", k)
                T["hT", u] = lp.mark(f"hT{u}", act.act(self.hT[u][:, :], bank(2 * u, 128), ACT.Copy,
                                                       w=[k, lp.prev(f"m1{u}")]))

            def B(u):
                k = pe.mm(bank(2 * u + 1, F), self.hT[u][:, :], wa[:, bass.ds(ex_pe[u] * F, F)],
                          w=[T["hT", u], lp.prev(f"aT{u}")])
                lp.mark(f"m1{u}", k)
                T["a", u] = mid(self, u, bank(2 * u + 1, F), ex_dve.get(u), k, lp)

            def Cc(u):
                for f in range(NF):
                    k = pe.tr(bank(2 * u + 1, 128, 128 * f), self.ha[u][:, f * 128:(f + 1) * 128], self.c["ident"],
                              w=[T["a", u]], inc=(f == NF - 1))
                lp.mark(f"trm{u}", k)
                eng = act if NF == 2 and u % 2 else d
                if eng is act:
                    k = act.act(self.aT[u][:, 0:128 * NF], bank(2 * u + 1, 128 * NF), ACT.Copy, w=[k, lp.prev(f"m2{u}")])
                else:
                    k = d.cp(self.aT[u][:, 0:128 * NF], bank(2 * u + 1, 128 * NF), w=[k, lp.prev(f"m2{u}")])
                T["aT", u] = lp.mark(f"aT{u}", k)

            def D(u):
                for f in range(NF):
                    k = pe.mm(bank(2 * u, 128), self.aT[u][:, f * 128:(f + 1) * 128],
                              wb_[:, bass.ds(ex_pe[u] * (128 * NF) + 128 * f, 128)], first=(f == 0), last=(f == NF - 1),
                              w=[T["aT", u], lp.prev(f"y{u}")])
                lp.mark(f"m2{u}", k)
                src = bank(2 * u, 128)
                ws = [k, lp.prev(f"out{u}")]
                if b2 is None:
                    k = d.cp(self.y[u][:, :], src, w=ws)
                else:
                    d.wait(ws)
                    k = d.stt(self.y[u][:, :], src, yscale, b2[:, bass.ds(ex_dve[u] * C, C)], ALU.mult, ALU.add)
                lp.mark(f"y{u}", k)
                lp.mark(f"out{u}", act.dma(ys[bass.ds((i * U + u) * P, P), :], self.y[u][:, :], self.ch_out[u], w=[k]))

            for u in range(U):
                expert(u)
                A(u)
            A2(0)
            A2(1)
            B(0)
            A2(2)
            B(1)
            A2(3)
            B(2)
            Cc(0)
            B(3)
            D(0)
            Cc(1)
            D(1)
            Cc(2)
            D(2)
            Cc(3)
            D(3)

        self.p.run_loop(ntile // U, body)
        done = [self.dve.now(), self.act.now()]
        self.banks.free = [list(done) for _ in range(8)]
        return [Token(c, c.n, None) for c in self.ch_out]

    def dispatch(self, rows, xs, n, filled, w, limit=None):
        for t in range(NT):
            for j in range(n):
                self.pool.wait(list(w) + list(filled))
                if limit is None:
                    k = self.pool.scatter_rows(xs[:, :], self.idx[:, j, t:t + 1], rows[:, t, :], self.ch_row)
                else:
                    self.pool.eng.indirect_dma_start(
                        xs[:, :], bass.IndirectOffsetOnAxis(ap=self.idx[:, j, t:t + 1], axis=0), rows[:, t, :], None,
                        bounds_check=limit, oob_is_err=False).then_inc(self.ch_row.sem, 16)
                    k = self.ch_row.took()
        return k

    def collect(self, outs, ys, idxs, w):
        for t in range(NT):
            for o, j in zip(outs, idxs):
                k = self.pool.gather_rows(o[:, t, :], ys[:, :], self.idx[:, j, t:t + 1], self.ch_row, w=w)
        return k

    def clear_rows(self, xs, ntile):
        ch = self.p.channel(f"ch_zero{self.p.n_sb}", self.sp)
        self.p.n_sb += 1
        return self.sp.dma(xs[0:ntile * P, :].rearrange("(t p) c -> p t c", p=P),
                           self.zero[:, :].unsqueeze(1).broadcast_to((P, ntile, C)), ch, [self.k_zero])

    def start(self):
        sp, d, pool = self.sp, self.dve, self.pool
        ch = self.p.channel("ch_x", sp)
        self.k_x = sp.dma(self.x[:, :, :], self.ins["x"].rearrange("(t p) c -> p t c", p=P), ch)
        self.k_c = self.load(sp, self.c, "consts")
        self.k_w0 = [self.load(sp, self.w0, "w0"), self.load(sp, self.r0, "r0", rows=True)]
        self.zero = self.p.sbuf("zero", [P, C])
        self.k_zero = pool.fill(self.zero[:, :], 0.0)
        self.k_edge = pool.fill(self.xT[:, :, :], 0.0)
        dt = self.nc.dram_tensor
        self.xs = [dt(f"xs{n}", (t * P, C), F32, kind="Internal").ap() for n, t in enumerate((24, 24, 40, 40))]
        self.ys = [dt(f"ys{n}", (t * P, C), F32, kind="Internal").ap() for n, t in enumerate((24, 24, 40, 40))]
        self.k_clear = [self.clear_rows(x, t) for x, t in zip(self.xs, (24, 24, 40, 40))]
        self.k_w1 = [self.load(sp, self.w1, "w1"), self.load(sp, self.r1, "r1", rows=True)]
        self.k_w2 = [self.load(sp, self.w2, "w2"), self.load(sp, self.r2, "r2", rows=True)]

    def normed(self, w):
        self.dve.wait([self.k_x])
        k = self.layernorm(self.x, self.xn, w)
        self.k_xn = k
        self.k_xT = self.transposed(self.xn, lambda q: self.xT[:, 2 * q:2 * q + 2, 1:1 + NS], [k, self.k_c],
                                    w_dst=[self.k_edge, self.pe.now()])
        return k

    def gated(self, s, w):
        k = self.act.act(self.g[:, :, :], self.g[:, :, :], ACT.Silu, w=w)
        k = self.dve.tt(self.g[:, :, :], self.g[:, :, :], s[:, :, :], ALU.mult, w=[k])
        return self.dve.tt(self.x[:, :, :], self.x[:, :, :], self.g[:, :, :], ALU.add, w=[k])

    def layer0_linear_attention(self):
        pe, d, act, pool, c, w0 = self.pe, self.dve, self.act, self.pool, self.c, self.w0
        ar = self.arena
        e, r = ar[:, 0:512], ar[:, 512:1024]
        ue = [ar[:, 1024:1536], ar[:, 1536:2048]]
        t1 = ar[:, 2048:2560]
        ro = [ar[:, 2560:3072], ar[:, 3072:3584]]
        kt = ar[:, 3584:4096].rearrange("p (r c) -> p r c", c=C)
        kvm, mz, zz = ar[:, 4096:4224], ar[:, 4224:4232], ar[:, 4232:4240]
        km = self.v[11]
        last = {}
        for j in range(4):
            X = self.xT[:, 2 * j:2 * j + 2, 1:1 + NS]
            kin = [self.k_xT[j]] + self.k_w0
            for n, (w, b) in enumerate((("q", "q_b"), ("k", "k_b"))):
                i, ps, wb = self.banks.take()
                k = pe.mm(ps, w0[w], X, w=kin + wb)
                ke = act.act(e, ps, ACT.Exp, bias=w0[b], w=[k, last.get("u")])
                kr = act.act(r, ps, ACT.Relu, bias=w0[b], w=[k, last.get("u")])
                self.banks.give(i, kr)
                for h in range(2):
                    sl = slice(h * NS, (h + 1) * NS)
                    k = d.stt(ue[n][:, sl], e[:, sl], 1.0, r[:, sl], ALU.min, ALU.add,
                              w=[ke, kr, last.get(("den", n)), last.get(("rot", n))], acc=km[:, h:h + 1] if n else None)
                last["u"] = ku = k
                last["u", n] = ku
                i, ps, wb = self.banks.take()
                k = last["rot", n] = pe.mm(ps, c["swap"], ue[n], w=[ku] + wb)
                two = lambda a: a.rearrange("p (b n) -> p b n", n=NS)
                k1 = pool.tt(two(t1), two(ue[n]), grow(c["rope_cos"], 2), ALU.mult, w=[ku, last.get("t1"), self.k_c])
                k2 = d.tt(two(ro[n]), two(ps), grow(c["rope_sin"], 2), ALU.mult, w=[k, last.get(("ro", n))])
                self.banks.give(i, k2)
                last["t1"] = k = d.tt(ro[n], ro[n], t1, ALU.add, w=[k1, k2])
                last["r", n] = k
            for h in range(2):
                i, ps, wb = self.banks.take()
                for q in range(2):
                    k = pe.tr(ps[:, q * 128:(q + 1) * 128], ro[1][:, (2 * h + q) * 128:(2 * h + q + 1) * 128],
                              c["ident"], w=[last["r", 1]] + wb)
                k = act.act(kt[:, 0:2, :], ps[:, 0:256].rearrange("p (r c) -> p r c", c=C), ACT.Copy,
                            w=[k, last.get("kv")])
                self.banks.give(i, k)
                i, ps, wb = self.banks.take()
                for q in range(2):
                    kk = pe.mm(ps[:, 0:128], kt[:, q, :], self.xn[:, 4 * j + 2 * h + q, :], first=(q == 0),
                               last=(q == 1), w=[k, self.k_xn] + wb)
                last["kv"] = kk
                k = d.tt(kvm, ps[:, 0:128], c["kv_mask"], ALU.mult, w=[kk, last.get("o")])
                self.banks.give(i, k)
                kz = d.ts(mz, c["heads"], km[:, h:h + 1], w=[last["u", 1], last.get("o")])
                for q in range(2):
                    t = 4 * j + 2 * h + q
                    sl = slice((2 * h + q) * 128, (2 * h + q + 1) * 128)
                    i, ps, wb = self.banks.take()
                    pe.mm(ps[:, 0:128], ro[0][:, sl], kvm, w=[k, last["r", 0]] + wb)
                    pe.mm(ps[:, 128:136], ue[0][:, sl], mz, w=[kz])
                    for m in range(3):
                        b = 2 * j + h
                        kk = pe.mm(ps[:, 256:384], self.xT[:, b, m + 128 * q:m + 128 * q + 128],
                                   w0["lepe"][:, m * 128:(m + 1) * 128], first=(m == 0), last=(m == 2))
                    last["o"] = last["den", 0] = last["ro", 0] = last["ro", 1] = last["den", 1] = kk
                    k1 = d.ts(zz, ps[:, 128:136], 1e-6, op0=ALU.add, w=[kk, self.dve.now()])
                    k1 = d.rcp(zz, zz, w=[k1])
                    st = self.s[:, t, :]
                    k1 = d.tt(st.rearrange("p (h e) -> p h e", e=16), ps[:, 0:128].rearrange("p (h e) -> p h e", e=16),
                              grow_in(zz, 16), ALU.mult, w=[k1])
                    k1 = d.tt(st, st, ps[:, 256:384], ALU.add, w=[k1])
                    self.banks.give(i, k1)
        return d.tt(self.s[:, :, :], self.s[:, :, :], grow(self.r0["lepe_b"], NT), ALU.add, w=[k1])

    def layer0_attention(self):
        pe, d, act, pool, c = self.pe, self.dve, self.act, self.pool, self.c
        qkv = self.qkv
        for t in range(NT):
            i, ps, wb = self.banks.take()
            k = pe.mm(ps[:, 0:384], self.xT_tile(t), self.w0["qkv"], w=self.k_w0 + self.k_xT + wb)
            k = d.tt(qkv[:, t, :], ps[:, 0:384], self.r0["qkv_b"], ALU.add, w=[k])
            self.banks.give(i, k)
        kq = k
        prod = self.arena[:, 0:1024]
        sc = self.arena[:, 1024:2048]
        mx, sm = self.arena[:, 2048:2176], self.arena[:, 2176:2304]
        prod2 = self.arena[:, 2304:3328]
        ctx = self.t2

        def rows(part, h):
            return qkv[:, :, :].rearrange("p (s h) c -> p h s c", h=2)[:, h, :, part * 128:(part + 1) * 128]

        for h in range(2):
            for t in range(8):
                q = qkv[:, 2 * t + h, 0:128]
                k1 = pool.tt(prod.rearrange("p (s c) -> p s c", c=C), rows(1, h), grow(q, 8), ALU.mult,
                             w=[kq, d.now()]) if t % 3 == 2 else \
                    d.tt(prod.rearrange("p (s c) -> p s c", c=C), rows(1, h), grow(q, 8), ALU.mult, w=[kq, d.now()])
                k = d.red(sc[:, t * 128:(t + 1) * 128], prod.rearrange("p (a x) -> p a x", x=8), ALU.add,
                          w=[k1, act.now(), d.now()])
            ths = sc.rearrange("p (t s h) -> p t h s", s=8, h=16)
            th = lambda a: a.rearrange("p (t h) -> p t h", h=16)
            k = d.red(th(mx), ths, ALU.max, w=[k])
            tsh = sc.rearrange("p (t s h) -> p t s h", s=8, h=16)
            bc = lambda a: th(a).unsqueeze(2).broadcast_to((P, 8, 8, 16))
            k = d.tt(tsh, tsh, bc(mx), ALU.subtract, w=[k])
            k = act.act(sc, sc, ACT.Exp, scale=float(np.float32(8.0) ** np.float32(-0.5)), w=[k])
            k = d.red(th(sm), ths, ALU.add, w=[k])
            k = d.rcp(sm, sm, w=[k])
            ks = d.tt(tsh, tsh, bc(sm), ALU.mult, w=[k])
            for t in range(8):
                pr = prod2.rearrange("p (h x s) -> p h x s", h=16, x=8)
                pt = sc[:, t * 128:(t + 1) * 128].rearrange("p (s h) -> p h s", h=16).unsqueeze(2).broadcast_to((P, 16, 8, 8))
                v = rows(2, h).rearrange("p s (h x) -> p h x s", h=16)
                k1 = d.tt(pr, pt, v, ALU.mult, w=[ks, d.now()])
                k = d.red(ctx[:, 2 * t + h, :], prod2.rearrange("p (c s) -> p c s", s=8), ALU.add, w=[k1])
        kT = self.transposed(ctx, lambda q: self.tT[:, q * 512:(q + 1) * 512], [k], w_dst=[pe.now()])
        for t in range(NT):
            i, ps, wb = self.banks.take()
            k = pe.mm(ps[:, 0:128], self.tT[:, t * 128:(t + 1) * 128], self.w0["out"], w=kT + wb)
            k = d.tt(self.t1[:, t, :], ps[:, 0:128], self.xn[:, t, :], ALU.add, w=[k])
            self.banks.give(i, k)
        return d.tt(self.t1[:, :, :], self.t1[:, :, :], grow(self.r0["out_b"], NT), ALU.add, w=[k])

    def mid_gelu(self, F, b1):
        def mid(net, u, ps, ex, k, lp):
            d = net.dve
            d.wait([k, lp.prev(f"g{u}")])
            k = d.put(lambda: d.eng.tensor_tensor(net.hm[u][:, 0:F], ps, b1[:, bass.ds(ex * F, F)], ALU.add))
            k = net.act.act(net.ha[u][:, 0:F], net.hm[u][:, 0:F], ACT.Gelu, w=[k, lp.prev(f"trm{u}")])
            return lp.mark(f"g{u}", k)
        return mid

    def layer0_mixture(self, k_in):
        d, r0, w0 = self.dve, self.r0, self.w0
        h = self.t1
        k = self.layernorm(self.t1, h, lambda t: [k_in], r0["ln1_g"], r0["ln1_b"])
        kT = self.transposed(h, lambda q: self.tT[:, q * 512:(q + 1) * 512], [k], w_dst=[self.pe.now()])
        lg = self.k8[0][:, :, :]
        k = self.logits(lambda t: self.tT[:, t * 128:(t + 1) * 128], w0["router"], r0["router_b"], lg, kT)
        oh, m, k = self.top2(lg, [k])
        i1, i2 = self.v[6][:, :], self.v[7][:, :]
        io = grow(self.c["iota8"], NT)
        k = self.place(oh[0][:, :, :], io, i1, [k])
        k = self.place(oh[1][:, :, :], io, i2, [k])
        k = d.tt(i1, i1, i2, ALU.max, w=[k])
        k = d.tt(oh[0][:, :, :], io, grow_in(i1, E), ALU.is_equal, w=[k])
        k, kt = self.slots([oh[0]], [k])
        kd = self.dispatch(h, self.xs[0], 1, [self.k_clear[0]], [k])
        ko = self.experts(self.xs[0], self.ys[0], 24, kt, [kd, kt], self.mid_gelu(C, r0["b1"]), C, 1,
                          w0["w1"], w0["w2"], r0["b1"], r0["b2"])
        kc = self.collect([self.t2], self.ys[0], [0], ko + [d.now()])
        k = d.tt(self.t1[:, :, :], self.t1[:, :, :], self.t2[:, :, :], ALU.add, w=[kc])
        return self.layernorm(self.t1, self.g, lambda t: [k], r0["ln2_g"], r0["ln2_b"])

    def layer0(self):
        self.normed(lambda t: [self.k_x])
        ks = self.layer0_linear_attention()
        k = self.layer0_attention()
        k = self.layer0_mixture(k)
        return self.gated(self.s, [k, ks])

    def layer1_attention(self):
        pe, d, act, pool, w1, r1 = self.pe, self.dve, self.act, self.pool, self.w1, self.r1
        start = [e.now() for e in (pe, d, act, pool)]
        k = self.layernorm(self.xn, self.t1, lambda t: [self.k_xn])
        kT = self.transposed(self.t1, lambda q: self.tT[:, q * 512:(q + 1) * 512], [k] + self.k_w1,
                             gain=w1["ln_g"], bias=w1["ln_b"], w_dst=[pe.now()])
        wk = self.work
        for e in (d, act, pool):
            e.wait(start)
        hid = [wk[:, 0:1024].rearrange("p (r n) -> p r n", n=512), wk[:, 1024:2048].rearrange("p (r n) -> p r n", n=512)]
        qk, qT, kk_ = wk[:, 2048:2304], wk[:, 2304:2560], wk[:, 2560:2816]
        at = [wk[:, 2816:3328], wk[:, 3328:3840]]
        rl = wk[:, 3840:4352]
        og, ogT = wk[:, 4352:4864], wk[:, 4864:5376]
        last = {}
        for b in range(NB):
            hb = hid[b % 2]
            for r in range(2):
                t = 2 * b + r
                i, ps, wb = self.banks.take()
                k = pe.mm(ps, self.tT[:, t * 128:(t + 1) * 128], w1["hidden"], w=kT + wb)
                k = d.tt(hb[:, r, :], ps, r1["hidden_b"], ALU.add, w=[k, last.get(("av", b - 2)), last.get(("og", b - 2))])
                self.banks.give(i, k)
            kh = act.act(hb, hb, ACT.Silu, w=[k])
            i, ps, wb = self.banks.take()
            k = pe.mm(ps[:, 0:NS], w1["qk"], self.tT[:, b * NS:(b + 1) * NS], w=kT + wb)
            k = act.act(qk, ps[:, 0:NS], ACT.Silu, bias=w1["qk_b"], w=[k, last.get("qk")])
            self.banks.give(i, k)
            kq = d.ts(qT, qk, w1["osw"][:, 0:1], w1["osb"][:, 0:1], ALU.mult, ALU.add, w=[k, last.get("sim")])
            last["qk"] = kkk = d.ts(kk_, qk, w1["osw"][:, 1:2], w1["osb"][:, 1:2], ALU.mult, ALU.add, w=[k])
            a = at[b % 2]
            i, ps, wb = self.banks.take()
            for r in range(2):
                k = pe.mm(ps[:, r * NS:(r + 1) * NS], kk_[:, r * 128:(r + 1) * 128], qT, w=[kq, kkk] + wb)
            last["sim"] = k
            k = act.act(rl, ps, ACT.Relu, scale=1.0 / NS, w=[k, last.get("a")])
            self.banks.give(i, k)
            last["a"] = ka = pool.tt(a, rl, rl, ALU.mult, w=[k, last.get(("av", b - 2))])
            for r in range(2):
                i, ps, wb = self.banks.take()
                for j in range(2):
                    k = pe.mm(ps[:, 0:256], a[:, j * NS + r * 128:j * NS + r * 128 + 128], hb[:, j, 0:256],
                              first=(j == 0), last=(j == 1), w=[ka, kh] + wb)
                last["av", b] = k
                k = d.tt(og[:, r * 256:(r + 1) * 256], ps[:, 0:256], hb[:, r, 256:512], ALU.mult,
                         w=[k, last.get("ogtr")])
                self.banks.give(i, k)
            last["og", b] = k
            i, ps, wb = self.banks.take()
            for r in range(4):
                k = pe.tr(ps[:, r * 128:(r + 1) * 128], og[:, r * 128:(r + 1) * 128], self.c["ident"], w=[k] + wb if r == 0 else (),
                          inc=(r == 3))
            last["ogtr"] = k
            k = act.act(ogT, ps, ACT.Copy, w=[k, last.get("wout")])
            self.banks.give(i, k)
            i, ps, wb = self.banks.take()
            for r in range(2):
                for f in range(2):
                    kk = pe.mm(ps[:, r * 128:(r + 1) * 128], ogT[:, (2 * r + f) * 128:(2 * r + f + 1) * 128],
                               w1["out"][:, f * 128:(f + 1) * 128], first=(f == 0), last=(f == 1), w=[k] + wb)
            last["wout"] = kk
            k = d.tt(self.s[:, 2 * b:2 * b + 2, :], ps[:, 0:256].rearrange("p (r c) -> p r c", c=C),
                     grow(r1["out_b"], 2), ALU.add, w=[kk])
            self.banks.give(i, k)
        return k

    def pair_softmax(self, m, w1, w2, w):
        d, t = self.dve, self.v[9][:, :]
        k = d.tt(t, m[1], m[0], ALU.subtract, w=w)
        k = self.act.act(t, t, ACT.Exp, w=[k])
        k = d.ts(w1, t, 1.0, op0=ALU.add, w=[k])
        k = d.rcp(w1, w1, w=[k])
        return d.tt(w2, t, w1, ALU.mult, w=[k])

    def layer1_slots(self):
        d, pe, c = self.dve, self.pe, self.c
        CAP = (TOK * 5 + 4 * E - 1) // (4 * E)
        lg = self.k8[0][:, :, :]
        k = self.logits(self.xT_tile, self.w1["router"], self.r1["router_b"], lg, self.k_xT + self.k_w1)
        oh, m, k = self.top2(lg, [k])
        g = [self.gates[:, 0, :], self.gates[:, 1, :]]
        k = self.pair_softmax(m, g[0], g[1], [k])
        val, u = self.k8[0][:, :, :], self.k8[3][:, :, :]
        k1 = d.tt(val, oh[0][:, :, :], grow_in(g[0], E), ALU.mult, w=[k])
        k2 = d.tt(u, oh[1][:, :, :], grow_in(g[1], E), ALU.mult, w=[k])
        k = d.tt(val, val, u, ALU.add, w=[k1, k2])
        thr, cand, step = self.ei, self.p.sbuf("cand", [P, E], I32), self.p.sbuf("step", [P, E], I32)
        part = self.e8[0][:, :]
        bits_i = self.p.sbuf("bits_i", [P, 30], I32)
        k = d.cp(bits_i[:, :], c["bits"], w=[k])
        k = d.fill(thr[:, :], 0, w=[k])
        pe.wait([k])

        def body(i, lp):
            bit_i = bits_i[:, bass.ds(i, 1)]
            bit_f = self.bits_f[:, bass.ds(i, 1)]
            k = d.tt(cand[:, :], thr[:, :], bit_i.broadcast_to((P, E)), ALU.bitwise_or, w=[lp.prev("thr")])
            k = d.tt(u, val, grow(cand[:, :].bitcast(F32), NT), ALU.is_ge, w=[k])
            k = d.red(part, u.rearrange("p t e -> p e t"), ALU.add, w=[k, lp.prev("mm")])
            i0, ps, wb = self.banks.take()
            k = lp.mark("mm", pe.mm(ps[:, 0:E], c["ones"], part, w=[k] + wb))
            d.wait([k])
            k = d.ts(step[:, :], ps[:, 0:E], float(CAP), bit_f, ALU.is_ge, ALU.mult)
            self.banks.give(i0, k)
            lp.mark("thr", d.tt(thr[:, :], thr[:, :], step[:, :], ALU.bitwise_or, w=[k]))

        self.bits_f = c["bits"]
        self.banks.run_loop(30, body)
        k = d.now()
        over, tie, both = self.k8[4], self.p.sbuf("tie", [P, NT, E]), self.p.sbuf("chosen", [P, NT, E])
        tb = grow(thr[:, :].bitcast(F32), NT)
        k1 = d.tt(over[:, :, :], val, tb, ALU.is_gt, w=[k])
        k2 = d.tt(both[:, :, :], oh[0][:, :, :], oh[1][:, :, :], ALU.add, w=[k])
        k3 = d.tt(tie[:, :, :], val, tb, ALU.is_equal, w=[k])
        k3 = d.tt(tie[:, :, :], tie[:, :, :], both[:, :, :], ALU.mult, w=[k2, k3])
        part2 = self.e8[1][:, :]
        k1 = d.red(part, over[:, :, :].rearrange("p t e -> p e t"), ALU.add, w=[k1])
        i0, ps, wb = self.banks.take()
        k1 = pe.mm(ps[:, 0:E], c["ones"], part, w=[k1] + wb)
        k1 = d.ts(part2, ps[:, 0:E], -1.0, float(CAP), ALU.mult, ALU.add, w=[k1])
        self.banks.give(i0, k1)
        rank, incl = self.k8[6], self.k8[7][:, :, :].rearrange("p t e -> p (t e)")
        k = self.prefix(tie, rank[:, :, :], incl, [k3, k1])
        k = d.tt(u, rank[:, :, :], grow(part2, NT), ALU.is_lt, w=[k])
        k = d.tt(u, u, tie[:, :, :], ALU.mult, w=[k])
        k = d.tt(over[:, :, :], over[:, :, :], u, ALU.add, w=[k])
        k = self.prefix(over, rank[:, :, :], incl, [k])
        k = d.tt(rank[:, :, :], rank[:, :, :], grow(c["iota384"], NT), ALU.add, w=[k])
        took, slot, t = self.v[8][:, :], self.v[9][:, :], self.v[0][:, :]
        for n in range(2):
            k = self.place(oh[n][:, :, :], over[:, :, :], took, [k])
            k = self.place(oh[n][:, :, :], rank[:, :, :], slot, [k])
            k = d.tt(t, slot, took, ALU.mult, w=[k])
            k = d.cp(self.idx[:, 2 + n, :], t, w=[k])
            k = d.ts(slot, took, -65536.0, 65536.0, ALU.mult, ALU.add, w=[k])
            k = d.tt(t, t, slot, ALU.add, w=[k])
            k = d.cp(self.idx[:, n, :], t, w=[k])
            k = d.tt(g[n], g[n], took, ALU.mult, w=[k])
        kt = d.cp(self.tile_e[:, :], c["tile_third"][0:1, :], w=[k])
        return kt

    def weighted(self, out, ins, w):
        d = self.dve
        for t in range(NT):
            k = d.stt(out[:, t, :], ins[0][:, t, :], self.gates[:, 0, t:t + 1], out[:, t, :], ALU.mult, ALU.add, w=w)
        w = [k]
        for t in range(NT):
            k = d.stt(out[:, t, :], ins[1][:, t, :], self.gates[:, 1, t:t + 1], out[:, t, :], ALU.mult, ALU.add, w=w)
        return k

    def layer1_mixture(self, k_slots, k_free):
        d, r1 = self.dve, self.r1
        kd = self.dispatch(self.xn, self.xs[1], 2, [self.k_clear[1]], [k_slots], limit=24 * P - 1)
        ko = self.experts(self.xs[1], self.ys[1], 24, k_slots, [kd, k_slots] + k_free, self.mid_gelu(512, r1["b1"]), 512, 4,
                          self.w1["w1"], self.w1["w2"], r1["b1"], r1["b2"])
        both = [self.work[:, n * 2048:(n + 1) * 2048].rearrange("p (t c) -> p t c", c=C) for n in range(2)]
        kc = self.collect(both, self.ys[1], [2, 3], ko + [d.now(), self.act.now(), self.pe.now()])
        k = d.cp(self.t1[:, :, :], self.xn[:, :, :])
        k = self.weighted(self.t1, both, [kc, k])
        return self.layernorm(self.t1, self.g, lambda t: [k], r1["gamma"], r1["beta"])

    def layer1(self):
        k = self.dve.now()
        self.normed(lambda t: [k])
        ks = self.layer1_attention()
        kr = self.layer1_slots()
        k = self.layer1_mixture(kr, [ks, self.pe.now(), self.act.now(), self.pool.now()])
        return self.gated(self.s, [k, ks])

    def load_layer3(self):
        w = [e.now() for e in (self.pe, self.dve, self.act, self.pool)] + self.k_w0 + self.k_w1
        self.k_w3 = [self.load(self.sp, self.w3, "w3", w=w), self.load(self.sp, self.r3, "r3", w=w, rows=True)]

    def layer2_attention(self):
        pe, d, act, pool, w2, r2, c = self.pe, self.dve, self.act, self.pool, self.w2, self.r2, self.c
        start = [e.now() for e in (pe, d, act, pool)]
        for e in (d, act, pool):
            e.wait(start)
        wk = self.work
        wq, wkk = wk[:, 0:128], wk[:, 128:256]
        bq = wk[:, 256:258]
        i, ps, wb = self.banks.take()
        pe.mm(ps[:, 0:128], w2["wq"], c["rot2"], w=self.k_w2 + wb, inc=False)
        pe.mm(ps[:, 128:256], w2["wk"], c["rot2"], inc=False)
        pe.mm(ps[:, 256:257], c["rot2"], w2["bq"], inc=False)
        k = pe.mm(ps[:, 257:258], c["rot2"], w2["bk"])
        k0 = d.cp(wk[:, 0:258], ps[:, 0:258], w=[k])
        self.banks.give(i, k0)
        last = {}
        for b in range(NB):
            X = self.xT[:, b, 1:1 + NS]
            o = 512 + (b % 2) * 2304
            qT, kT = wk[:, o:o + 256], wk[:, o + 256:o + 512]
            v = wk[:, o + 512:o + 768]
            pr, pT = wk[:, o + 768:o + 1280], wk[:, o + 1280:o + 1792]
            st = wk[:, o + 1792:o + 1800]
            old = [last.get(("pv", b - 2))]
            for dst, w, bb in ((qT, wq, 0), (kT, wkk, 1)):
                i, ps, wb = self.banks.take()
                k = pe.mm(ps[:, 0:NS], w, X, w=self.k_xT + [k0] + wb)
                k = d.stt(dst, ps[:, 0:NS], bq[:, bb:bb + 1], c["rope2"], ALU.add, ALU.mult, w=[k] + old)
                self.banks.give(i, k)
            kqk = k
            i, ps, wb = self.banks.take()
            for r in range(2):
                k = pe.mm(ps[:, r * 128:(r + 1) * 128], self.xT_tile(2 * b + r), w2["wv"], w=wb)
            kv = d.tt(v.rearrange("p (r c) -> p r c", c=C), ps[:, 0:256].rearrange("p (r c) -> p r c", c=C),
                      grow(r2["bv"], 2), ALU.add, w=[k] + old)
            self.banks.give(i, kv)
            i, ps, wb = self.banks.take()
            for r in range(2):
                k = pe.mm(ps[:, r * NS:(r + 1) * NS], qT[:, r * 128:(r + 1) * 128], kT, w=[kqk] + wb)
            k1 = d.red(st[:, 0:2], ps.rearrange("p (r n) -> p r n", n=NS), ALU.max, w=[k] + old)
            k1 = d.ts(st[:, 2:4], st[:, 0:2], -0.125, w=[k1])
            for r in range(2):
                k = act.act(pr[:, r * NS:(r + 1) * NS], ps[:, r * NS:(r + 1) * NS], ACT.Exp, bias=st[:, 2 + r:3 + r],
                            scale=0.125, acc=st[:, 4 + r:5 + r], w=[k1])
            self.banks.give(i, k)
            kr = d.rcp(st[:, 6:8], st[:, 4:6], w=[k])
            i, ps, wb = self.banks.take()
            for r in range(2):
                for q in range(2):
                    kk = pe.tr(ps[:, r * NS + q * 128:r * NS + (q + 1) * 128], pr[:, q * NS + r * 128:q * NS + (r + 1) * 128],
                               c["ident"], w=[k] + wb, inc=(r + q == 2))
            k = act.act(pT, ps, ACT.Copy, w=[kk] + old)
            self.banks.give(i, k)
            i, ps, wb = self.banks.take()
            for q in range(2):
                for r in range(2):
                    kk = pe.mm(ps[:, q * 128:(q + 1) * 128], pT[:, r * NS + q * 128:r * NS + (q + 1) * 128],
                               v[:, r * 128:(r + 1) * 128], first=(r == 0), last=(r == 1), w=[k, kv] + wb)
            last["pv", b] = kk
            for q in range(2):
                k = d.ts(self.s[:, 2 * b + q, :], ps[:, q * 128:(q + 1) * 128], st[:, 6 + q:7 + q], w=[kk, kr])
            self.banks.give(i, k)
            last["s"] = k
        return k

    def layer2_recurrence(self):
        pe, d, act, pool, w2, r2 = self.pe, self.dve, self.act, self.pool, self.w2, self.r2
        wk = self.work
        base = 512 + 2 * 2304
        cc = [wk[:, base:base + 256], wk[:, base + 256:base + 512]]
        f, ig, g = (wk[:, base + 512 + 256 * n:base + 768 + 256 * n] for n in range(3))
        k = pool.ts(cc[0], grow(w2["c0"], 1)[:, 0, :].broadcast_to((P, 256)), 1.0, w=self.k_w2)
        for t in range(8):
            X = self.xT[:, t, 1:1 + NS]
            c, cn = cc[t % 2], cc[(t + 1) % 2]
            ks = []
            for dst, w, u, b, fn in ((f, "wf", "uf", "bf", ACT.Sigmoid), (ig, "wi", "ui", "bi", ACT.Sigmoid), (g, "wc", "uc", "bc", ACT.Tanh)):
                i, ps, wb = self.banks.take()
                pe.mm(ps[:, 0:NS], w2[w], X, last=False, w=self.k_xT + wb)
                kk = pe.mm(ps[:, 0:NS], w2[u], c, first=False, w=[k])
                kk = act.act(dst, ps[:, 0:NS], fn, bias=w2[b], w=[kk, k])
                self.banks.give(i, kk)
                ks.append(kk)
            k1 = d.tt(cn, f, c, ALU.mult, w=[ks[0]])
            k2 = d.tt(g, ig, g, ALU.mult, w=[ks[2]])
            k = d.tt(cn, cn, g, ALU.add, w=[k1, k2])
        cT = cc[0]
        for t in range(NT):
            i, ps, wb = self.banks.take()
            pe.mm(ps[:, 0:128], self.xT_tile(t), w2["wo"], last=False, w=wb)
            kk = pe.mm(ps[:, 0:128], cT[:, 128 * (t % 2):128 * (t % 2) + 128], w2["uo"], first=False, w=[k])
            kk = d.tt(self.g[:, t, :], ps[:, 0:128], r2["bo"], ALU.add, w=[kk])
            self.banks.give(i, kk)
        return act.act(self.g[:, :, :], self.g[:, :, :], ACT.Tanh, w=[kk])

    def layer2(self):
        k = self.dve.now()
        self.normed(lambda t: [k])
        ks = self.layer2_attention()
        k = self.layer2_recurrence()
        return self.gated(self.s, [k, ks])

    def layer3_gates(self):
        pe, d, act, pool, w3, r3 = self.pe, self.dve, self.act, self.pool, self.w3, self.r3
        start = [e.now() for e in (pe, d, act, pool)]
        k = self.layernorm(self.xn, self.t1, lambda t: [self.k_xn])
        kT = self.transposed(self.t1, lambda q: self.tT[:, q * 512:(q + 1) * 512], [k] + self.k_w3,
                             gain=w3["ln_g"], bias=w3["ln_b"], w_dst=[pe.now()])
        self.k_nT = kT
        tile = lambda t: self.tT[:, t * 128:(t + 1) * 128]
        hl = self.stats[:, :, 0:2]
        k = self.logits(tile, w3["halt"], r3["halt_b"], hl, kT)
        alpha, rem, wsum, h = (self.v[i][:, :] for i in (11, 6, 12, 8))
        self.alpha, self.wsum = alpha, wsum
        ka = act.act(alpha, hl[:, :, 0], ACT.Sigmoid, w=[k])
        for step in range(3):
            if step < 2:
                k = act.act(h, hl[:, :, 1], ACT.Sigmoid, bias=r3["step_b"][:, step:step + 1], w=[k])
                if step == 0:
                    k1 = d.cp(wsum, h, w=[k])
                    k2 = d.ts(rem, h, -1.0, 1.0, ALU.mult, ALU.add, w=[k])
                    k = d.ts(rem, rem, 0.0, op0=ALU.max, w=[k1, k2])
                else:
                    k = d.tt(h, h, rem, ALU.mult, w=[k])
                    k1 = d.tt(wsum, wsum, h, ALU.add, w=[k])
                    k = d.tt(rem, rem, h, ALU.subtract, w=[k1])
                    k = d.ts(rem, rem, 0.0, op0=ALU.max, w=[k])
            else:
                k = d.tt(wsum, wsum, rem, ALU.add, w=[k])
        for e in (d, act, pool):
            e.wait(start)
        wk = self.work
        xp = wk[:, 0:518].rearrange("p (b n) -> p b n", b=2)
        y, sg, z, xc = (wk[:, 520 + 512 * n:1032 + 512 * n] for n in range(4))
        two = lambda a: a.rearrange("p (b n) -> p b n", n=NS)
        kf = pool.fill(wk[:, 0:518], 0.0)
        last = {}
        for j in range(4):
            X = self.tT[:, j * 512:(j + 1) * 512]
            i, ps, wb = self.banks.take()
            k = pe.mm(ps, w3["ssm"][:, 0:128], X, w=kT + wb)
            k = act.act(xp[:, :, 3:3 + NS], two(ps), ACT.Copy, w=[k, kf, last.get("y")])
            self.banks.give(i, k)
            cw = w3["conv_w"]
            k = d.ts(two(y), xp[:, :, 0:NS], cw[:, 0:1], w3["conv_b"], ALU.mult, ALU.add, w=[k, last.get("sg")])
            for m in range(1, 4):
                k = d.stt(two(y), xp[:, :, m:m + NS], cw[:, m:m + 1], two(y), ALU.mult, ALU.add, w=[k])
            last["y"] = k
            last["sg"] = k1 = act.act(sg, y, ACT.Sigmoid, w=[k, last.get("xc")])
            i, ps, wb = self.banks.take()
            k = pe.mm(ps, w3["ssm"][:, 128:256], X, w=wb)
            k2 = act.act(z, ps, ACT.Sigmoid, w=[k])
            self.banks.give(i, k2)
            k = pool.tt(xc, y, sg, ALU.mult, w=[k1, last.get("out")])
            k = last["xc"] = d.tt(xc, xc, z, ALU.mult, w=[k, k2])
            last["sg"] = k
            i, ps, wb = self.banks.take()
            for q in range(4):
                kk = pe.mm(ps[:, q * 128:(q + 1) * 128], xc[:, q * 128:(q + 1) * 128], w3["ssm_out"], w=[k] + wb)
            last["out"] = kk
            k = d.cp(self.s[:, 4 * j:4 * j + 4, :], ps.rearrange("p (r c) -> p r c", c=C), w=[kk])
            self.banks.give(i, k)
            i, ps, wb = self.banks.take()
            for q in range(4):
                kk = pe.mm(ps[:, q * 128:(q + 1) * 128], tile(4 * j + q), w3["gate"], w=wb)
            k = act.act(self.g[:, 4 * j:4 * j + 4, :], ps.rearrange("p (r c) -> p r c", c=C), ACT.Sigmoid, w=[kk])
            self.banks.give(i, k)

    def layer3_attention(self):
        pe, d, act, pool, w3, c = self.pe, self.dve, self.act, self.pool, self.w3, self.c
        wk = self.work
        start = [e.now() for e in (pe, d, act, pool)]
        for e in (d, act, pool):
            e.wait(start)
        at = [0]

        def part(n):
            at[0] += n
            return wk[:, at[0] - n:at[0]]

        nb = part(256)
        qP, kP = part(1024), part(1024)
        qP3, kP3 = (a.rearrange("p (g n) -> p g n", g=4) for a in (qP, kP))
        V = part(1024)
        V4 = V.rearrange("p (r h x) -> p r h x", r=2, h=16)
        mp = part(1024)
        mp4 = mp.rearrange("p (r h x) -> p r h x", r=2, h=16)
        PT = [part(512) for _ in range(4)]
        oT = [part(256) for _ in range(2)]
        ot = part(256).rearrange("p (r c) -> p r c", r=2)
        otT = part(256)
        den = part(8).rearrange("p (r g) -> p r g", r=2)
        k1 = pool.fill(V, 0.0)
        k1 = pool.fill(V4[:, :, :, 8], 1.0, w=[k1])
        k2 = pool.fill(mp, 0.0)
        for e in (pe, d, act):
            e.wait([k1, k2])
        scale = float(np.float32(8.0) ** np.float32(-0.5))

        def body(b, lp):
            L = {}
            k = act.act(nb, self.tT[:, bass.ds(b * NS, NS)], ACT.Copy, w=[lp.prev("proj")])
            knb = k
            for n, (dst, w) in enumerate(((qP3, "q"), (kP3, "k"))):
                for g2 in range(2):
                    i, ps, wb = self.banks.take()
                    for g in range(2):
                        gg = 2 * g2 + g
                        k = pe.mm(ps[:, g * NS:(g + 1) * NS], w3[w][:, gg * 128:(gg + 1) * 128], nb, w=[knb] + wb)
                    src = ps.rearrange("p (g n) -> p g n", g=2)
                    old = [lp.prev("pass2")]
                    if n:
                        k = act.act(dst[:, 2 * g2:2 * g2 + 2, :], src, ACT.Identity, bias=c["one_row8"], w=[k] + old)
                    else:
                        k = d.cp(dst[:, 2 * g2:2 * g2 + 2, :], src, w=[k] + old)
                    self.banks.give(i, k)
                    L[n, g2] = k
            i, ps, wb = self.banks.take()
            for r in range(2):
                k = pe.mm(ps[:, r * 128:(r + 1) * 128], nb[:, r * 128:(r + 1) * 128], w3["v"], w=wb)
            lp.mark("proj", k)
            kV = d.cp(V4[:, :, :, 0:8], ps[:, 0:256].rearrange("p (r h x) -> p r h x", r=2, h=16), w=[k, lp.prev("pv")])
            self.banks.give(i, kV)
            for gp, r in ((0, 0), (0, 1), (1, 0), (1, 1)):
                for g in range(4):
                    i, ps, wb = self.banks.take()
                    for hh in range(2):
                        g4, p0 = 2 * gp + hh, 32 * g
                        k = pe.mm(ps[:, hh * NS:(hh + 1) * NS], qP3[p0:p0 + 32, g4, r * 128:(r + 1) * 128],
                                  kP3[p0:p0 + 32, g4, :], w=[L[0, g4 // 2], L[1, g4 // 2]] + wb)
                    out = mp4[:, r, 8 * gp + g:8 * gp + g + 5:4, 8]
                    src = ps.rearrange("p (h n) -> p h n", h=2)
                    d.wait([k, lp.prev("mtr")])
                    k = d.put(lambda: d.eng.tensor_reduce(out, src, AX, ALU.max, negate=True))
                    self.banks.give(i, k)
            kp1 = pe.now()
            kmax = k
            for g2 in range(2):
                i, ps, wb = self.banks.take()
                for g in range(2):
                    for r in range(2):
                        gg = 2 * g2 + g
                        k = pe.tr(ps[:, (2 * g + r) * 128:(2 * g + r + 1) * 128], mp[:, r * 512 + gg * 128:r * 512 + (gg + 1) * 128],
                                  c["ident"], w=[kmax] + wb)
                dst = qP[:, g2 * 512:(g2 + 1) * 512]
                k = d.tt(dst, dst, ps, ALU.add, w=[k, kp1])
                self.banks.give(i, k)
                L["q2", g2] = k
            lp.mark("mtr", pe.now())
            first, pend = {}, []

            def pv(g4):
                i, po, wb = self.banks.take()
                for g in range(4):
                    for kt in range(2):
                        k = pe.mm(po[32 * g:32 * g + 32, 0:NS], V4[:, kt, 4 * g4 + g, :], PT[g][:, kt * NS:(kt + 1) * NS],
                                  first=(kt == 0), last=(kt == 1), w=[first["e", g4, g], kV] + wb)
                    first["pv", g4, g] = lp.mark(f"pv{g}", k)
                lp.mark("pv", k)
                o = oT[g4 % 2]
                k = act.act(o, po[:, 0:NS], ACT.Copy, w=[k, first.get(("otr", g4 - 2), lp.prev(f"otr{g4 % 2}"))])
                self.banks.give(i, k)
                i, ps, wb = self.banks.take()
                for r in range(2):
                    k = pe.tr(ps[:, r * 128:(r + 1) * 128], o[:, r * 128:(r + 1) * 128], c["ident"], w=[k] + wb if r == 0 else ())
                first["otr", g4] = lp.mark(f"otr{g4 % 2}", k)
                s4 = ps[:, 0:256].rearrange("p (r g x) -> p r g x", r=2, g=4)
                k = d.rcp(den, s4[:, :, :, 8], w=[k, d.now()])
                dst = ot.rearrange("p r (h x) -> p r h x", h=16)[:, :, 4 * g4:4 * g4 + 4, :]
                bc = den.unsqueeze(3).broadcast_to((P, 2, 4, 8))
                k = d.tt(dst, s4[:, :, :, 0:8], bc, ALU.mult, w=[k, lp.prev("ottr")])
                self.banks.give(i, k)
                return k

            for g4 in range(4):
                for g in range(4):
                    i, ps, wb = self.banks.take()
                    for kt in range(2):
                        k = pe.mm(ps[:, kt * NS:(kt + 1) * NS], kP3[32 * g:32 * g + 32, g4, kt * 128:(kt + 1) * 128],
                                  qP3[32 * g:32 * g + 32, g4, :], w=[L["q2", g4 // 2]] + wb)
                    lp.mark("pass2", k)
                    old = first.get(("pv", g4 - 1, g), lp.prev(f"pv{g}"))
                    k = act.act(PT[g], ps, ACT.Exp, scale=scale, w=[k, old])
                    self.banks.give(i, k)
                    first["e", g4, g] = k
                ko = pv(g4)
            i, ps, wb = self.banks.take()
            for r in range(2):
                k = pe.tr(ps[:, r * 128:(r + 1) * 128], ot[:, r, :], c["ident"], w=[ko] + wb if r == 0 else ())
            lp.mark("ottr", k)
            k = act.act(otT, ps[:, 0:256], ACT.Copy, w=[k, lp.prev("wout")])
            self.banks.give(i, k)
            i, ps, wb = self.banks.take()
            for r in range(2):
                k = pe.mm(ps[:, r * 128:(r + 1) * 128], otT[:, r * 128:(r + 1) * 128], w3["attn_out"], w=[k] + wb if r == 0 else ())
            lp.mark("wout", k)
            d.wait([k])
            k = d.put(lambda: d.eng.tensor_copy(self.t1[:, bass.ds(2 * b, 2), :], ps[:, 0:256].rearrange("p (r c) -> p r c", r=2)))
            self.banks.give(i, k)

        self.banks.run_loop(8, body)
        return d.now()

    def layer3_mixture(self, k):
        d, act, pool, r3, w3 = self.dve, self.act, self.pool, self.r3, self.w3
        s, t1, g = self.s, self.t1, self.g
        A = lambda t: t[:, :, :]
        k = d.tt(A(t1), A(t1), A(g), ALU.mult, w=[k, act.now()])
        k = d.tt(A(t1), A(t1), A(s), ALU.subtract, w=[k])
        k = d.tt(A(t1), A(t1), grow_in(self.alpha, C), ALU.mult, w=[k])
        k = d.tt(A(s), A(s), A(t1), ALU.add, w=[k])
        k = d.tt(A(s), A(s), grow(r3["ls1"], NT), ALU.mult, w=[k])
        k = d.tt(A(s), A(s), A(self.xn), ALU.add, w=[k])
        k = self.layernorm(s, t1, lambda t: [k], r3["ln2_g"], r3["ln2_b"])
        kT = self.transposed(t1, lambda q: self.tT[:, q * 512:(q + 1) * 512], [k], w_dst=[self.pe.now()])
        lg = self.k8[0][:, :, :]
        zero8 = self.zero[:, 0:8]
        k = self.logits(lambda t: self.tT[:, t * 128:(t + 1) * 128], w3["router"], zero8, lg, kT)
        oh, m, k = self.top2(lg, [k])
        Z, p2, sm = self.v[0][:, :], self.v[1][:, :], self.v[2][:, :]
        k1 = d.tt(lg, lg, grow_in(m[0], E), ALU.subtract, w=[k])
        k2 = d.tt(p2, m[1], m[0], ALU.subtract, w=[k])
        k1 = act.act(lg, lg, ACT.Exp, w=[k1])
        k2 = act.act(p2, p2, ACT.Exp, w=[k2])
        k = d.red(Z, lg, ALU.add, w=[k1])
        k = d.rcp(Z, Z, w=[k])
        k = d.tt(p2, p2, Z, ALU.mult, w=[k, k2])
        k = d.tt(sm, p2, Z, ALU.add, w=[k])
        k = d.ts(sm, sm, 1e-8, op0=ALU.add, w=[k])
        k = d.rcp(sm, sm, w=[k])
        k1 = d.tt(self.gates[:, 0, :], Z, sm, ALU.mult, w=[k])
        k2 = d.tt(self.gates[:, 1, :], p2, sm, ALU.mult, w=[k])
        k, kt = self.slots(oh, [k1, k2])
        kd = self.dispatch(t1, self.xs[2], 2, [self.k_clear[2]], [k])

        def mid(net, u, ps, ex, k, lp):
            k = act.act(net.hm[u][:, 0:256], ps[:, 0:256], ACT.Silu, w=[k, lp.prev(f"g{u}")])
            return lp.mark(f"g{u}", d.tt(net.ha[u][:, 0:256], net.hm[u][:, 0:256], ps[:, 256:512], ALU.mult,
                                         w=[k, lp.prev(f"trm{u}")]))

        ko = self.experts(self.xs[2], self.ys[2], 40, kt, [kd, kt, k] + [e.now() for e in (self.pe, d, act, pool)], mid,
                          512, 2, w3["w13"], w3["w2"])
        both = [self.work[:, n * 2048:(n + 1) * 2048].rearrange("p (t c) -> p t c", c=C) for n in range(2)]
        kc = self.collect(both, self.ys[2], [0, 1], ko + [d.now(), act.now(), self.pe.now()])
        k = d.fill(A(t1), 0.0)
        k = self.weighted(t1, both, [kc, k])
        k = d.tt(A(t1), A(t1), grow(r3["ls2"], NT), ALU.mult, w=[k])
        k = d.tt(A(s), A(s), A(t1), ALU.add, w=[k])
        k = d.tt(A(s), A(s), grow_in(self.wsum, C), ALU.mult, w=[k])
        return d.tt(A(s), A(s), A(self.xn), ALU.add, w=[k])

    def layer3_ffn(self):
        d, act, pool, r3, w3 = self.dve, self.act, self.pool, self.r3, self.w3
        t1 = self.t1
        A = lambda t: t[:, :, :]
        ms, rs = self.v[0][:, :], self.v[1][:, :]
        start = [d.now(), self.pe.now(), pool.now()]
        for t in range(NT):
            k = act.act(t1[:, t, :], self.xn[:, t, :], ACT.Square, w=start, acc=ms[:, t:t + 1])
        k = d.ts(ms, ms, 1.0 / C, EPS, ALU.mult, ALU.add, w=[k])
        k = self.rsqrt(rs, ms, [k])
        for t in range(NT):
            kk = d.stt(t1[:, t, :], self.xn[:, t, :], rs[:, t:t + 1], r3["norm"], ALU.mult, ALU.mult, w=[k])
        kT = self.transposed(t1, lambda q: self.tT[:, q * 512:(q + 1) * 512], [kk], w_dst=[self.pe.now()])
        lg = self.k8[0][:, :, :]
        k = self.logits(lambda t: self.tT[:, t * 128:(t + 1) * 128], w3["gate_w"], r3["gate_b"], lg, kT)
        oh, m, k = self.top2(lg, [k])
        k = self.pair_softmax(m, self.gates[:, 0, :], self.gates[:, 1, :], [k])
        k, kt = self.slots(oh, [k])
        kd = self.dispatch(t1, self.xs[3], 2, [self.k_clear[3]], [k])
        b1 = r3["mlp1_b"]
        ALPHA = 1.702

        def mid(net, u, ps, ex, k, lp):
            d.wait([k, lp.prev(f"g{u}")])
            k = d.put(lambda: d.eng.tensor_tensor(net.hm[u], ps, b1[:, bass.ds(ex * 512, 512)], ALU.add))
            k1 = d.ts(net.hm[u][:, 0:256], net.hm[u][:, 0:256], 7.0, op0=ALU.min, w=[k])
            k2 = d.ts(net.hm[u][:, 256:512], net.hm[u][:, 256:512], 7.0, -7.0, ALU.min, ALU.max, w=[k])
            k1 = act.act(net.ha[u][:, 256:512], net.hm[u][:, 0:256], ACT.Silu, scale=ALPHA, w=[k1, lp.prev(f"g{u}")])
            return lp.mark(f"g{u}", d.stt(net.ha[u][:, 0:256], net.hm[u][:, 256:512], 1.0, net.ha[u][:, 256:512],
                                          ALU.add, ALU.mult, w=[k1, k2, lp.prev(f"trm{u}")]))

        ko = self.experts(self.xs[3], self.ys[3], 40, kt, [kd, kt, k] + [e.now() for e in (self.pe, d, act, pool)], mid,
                          512, 2, w3["mlp1"], w3["mlp2"], b1, r3["mlp2_b"], yscale=1.0 / ALPHA)
        both = [self.work[:, n * 2048:(n + 1) * 2048].rearrange("p (t c) -> p t c", c=C) for n in range(2)]
        kc = self.collect(both, self.ys[3], [0, 1], ko + [d.now(), act.now(), self.pe.now()])
        k = d.cp(A(self.g), A(self.xn))
        return self.weighted(self.g, both, [kc, k])

    def layer3(self):
        k = self.dve.now()
        self.normed(lambda t: [k])
        self.layer3_gates()
        k = self.layer3_attention()
        ks = self.layer3_mixture(k)
        k = self.layer3_ffn()
        return self.gated(self.s, [k, ks])


def build(nc, ins, out, upto=4):
    n = Net(nc, ins)
    n.start()
    n.layer0()
    if upto > 1:
        n.layer1()
    n.load_layer3()
    if upto > 2:
        n.layer2()
    if upto > 3:
        n.layer3()
    src = n.x
    k = n.sp.dma(out.rearrange("(t p) c -> p t c", p=P), src[:, :, :], n.ch_out_x, [n.dve.now()])
    n.sp.wait([k])
    for e in n.p.engines[:4]:
        n.sp.wait([e.now()])
    return n


def constants():
    f = np.float32
    i = np.arange(P)
    t = {"ident": np.eye(P), "ones": np.ones((P, P)), "before": (i[:, None] < i[None, :]),
         "swap": (i[:, None] == (i[None, :] + 64) % P)}
    channel = np.where(i < 64, 2 * i, 2 * (i - 64) + 1)
    t["heads"] = (channel[:, None] // 16 == np.arange(8)[None, :]) / f(NS)
    t["kv_mask"] = (i[:, None] // 16 == i[None, :] // 16) / np.sqrt(f(NS))
    n = np.arange(NS, dtype=f)
    theta = f(1.0) / f(10000.0) ** (np.arange(64, dtype=f) / f(64))
    ang = (n[:, None] * theta).T
    t["rope_cos"] = np.concatenate([np.cos(ang)] * 2)
    t["rope_sin"] = np.concatenate([-np.sin(ang), np.sin(ang)])
    rot = np.eye(P)
    rot[2 * np.arange(64) + 1, 2 * np.arange(64)] = -1
    rot[2 * np.arange(64), 2 * np.arange(64) + 1] = 1
    t["rot2"] = rot
    inv = f(10000.0) ** (np.arange(0, 64, 2, dtype=f) / f(64))
    rad = n[:, None] / inv
    t["rope2"] = np.repeat(np.stack((np.sin(rad), np.cos(rad)), axis=-1).reshape(NS, -1), 2, axis=-1).T
    t["iota8"] = np.tile(np.arange(8), (P, 1))
    t["iota384"] = np.tile(np.arange(8) * 384, (P, 1))
    t["tile_start"] = np.tile(np.arange(40) * P, (P, 1))
    t["tile_third"] = np.tile(np.minimum(np.arange(40) // 3, 7), (P, 1))
    t["scan_mask"] = np.tile(i % NT != 0, (P, 1))
    t["one_row8"] = ((i % 32) == 8)[:, None]
    t["bits"] = np.tile(2.0 ** np.arange(29, -1, -1), (P, 1))
    return t


def packed(fields, values):
    return np.ascontiguousarray(np.concatenate([np.asarray(values[n], np.float32).reshape(-1, w) for n, w in fields], axis=1))


def lay_out(a):
    T = np.transpose
    even_first = np.r_[0:C:2, 1:C:2]
    o = {"x": a["L0_attn_x"].reshape(TOK, C), "consts": packed(CONSTS, constants())}
    g = lambda p: (lambda n: np.asarray(a[p + n]))
    A, B = g("L0_attn_"), g("L0_ffn_")
    o["w0"] = packed(W0, {
        "q": A("qk_w")[:, :C][:, even_first], "k": A("qk_w")[:, C:][:, even_first],
        "lepe": T(A("lepe_w"), (1, 0, 2)).reshape(C, 384), "qkv": B("in_proj_w").T, "out": B("out_w").T,
        "router": B("router_w").T, "q_b": A("qk_b")[:C][even_first][:, None], "k_b": A("qk_b")[C:][even_first][:, None],
        "w1": T(B("w1"), (2, 0, 1)).reshape(C, 1024), "w2": T(B("w2"), (2, 0, 1)).reshape(C, 1024)})
    o["r0"] = packed(R0, {"lepe_b": A("lepe_b"), "qkv_b": B("in_proj_b"), "out_b": B("out_b"), "ln1_g": B("ln1_g"),
                          "ln1_b": B("ln1_b"), "ln2_g": B("ln2_g"), "ln2_b": B("ln2_b"), "router_b": B("router_b"),
                          "b1": B("b1"), "b2": B("b2")})
    A, B = g("L1_attn_"), g("L1_ffn_")
    o["w1"] = packed(W1, {
        "hidden": A("W_hidden"), "qk": A("W_qk"), "out": T(A("W_out").reshape(2, C, C), (1, 0, 2)).reshape(C, 256),
        "router": B("Wr"), "ln_g": A("ln_scale")[:, None], "ln_b": A("ln_bias")[:, None], "qk_b": A("b_qk")[:, None],
        "osw": A("os_weight").T, "osb": A("os_bias").T, "w1": T(B("W1"), (1, 0, 2)).reshape(C, 4096),
        "w2": T(B("W2").reshape(E, 4, C, C), (2, 0, 1, 3)).reshape(C, 4096)})
    o["r1"] = packed(R1, {"hidden_b": A("b_hidden"), "out_b": A("b_out"), "router_b": B("br"), "gamma": B("gamma"),
                          "beta": B("beta"), "b1": B("b1"), "b2": B("b2")})
    A, B = g("L2_attn_"), g("L2_ffn_")
    o["w2"] = packed(W2, {
        "wq": A("Wq"), "wk": A("Wk"), "wv": A("Wv").T, "wf": B("wf").T, "wi": B("wi").T, "wc": B("wc").T,
        "uf": B("uf").T, "ui": B("ui").T, "uc": B("uc").T, "wo": B("wo").T, "uo": B("uo").T,
        "bq": A("bq")[:, None], "bk": A("bk")[:, None], "bf": B("bf")[:, None], "bi": B("bi")[:, None],
        "bc": B("bc")[:, None], "c0": B("in_c")[:, None]})
    o["r2"] = packed(R2, {"bv": A("bv"), "bo": B("bo")})
    A, B = g("L3_attn_"), g("L3_ffn_")

    def heads(w):
        z = np.zeros((C, 16, 32), np.float32)
        z[:, :, 0:8] = w.reshape(C, 16, 8)
        return z.reshape(C, 512)

    qkv = A("Wqkv")
    w13 = np.stack([T(A("W1"), (1, 0, 2)), T(A("W3"), (1, 0, 2))], axis=2).reshape(C, 4096)
    halves = np.r_[0:512:2, 1:512:2]
    o["w3"] = packed(W3, {
        "q": heads(qkv[:, 0:C]), "k": heads(qkv[:, C:2 * C]), "v": qkv[:, 2 * C:], "gate": A("Wgate"),
        "ssm": A("Win_ssm"), "ssm_out": A("Wout_ssm"), "attn_out": A("Wout"), "halt": A("Wr"), "router": A("Wg"),
        "gate_w": B("gate_w"), "ln_g": A("ln1_g")[:, None], "ln_b": A("ln1_b")[:, None],
        "conv_w": A("conv_w").reshape(C, 4), "conv_b": A("conv_b")[:, None], "w13": w13,
        "w2": T(A("W2").reshape(E, 2, C, C), (2, 0, 1, 3)).reshape(C, 2048),
        "mlp1": T(B("mlp1_w")[:, :, halves], (1, 0, 2)).reshape(C, 4096),
        "mlp2": T(B("mlp2_w").reshape(E, 2, C, C), (2, 0, 1, 3)).reshape(C, 2048)})
    o["r3"] = packed(R3, {"ln2_g": A("ln2_g"), "ln2_b": A("ln2_b"), "ls1": A("ls1"), "ls2": A("ls2"),
                          "halt_b": A("br"), "step_b": A("step_bias"), "norm": B("norm_scale"), "gate_b": B("gate_b"),
                          "mlp1_b": B("mlp1_b")[:, halves], "mlp2_b": B("mlp2_b")})
    return o


def kernel(**inputs):
    import concourse.bacc as bacc
    from concourse.bass_utils import run_bass_kernel_spmd

    nc = bacc.Bacc("TRN2", target_bir_lowering=False, num_devices=1)
    arrays = {f"in_{k}": np.ascontiguousarray(v) for k, v in lay_out({k: np.asarray(v) for k, v in inputs.items()}).items()}
    ins = {k[3:]: nc.dram_tensor(k, v.shape, F32, kind="ExternalInput").ap() for k, v in arrays.items()}
    out = nc.dram_tensor("out", (TOK, C), F32, kind="ExternalOutput").ap()
    build(nc, ins, out)
    r = run_bass_kernel_spmd(nc, [arrays], core_ids=[0])
    return r.results[0]["out"].reshape(NB, NS, C)
```

```python
import numpy as np
import concourse.bass as bass
from concourse import mybir
from concourse.alu_op_type import AluOpType as ALU

F32 = mybir.dt.float32
BF16 = mybir.dt.bfloat16
I32 = mybir.dt.int32
U32 = mybir.dt.uint32
ACT = mybir.ActivationFunctionType
AX = mybir.AxisListType.X

P = 128
C = 128
NB, NS = 8, 256
NT = NB * NS // P
TOK = NB * NS
E = 8
EPS = 1e-5
LEAD = 4
TILES = 52
PAD = 1000


class Token:

    def __init__(self, src, off, loop, back=0):
        self.src, self.off, self.loop, self.back = src, off, loop, back


class Loop:

    def __init__(self, count):
        self.count, self.i, self.base, self.per, self.marks = count, 0, {}, {}, {}

    def mark(self, name, tok):
        self.marks[name] = tok
        return tok

    def prev(self, name, back=1):
        t = self.marks.get(name)
        return None if t is None else Token(t.src, t.off, self, back)


class Source:

    def __init__(self, prog, name, step):
        self.prog, self.step, self.n, self.pad = prog, step, 0, PAD
        self.sem = prog.nc.alloc_semaphore(name)
        prog.sources.append(self)

    def took(self):
        self.n += self.step
        lp = self.prog.loop
        return Token(self, self.n if lp is None else self.n - lp.base.get(self, 0), lp)

    def value(self, t):
        lp = t.loop
        if lp is None:
            return self.pad + t.off
        k = lp.per.get(self, 0)
        if lp is self.prog.loop:
            return lp.i * k + (self.pad + lp.base.get(self, 0) + t.off - k * t.back)
        return self.pad + lp.base.get(self, 0) + (lp.count - 1) * k + t.off


class Engine(Source):
    def __init__(self, prog, name, eng):
        super().__init__(prog, "done_" + name, 1)
        self.eng = eng
        self.seen = {}

    def wait(self, toks):
        for t in toks:
            if t is None or self.prog.dry:
                continue
            key = (t.src, t.loop if t.loop is self.prog.loop else None)
            rank = (-t.back, t.off) if key[1] is not None else (0, t.src.value(t))
            if key in self.seen and self.seen[key] >= rank:
                continue
            self.seen[key] = rank
            self.eng.wait_ge(t.src.sem, t.src.value(t))

    def put(self, build, w=(), inc=True):
        self.wait(w)
        if not self.prog.dry:
            ins = build()
            if inc:
                ins.then_inc(self.sem, 1)
        return self.took() if inc else None

    def now(self):
        lp = self.prog.loop
        return Token(self, self.n if lp is None else self.n - lp.base.get(self, 0), lp)

    def tt(self, out, a, b, op, w=()):
        return self.put(lambda: self.eng.tensor_tensor(out, a, b, op), w)

    def ts(self, out, a, s1, s2=None, op0=ALU.mult, op1=None, w=()):
        if op1 is None:
            return self.put(lambda: self.eng.tensor_scalar(out, a, s1, None, op0), w)
        return self.put(lambda: self.eng.tensor_scalar(out, a, s1, s2, op0, op1), w)

    def stt(self, out, a, s, b, op0, op1, w=(), acc=None):
        return self.put(lambda: self.eng.scalar_tensor_tensor(out=out, in0=a, scalar=s, in1=b, op0=op0, op1=op1,
                                                              accum_out=acc), w)

    def cp(self, out, a, w=()):
        return self.put(lambda: self.eng.tensor_copy(out, a), w)

    def red(self, out, a, op, w=()):
        return self.put(lambda: self.eng.tensor_reduce(out, a, AX, op), w)

    def rcp(self, out, a, w=()):
        return self.put(lambda: self.eng.reciprocal(out, a), w)

    def fill(self, out, val, w=()):
        return self.put(lambda: self.eng.memset(out, val), w)

    def act(self, out, a, func, w=(), bias=0.0, scale=1.0, acc=None):
        return self.put(lambda: self.eng.activation(out, a, func, bias=bias, scale=scale, accum_out=acc), w)

    def mm(self, out, lhsT, rhs, first=True, last=True, w=(), inc=None, shared=False):
        inc = last if inc is None else inc
        return self.put(lambda: self.eng.matmul(out, lhsT, rhs, start=first, stop=last, skip_group_check=shared), w, inc)

    def tr(self, out, a, ident, w=(), inc=True):
        return self.put(lambda: self.eng.transpose(out, a, ident), w, inc)

    def dma(self, out, a, ch, w=()):
        self.wait(w)
        if not self.prog.dry:
            self.eng.dma_start(out, a).then_inc(ch.sem, 16)
        return ch.took()

    def scatter_rows(self, table, idx, rows, ch, w=()):
        self.wait(w)
        if not self.prog.dry:
            self.eng.indirect_dma_start(table, bass.IndirectOffsetOnAxis(ap=idx, axis=0), rows, None).then_inc(ch.sem, 16)
        return ch.took()

    def gather_rows(self, rows, table, idx, ch, w=()):
        self.wait(w)
        if not self.prog.dry:
            self.eng.indirect_dma_start(rows, None, table, bass.IndirectOffsetOnAxis(ap=idx, axis=0)).then_inc(ch.sem, 16)
        return ch.took()


class Program:

    def __init__(self, nc):
        self.nc, self.sources, self.loop, self.dry = nc, [], None, False
        self.pe = Engine(self, "pe", nc.tensor)
        self.dve = Engine(self, "dve", nc.vector)
        self.act = Engine(self, "act", nc.scalar)
        self.pool = Engine(self, "pool", nc.gpsimd)
        self.sp = Engine(self, "sp", nc.sync)
        self.engines = [self.pe, self.dve, self.act, self.pool, self.sp]
        for e in self.engines:
            e.eng.sem_inc(e.sem, PAD)
        self.n_sb = 0

    def channel(self, name, issuer):
        ch = Source(self, name, 16)
        if issuer is self.pool:
            ch.pad = 0
        else:
            issuer.eng.sem_inc(ch.sem, PAD)
        return ch

    def run_loop(self, count, body):
        lp = Loop(count)
        lp.base = {s: s.n for s in self.sources}
        kept = {s: s.n for s in self.sources}
        self.loop, self.dry = lp, True
        body(0, lp)
        lp.per = {s: s.n - kept[s] for s in self.sources}
        for s in self.sources:
            s.n = kept[s]
        self.dry = False
        for e in self.engines:
            e.seen = {}
        with self.nc.Fori(0, count) as i:
            lp.i = i
            body(i, lp)
        lp.i = 0
        self.loop = None
        for s in self.sources:
            s.n = kept[s] + count * lp.per[s]
        for e in self.engines:
            e.seen = {}

    def sbuf(self, name, shape, dt=F32):
        return self.nc.alloc_sbuf_tensor(name, shape, dt)


class Steps:

    def __init__(self, prog):
        self.prog, self.last = prog, {}

    def did(self, name, k):
        self.last[name] = k
        if self.prog.loop is not None:
            self.prog.loop.mark(name, k)
        return k

    def since(self, name):
        lp, t = self.prog.loop, self.last.get(name)
        return t if lp is None or (t is not None and t.loop is lp) else lp.prev(name)


class Banks:

    def __init__(self, prog, nc):
        self.prog = prog
        self.ps = nc.alloc_psum_tensor("banks", [P, 8 * 512], F32)
        self.k, self.n, self.free, self.local = 0, 8, [[] for _ in range(8)], set()

    def take(self, width=512):
        i = self.k % self.n
        self.k += 1
        lp = self.prog.loop
        w = self.free[i]
        if lp is not None and i not in self.local:
            w = [lp.prev(f"bank{i}.{n}") for n in range(2)]
        return i, self.ps[:, i * 512:i * 512 + width], w

    def only(self, n):
        self.k, self.n = 0, n

    def give(self, i, *toks):
        self.free[i] = list(toks)
        lp = self.prog.loop
        if lp is not None:
            self.local.add(i)
            for n, t in enumerate(toks):
                lp.mark(f"bank{i}.{n}", t)

    def run_loop(self, count, body):
        self.prog.pe.wait([t for f in self.free for t in f])

        def whole(i, lp):
            self.k, self.local = 0, set()
            self.free = [[] for _ in range(8)]
            body(i, lp)

        self.prog.run_loop(count, whole)
        self.k = 0


def grow(ap, n):
    return ap.unsqueeze(1).broadcast_to((ap.shape[0], n, ap.shape[1]))


def grow_in(ap, n):
    return ap.unsqueeze(2).broadcast_to((ap.shape[0], ap.shape[1], n))


class Pack:

    def __init__(self, fields):
        self.at, n = {}, 0
        for name, width in fields:
            self.at[name] = (n, n + width)
            n += width
        self.width = n

    def on(self, tensor, start=0):
        self.tensor, self.start = tensor, start
        return self

    def __getitem__(self, name):
        a, b = self.at[name]
        return self.tensor[:, self.start + a:self.start + b]


CONSTS = [("ident", 128), ("ones", 128), ("before", 128), ("swap", 128), ("heads", 8), ("kv_mask", 128),
          ("rope_cos", 256), ("rope_sin", 256), ("rot2", 128), ("rope2", 256), ("iota8", 8), ("iota384", 8),
          ("tile_start", 52), ("tile_third", 52), ("octal", 4), ("scan_mask", 128), ("bits", 30)]
W0 = [("q", 128), ("k", 128), ("lepe", 384), ("qkv", 384), ("out", 128), ("router", 8), ("q_b", 1), ("k_b", 1),
      ("w1", 1024), ("w2", 1024)]
R0 = [("lepe_b", 128), ("qkv_b", 384), ("out_b", 128), ("ln1_g", 128), ("ln1_b", 128), ("ln2_g", 128),
      ("ln2_b", 128), ("router_b", 8), ("b1", 1024), ("b2", 1024)]
W1 = [("hidden", 512), ("qk", 128), ("out", 256), ("router", 8), ("ln_g", 1), ("ln_b", 1), ("qk_b", 1),
      ("osw", 2), ("osb", 2), ("w1", 4096), ("w2", 4096)]
R1 = [("hidden_b", 512), ("out_b", 128), ("router_b", 8), ("gamma", 128), ("beta", 128), ("b1", 4096), ("b2", 1024)]
W2 = [("wq", 128), ("wk", 128), ("wv", 128), ("wf", 128), ("wi", 128), ("wc", 128), ("uf", 128), ("ui", 128),
      ("uc", 128), ("wo", 128), ("uo", 128), ("bq", 1), ("bk", 1), ("bf", 1), ("bi", 1), ("bc", 1), ("c0", 1)]
R2 = [("bv", 128), ("bo", 128)]
W3 = [("q", 128), ("k", 128), ("v", 128), ("gate", 128), ("ssm", 256), ("ssm_out", 128), ("attn_out", 128),
      ("halt", 2), ("router", 8), ("gate_w", 8), ("ln_g", 1), ("ln_b", 1), ("conv_w", 4), ("conv_b", 1),
      ("w13", 4096), ("w2", 2048), ("mlp1", 4096), ("mlp2", 2048)]
R3 = [("ln2_g", 128), ("ln2_b", 128), ("ls1", 128), ("ls2", 128), ("halt_b", 2), ("step_b", 3), ("norm", 128),
      ("gate_b", 8), ("mlp1_b", 4096), ("mlp2_b", 1024)]


class Net:

    def __init__(self, nc, ins):
        self.nc = nc
        p = self.p = Program(nc)
        self.pe, self.dve, self.act, self.pool, self.sp = p.engines
        self.banks = Banks(p, nc)
        self.ins = ins
        sb = p.sbuf
        self.x = sb("x", [P, NT, C])
        self.xn = sb("xn", [P, NT, C])
        self.xT = sb("xT", [P, NB, NS + 2])
        self.s = sb("s", [P, NT, C])
        self.g = sb("g", [P, NT, C])
        self.t1 = sb("t1", [P, NT, C])
        self.t2 = self.g
        self.tT = sb("tT", [P, TOK])
        self.work = sb("work", [P, 10496])
        self.arena = self.work[:, 0:4352]
        self.qkv = self.work[:, 4352:10496].rearrange("p (t c) -> p t c", c=3 * C)
        self.c = Pack(CONSTS).on(sb("consts", [P, Pack(CONSTS).width]))
        w0, r0, w1, r1, w2, r2, w3, r3 = (Pack(f) for f in (W0, R0, W1, R1, W2, R2, W3, R3))
        room = max(w0.width + r0.width + w1.width + r1.width, w3.width + r3.width)
        wts = sb("weights", [P, room])
        self.w0, self.r0 = w0.on(wts, 0), r0.on(wts, w0.width)
        a = w0.width + r0.width
        self.w1, self.r1 = w1.on(wts, a), r1.on(wts, a + w1.width)
        self.w3, self.r3 = w3.on(wts, 0), r3.on(wts, w3.width)
        w2s = sb("weights2", [P, w2.width + r2.width])
        self.w2, self.r2 = w2.on(w2s, 0), r2.on(w2s, w2.width)
        self.stats = sb("stats", [P, NT, 6])
        self.v = [sb(f"small{i}", [P, NT]) for i in range(13)]
        self.k8 = [sb(f"byexpert{i}", [P, NT, E]) for i in range(8)]
        self.e8 = [sb(f"experts{i}", [P, E]) for i in range(6)]
        self.gates = sb("gates", [P, 2, NT])
        self.scrap = sb("scrap", [P, 1])
        self.idx = sb("idx", [P, 4, NT], I32)
        self.tile_f = sb("tile_f", [1, 52, E])
        self.tile_n = sb("tile_n", [1, 52])
        self.eight = sb("eight", [1, TILES // 4 - 1], I32)
        self.ei = sb("ei", [P, E], I32)
        self.vi = sb("vi", [P, NT], I32)
        U = self.R = 4
        at = [0]

        def part(n):
            at[0] += n
            return self.work[:, at[0] - n:at[0]]

        self.hs = [part(C) for _ in range(U)]
        self.hT = [part(C) for _ in range(U)]
        self.hm = [part(512) for _ in range(U)]
        self.ha = [part(512) for _ in range(U)]
        self.aT = [part(512) for _ in range(U)]
        self.y = [part(C) for _ in range(U)]
        self.ch_in = [p.channel(f"ch_in{u}", self.act) for u in range(U)]
        self.ch_out = [p.channel(f"ch_out{u}", self.sp) for u in range(U)]
        self.ch_row = p.channel("ch_row", self.pool)
        self.ch_out_x = p.channel("ch_out_x", self.sp)

    def load(self, eng, pack, name, w=(), rows=False):
        ch = self.p.channel("ch_" + name, eng)
        dst = pack.tensor[:, pack.start:pack.start + pack.width]
        src = self.ins[name]
        if rows:
            src = src.broadcast_to((P, pack.width))
        return eng.dma(dst, src, ch, w)

    def rsqrt(self, out, v, w):
        d, t = self.dve, self.v[10]
        k = d.ts(self.vi[:, :], v.bitcast(I32), 1, op0=ALU.logical_shift_right, w=w)
        k = d.ts(out.bitcast(I32), self.vi[:, :], -1.0, float(0x5F3759DF), ALU.mult, ALU.add, w=[k])
        for _ in range(3):
            k = d.tt(t[:, :], out, out, ALU.mult, w=[k])
            k = d.stt(t[:, :], t[:, :], -0.5, v, ALU.mult, ALU.mult, w=[k])
            k = d.stt(out, t[:, :], 1.5, out, ALU.add, ALU.mult, w=[k])
        return k

    def layernorm(self, src, dst, w, gain=None, bias=None):
        d, st = self.dve, self.stats
        diff, both, q, var, rstd, nmr = (self.v[i][:, :] for i in range(6))
        for t in range(NT):
            k = d.put(lambda: d.eng.bn_stats(st[:, t, :], src[:, t, :]), w(t))
        k1 = d.tt(diff, st[:, :, 1], st[:, :, 4], ALU.subtract, w=[k])
        k2 = d.tt(both, st[:, :, 1], st[:, :, 4], ALU.add, w=[k])
        k3 = d.tt(q, st[:, :, 2], st[:, :, 5], ALU.add, w=[k])
        k4 = d.tt(diff, diff, diff, ALU.mult, w=[k1])
        k5 = d.ts(q, q, 1.0 / C, EPS, ALU.mult, ALU.add, w=[k3])
        k6 = d.stt(var, diff, 0.25, q, ALU.mult, ALU.add, w=[k4, k5])
        k7 = self.rsqrt(rstd, var, [k6])
        k8 = d.stt(nmr, both, -0.5, rstd, ALU.mult, ALU.mult, w=[k7])
        for t in range(NT):
            k = d.ts(dst[:, t, :], src[:, t, :], rstd[:, t:t + 1], nmr[:, t:t + 1], ALU.mult, ALU.add, w=[k8])
        if gain is not None:
            k = d.tt(dst[:, :, :], dst[:, :, :], grow(gain, NT), ALU.mult, w=[k])
            k = d.tt(dst[:, :, :], dst[:, :, :], grow(bias, NT), ALU.add, w=[k])
        return k

    def transposed(self, src, dst4, w, gain=None, bias=None, w_dst=()):
        out = []
        for q in range(4):
            i, ps, wb = self.banks.take()
            for r in range(4):
                k = self.pe.tr(ps[:, r * 128:(r + 1) * 128], src[:, 4 * q + r, :], self.c["ident"],
                               w=list(w) + wb, inc=(r == 3))
            d = dst4(q)
            a = ps if len(d.shape) == 2 else ps.rearrange("p (b n) -> p b n", n=NS)
            if gain is not None:
                k = self.act.act(d, a, ACT.Identity, bias=bias, scale=gain, w=[k] + list(w_dst))
            else:
                eng = self.act if q % 2 else self.dve
                k = eng.act(d, a, ACT.Copy, w=[k] + list(w_dst)) if eng is self.act else eng.cp(d, a, w=[k] + list(w_dst))
            self.banks.give(i, k)
            out.append(k)
        return out

    def xT_tile(self, t):
        return self.xT[:, t // 2, 1 + 128 * (t % 2):129 + 128 * (t % 2)]

    def logits(self, tileT, weight, bias, out, w):
        n = weight.shape[1]
        i, ps, wb = self.banks.take()
        for t in range(NT):
            k = self.pe.mm(ps[:, t * n:(t + 1) * n], tileT(t), weight, w=list(w) + wb, inc=(t == NT - 1))
        k = self.dve.tt(out, ps[:, 0:NT * n].rearrange("p (t n) -> p t n", n=n), grow(bias, NT), ALU.add, w=[k])
        self.banks.give(i, k)
        return k

    def preset(self, func):
        one = self.scrap[:, 0:1]
        return self.act.act(one, one, func, w=[self.act.now()])

    def top2(self, lg, w):
        d = self.dve
        io = grow(self.c["iota8"], NT)
        m = [self.v[6][:, :], self.v[7][:, :]]
        oh = [self.k8[1], self.k8[2]]
        u, low, l2 = self.k8[3][:, :, :], self.v[8][:, :], self.k8[4][:, :, :]
        cur, k = lg, None
        for n in range(2):
            k = d.red(m[n], cur, ALU.max, w=list(w) if k is None else [k])
            k = d.tt(u, cur, grow_in(m[n], E), ALU.is_equal, w=[k])
            k = d.stt(u, u, -8.0, io, ALU.mult, ALU.add, w=[k])
            k = d.red(low, u, ALU.min, w=[k])
            k = d.tt(oh[n][:, :, :], u, grow_in(low, E), ALU.is_equal, w=[k])
            if n == 0:
                k = d.stt(l2, oh[0][:, :, :], -3.0e38, lg, ALU.mult, ALU.add, w=[k])
                cur = l2
        return oh, m, k

    def prefix(self, a, out, incl, w):
        d = self.dve
        i, ps, wb = self.banks.take()
        flat = a[:, :, :].rearrange("p t e -> p (t e)")
        self.pe.mm(ps[:, 0:128], self.c["before"], flat, w=list(w) + wb, inc=False)
        k = self.pe.mm(ps[:, 128:256], self.c["ones"], flat)
        tot = self.k8[5][:, :, :].rearrange("p t e -> p (t e)")
        tot3 = tot.rearrange("p (e t) -> p e t", t=NT)
        k = d.cp(tot3, ps[:, 128:256].rearrange("p (t e) -> p e t", e=E), w=[k])
        k = d.put(lambda: d.eng.tensor_tensor_scan(incl, self.c["scan_mask"], tot, 0.0, ALU.mult, ALU.add), [k])
        k = d.tt(tot, incl, tot, ALU.subtract, w=[k])
        k = d.tt(out, ps[:, 0:128].rearrange("p (t e) -> p t e", e=E),
                 tot.rearrange("p (e t) -> p t e", t=NT), ALU.add, w=[k])
        self.banks.give(i, k)
        return k

    def place(self, oh, D, out, w):
        d = self.dve
        u = self.k8[3][:, :, :]
        k = d.tt(u, oh, D, ALU.mult, w=w)
        return d.red(out, u, ALU.add, w=[k])

    def slots(self, ohs, w):
        d = self.dve
        a, k = ohs[0], None
        if len(ohs) == 2:
            a = self.k8[4]
            k = d.tt(a[:, :, :], ohs[0][:, :, :], ohs[1][:, :, :], ALU.add, w=w)
        D, incl = self.k8[6], self.k8[7][:, :, :].rearrange("p t e -> p (t e)")
        k = self.prefix(a, D[:, :, :], incl, list(w) + [k])
        cnt = incl.rearrange("p (e t) -> p e t", t=NT)[:, :, NT - 1]
        rounded, end, base = (self.e8[i][:, :] for i in range(3))
        k = d.ts(self.ei[:, :], cnt, 127.0, op0=ALU.add, w=[k])
        k = d.ts(self.ei[:, :], self.ei[:, :], 7, 7, ALU.logical_shift_right, ALU.logical_shift_left, w=[k])
        k = d.cp(rounded, self.ei[:, :], w=[k])
        k = d.put(lambda: d.eng.tensor_tensor_scan(end, self.c["ones"][:, 0:E], rounded, 0.0, ALU.mult, ALU.add), [k])
        k = d.tt(base, end, rounded, ALU.subtract, w=[k])
        kd = d.tt(D[:, :, :], D[:, :, :], grow(base, NT), ALU.add, w=[k])
        tf = self.tile_f[:, :, :]
        k = d.tt(tf, end[0:1, :].unsqueeze(1).broadcast_to((1, TILES, E)),
                 self.c["tile_start"][0:1, :].unsqueeze(2).broadcast_to((1, TILES, E)), ALU.is_le, w=[k])
        k = d.red(self.tile_n[:, :], tf, ALU.add, w=[k])
        k = d.ts(self.tile_n[:, :], self.tile_n[:, :], float(E - 1), op0=ALU.min, w=[k])
        kt = self.by_eights(self.tile_n[:, :], [k])
        for n, oh in enumerate(ohs):
            k = self.place(oh[:, :, :], D[:, :, :], self.v[9][:, :], [kd, kt])
            k = d.ts(self.idx[:, n, :], self.v[9][:, :], float(LEAD * P), op0=ALU.add, w=[k])
        return k, kt

    def by_eights(self, experts, w):
        d = self.dve
        v = self.tile_f[:, :, 0].rearrange("o (g u) -> o g u", u=4)
        k = d.tt(v, experts.rearrange("o (g u) -> o g u", u=4),
                 self.c["octal"][0:1, :].unsqueeze(1).broadcast_to((1, TILES // 4, 4)), ALU.mult, w=w)
        total = self.tile_f[:, 0:TILES // 4, 1]
        k = d.red(total, v, ALU.add, w=[k])
        return d.stt(self.eight[:, :], total[:, 1:], 4096.0, total[:, 0:TILES // 4 - 1], ALU.mult, ALU.add, w=[k])

    def experts(self, xs, ys, ntile, w, mid, func, F, NF, wa, wb_, b1=None, b2=None, yscale=1.0, mid_end=None):
        pe, d, act, sp = self.pe, self.dve, self.act, self.sp
        R = self.R
        steps = self.steps = Steps(self.p)
        since, did = steps.since, steps.did
        pe.wait([t for f in self.banks.free for t in f])
        for e in self.p.engines:
            e.wait(w)

        def bank(i, n=512):
            return self.banks.ps[:, i * 512:i * 512 + n]

        def rows_in(n, u):
            did(f"in{u}", act.dma(self.hs[u], xs[bass.ds((n + LEAD) * P, P), :], self.ch_in[u], w=[since(f"tr{u}")]))

        def turn(u):
            ps = bank(u % 2, 128)
            k = did(f"tr{u}", pe.tr(ps, self.hs[u], self.c["ident"], w=[since(f"in{u}"), since(f"hT{(u - 2) % R}")]))
            did(f"hT{u}", act.act(self.hT[u], ps, ACT.Copy, w=[k, since(f"m1{u}")]))

        def product1(u, ex_pe, ex_dve):
            ps = bank(2 + u, F)
            k = did(f"m1{u}", pe.mm(ps, self.hT[u], wa[:, bass.ds(ex_pe * F, F)], w=[since(f"hT{u}"), since(f"aT{u}")]))
            did(f"mid{u}", mid(self, u, ps, ex_dve, k, lambda n: since(f"{n}{u}")))

        def end_mid(u):
            k = since(f"mid{u}")
            did(f"a{u}", k if mid_end is None else mid_end(self, u, bank(2 + u, F), k, lambda n: since(f"{n}{u}")))

        def turn_mid(u):
            ps = bank(2 + u, 128 * NF)
            for f in range(NF):
                k = pe.tr(ps[:, 128 * f:128 * f + 128], self.ha[u][:, f * 128:(f + 1) * 128], self.c["ident"],
                          w=[since(f"a{u}")], inc=(f == NF - 1))
            did(f"trm{u}", k)
            dst, w = self.aT[u][:, 0:128 * NF], [k, since(f"m2{u}")]
            on_act = NF == 2 or (NF == 4 and u % 2)
            did(f"aT{u}", act.act(dst, ps, ACT.Copy, w=w) if on_act else d.cp(dst, ps, w=w))

        def product2(n, u, ex_pe, ex_dve):
            ps = bank(6 + u % 2, 128)
            for f in range(NF):
                k = pe.mm(ps, self.aT[u][:, f * 128:(f + 1) * 128], wb_[:, bass.ds(ex_pe * (128 * NF) + 128 * f, 128)],
                          first=(f == 0), last=(f == NF - 1), w=[since(f"aT{u}"), since(f"y{(u - 2) % R}")])
            did(f"m2{u}", k)
            d.wait([k, since(f"out{u}")])
            if b2 is None:
                k = d.cp(self.y[u], ps)
            else:
                k = d.stt(self.y[u], ps, yscale, b2[:, bass.ds(ex_dve * C, C)], ALU.mult, ALU.add)
            did(f"y{u}", k)
            did(f"out{u}", sp.dma(ys[bass.ds(n * P, P), :], self.y[u], self.ch_out[u], w=[k]))

        def body(i, lp):
            steps.last.clear()
            ex = {}
            for eng in (pe, d) if b2 is not None else (pe,):
                v = 0 if self.p.dry else eng.eng.value_load(self.eight[0:1, bass.ds(i, 1)], min_val=0, max_val=8 ** 8 - 1)
                for u in range(-R, R):
                    ex[eng, u] = (v >> (3 * (u + R))) & 7
            for u in range(R):
                for (eng, tile), e in ex.items():
                    if tile in (u, u - R) and not self.p.dry:
                        eng.eng.compute_val(e)
                turn((u + 1) % R)
                rows_in(i * R + u + 1 + R, (u + 1) % R)
                end_mid((u - 2) % R)
                turn_mid((u - 3) % R)
                product2(i * R + u, u, ex[pe, u - 4], ex.get((d, u - 4)))
                product1(u, ex[pe, u], ex.get((d, u)))

        for u in range(R):
            rows_in(u, u)
        turn(0)
        rows_in(R, 0)
        self.preset(func)
        self.p.run_loop(ntile // R + 1, body)
        act.wait([Token(c, c.n, None) for c in self.ch_in])
        done = [self.dve.now(), self.preset(func)]
        self.banks.free = [list(done) for _ in range(8)]
        return [Token(c, c.n, None) for c in self.ch_out]

    def dispatch(self, rows, xs, n, filled, w, limit=None):
        for t in range(NT):
            for j in range(n):
                self.pool.wait(list(w) + list(filled))
                if limit is None:
                    k = self.pool.scatter_rows(xs[:, :], self.idx[:, j, t:t + 1], rows[:, t, :], self.ch_row)
                else:
                    self.pool.eng.indirect_dma_start(
                        xs[:, :], bass.IndirectOffsetOnAxis(ap=self.idx[:, j, t:t + 1], axis=0), rows[:, t, :], None,
                        bounds_check=limit, oob_is_err=False).then_inc(self.ch_row.sem, 16)
                    k = self.ch_row.took()
        return k

    def collect(self, outs, ys, idxs, w):
        for t in range(NT):
            for o, j in zip(outs, idxs):
                k = self.pool.gather_rows(o[:, t, :], ys[:, :], self.idx[:, j, t:t + 1], self.ch_row, w=w)
        return k

    def clear_rows(self, xs, ntile):
        ch = self.p.channel(f"ch_zero{self.p.n_sb}", self.sp)
        self.p.n_sb += 1
        return self.sp.dma(xs[0:ntile * P, :].rearrange("(t p) c -> p t c", p=P),
                           self.zero[:, :].unsqueeze(1).broadcast_to((P, ntile, C)), ch, [self.k_zero])

    def start(self):
        sp, d, pool = self.sp, self.dve, self.pool
        ch = self.p.channel("ch_x", sp)
        self.k_x = sp.dma(self.x[:, :, :], self.ins["x"].rearrange("(t p) c -> p t c", p=P), ch)
        self.k_c = self.load(sp, self.c, "consts")
        self.k_w0 = [self.load(sp, self.w0, "w0"), self.load(sp, self.r0, "r0", rows=True)]
        self.zero = self.p.sbuf("zero", [P, C])
        self.k_zero = pool.fill(self.zero[:, :], 0.0)
        pool.fill(self.scrap[:, :], 0.0)
        self.k_edge = pool.fill(self.xT[:, :, :], 0.0)
        dt = self.nc.dram_tensor
        self.xs = [dt(f"xs{n}", ((t + 3 * LEAD + 1) * P, C), F32, kind="Internal").ap() for n, t in enumerate((24, 24, 40, 40))]
        self.ys = [dt(f"ys{n}", ((t + LEAD) * P, C), F32, kind="Internal").ap() for n, t in enumerate((24, 24, 40, 40))]
        self.k_clear = [self.clear_rows(x, t + 3 * LEAD + 1) for x, t in zip(self.xs, (24, 24, 40, 40))]
        self.k_w1 = [self.load(sp, self.w1, "w1"), self.load(sp, self.r1, "r1", rows=True)]
        self.k_w2 = [self.load(sp, self.w2, "w2"), self.load(sp, self.r2, "r2", rows=True)]

    def normed(self, w, turned=True):
        self.dve.wait([self.k_x])
        k = self.layernorm(self.x, self.xn, w)
        self.k_xn = k
        if not turned:
            return k
        self.k_xT = self.transposed(self.xn, lambda q: self.xT[:, 2 * q:2 * q + 2, 1:1 + NS], [k, self.k_c],
                                    w_dst=[self.k_edge, self.pe.now()])
        return k

    def gated(self, s, w):
        k = self.act.act(self.g[:, :, :], self.g[:, :, :], ACT.Silu, w=w)
        k = self.dve.tt(self.g[:, :, :], self.g[:, :, :], s[:, :, :], ALU.mult, w=[k])
        return self.dve.tt(self.x[:, :, :], self.x[:, :, :], self.g[:, :, :], ALU.add, w=[k])

    def layer0_linear_attention(self):
        pe, d, act, pool, c, w0 = self.pe, self.dve, self.act, self.pool, self.c, self.w0
        ar = self.arena
        e, r = ar[:, 0:512], ar[:, 512:1024]
        ue = [ar[:, 1024:1536], ar[:, 1536:2048]]
        t1 = ar[:, 2048:2560]
        ro = [ar[:, 2560:3072], ar[:, 3072:3584]]
        kt = ar[:, 3584:4096].rearrange("p (r c) -> p r c", c=C)
        kvm, mz, zz = ar[:, 4096:4224], ar[:, 4224:4232], ar[:, 4232:4240]
        km = self.v[11]
        last = {}
        for j in range(4):
            X = self.xT[:, 2 * j:2 * j + 2, 1:1 + NS]
            kin = [self.k_xT[j]] + self.k_w0
            for n, (w, b) in enumerate((("q", "q_b"), ("k", "k_b"))):
                i, ps, wb = self.banks.take()
                k = pe.mm(ps, w0[w], X, w=kin + wb)
                ke = act.act(e, ps, ACT.Exp, bias=w0[b], w=[k, last.get("u")])
                kr = act.act(r, ps, ACT.Relu, bias=w0[b], w=[k, last.get("u")])
                self.banks.give(i, kr)
                for h in range(2):
                    sl = slice(h * NS, (h + 1) * NS)
                    k = d.stt(ue[n][:, sl], e[:, sl], 1.0, r[:, sl], ALU.min, ALU.add,
                              w=[ke, kr, last.get(("den", n)), last.get(("rot", n))], acc=km[:, h:h + 1] if n else None)
                last["u"] = ku = k
                last["u", n] = ku
                i, ps, wb = self.banks.take()
                k = last["rot", n] = pe.mm(ps, c["swap"], ue[n], w=[ku] + wb)
                two = lambda a: a.rearrange("p (b n) -> p b n", n=NS)
                k1 = pool.tt(two(t1), two(ue[n]), grow(c["rope_cos"], 2), ALU.mult, w=[ku, last.get("t1"), self.k_c])
                k2 = d.tt(two(ro[n]), two(ps), grow(c["rope_sin"], 2), ALU.mult, w=[k, last.get(("ro", n))])
                self.banks.give(i, k2)
                last["t1"] = k = d.tt(ro[n], ro[n], t1, ALU.add, w=[k1, k2])
                last["r", n] = k
            for h in range(2):
                i, ps, wb = self.banks.take()
                for q in range(2):
                    k = pe.tr(ps[:, q * 128:(q + 1) * 128], ro[1][:, (2 * h + q) * 128:(2 * h + q + 1) * 128],
                              c["ident"], w=[last["r", 1]] + wb)
                k = act.act(kt[:, 0:2, :], ps[:, 0:256].rearrange("p (r c) -> p r c", c=C), ACT.Copy,
                            w=[k, last.get("kv")])
                self.banks.give(i, k)
                i, ps, wb = self.banks.take()
                for q in range(2):
                    kk = pe.mm(ps[:, 0:128], kt[:, q, :], self.xn[:, 4 * j + 2 * h + q, :], first=(q == 0),
                               last=(q == 1), w=[k, self.k_xn] + wb)
                last["kv"] = kk
                k = d.tt(kvm, ps[:, 0:128], c["kv_mask"], ALU.mult, w=[kk, last.get("o")])
                self.banks.give(i, k)
                kz = d.ts(mz, c["heads"], km[:, h:h + 1], w=[last["u", 1], last.get("o")])
                for q in range(2):
                    t = 4 * j + 2 * h + q
                    sl = slice((2 * h + q) * 128, (2 * h + q + 1) * 128)
                    i, ps, wb = self.banks.take()
                    pe.mm(ps[:, 0:128], ro[0][:, sl], kvm, w=[k, last["r", 0]] + wb)
                    pe.mm(ps[:, 128:136], ue[0][:, sl], mz, w=[kz])
                    for m in range(3):
                        b = 2 * j + h
                        kk = pe.mm(ps[:, 256:384], self.xT[:, b, m + 128 * q:m + 128 * q + 128],
                                   w0["lepe"][:, m * 128:(m + 1) * 128], first=(m == 0), last=(m == 2))
                    last["o"] = last["den", 0] = last["ro", 0] = last["ro", 1] = last["den", 1] = kk
                    k1 = d.ts(zz, ps[:, 128:136], 1e-6, op0=ALU.add, w=[kk, self.dve.now()])
                    k1 = d.rcp(zz, zz, w=[k1])
                    st = self.s[:, t, :]
                    k1 = d.tt(st.rearrange("p (h e) -> p h e", e=16), ps[:, 0:128].rearrange("p (h e) -> p h e", e=16),
                              grow_in(zz, 16), ALU.mult, w=[k1])
                    k1 = d.tt(st, st, ps[:, 256:384], ALU.add, w=[k1])
                    self.banks.give(i, k1)
        return d.tt(self.s[:, :, :], self.s[:, :, :], grow(self.r0["lepe_b"], NT), ALU.add, w=[k1])

    def layer0_attention(self):
        pe, d, act, pool, c = self.pe, self.dve, self.act, self.pool, self.c
        qkv = self.qkv
        for t in range(NT):
            i, ps, wb = self.banks.take()
            k = pe.mm(ps[:, 0:384], self.xT_tile(t), self.w0["qkv"], w=self.k_w0 + self.k_xT + wb)
            k = d.tt(qkv[:, t, :], ps[:, 0:384], self.r0["qkv_b"], ALU.add, w=[k])
            self.banks.give(i, k)
        kq = k
        prod = self.arena[:, 0:1024]
        sc = self.arena[:, 1024:2048]
        mx, sm = self.arena[:, 2048:2176], self.arena[:, 2176:2304]
        prod2 = self.arena[:, 2304:3328]
        ctx = self.t2

        def rows(part, h):
            return qkv[:, :, :].rearrange("p (s h) c -> p h s c", h=2)[:, h, :, part * 128:(part + 1) * 128]

        for h in range(2):
            for t in range(8):
                q = qkv[:, 2 * t + h, 0:128]
                k1 = pool.tt(prod.rearrange("p (s c) -> p s c", c=C), rows(1, h), grow(q, 8), ALU.mult,
                             w=[kq, d.now()]) if t % 3 == 2 else \
                    d.tt(prod.rearrange("p (s c) -> p s c", c=C), rows(1, h), grow(q, 8), ALU.mult, w=[kq, d.now()])
                k = d.red(sc[:, t * 128:(t + 1) * 128], prod.rearrange("p (a x) -> p a x", x=8), ALU.add,
                          w=[k1, act.now(), d.now()])
            ths = sc.rearrange("p (t s h) -> p t h s", s=8, h=16)
            th = lambda a: a.rearrange("p (t h) -> p t h", h=16)
            k = d.red(th(mx), ths, ALU.max, w=[k])
            tsh = sc.rearrange("p (t s h) -> p t s h", s=8, h=16)
            bc = lambda a: th(a).unsqueeze(2).broadcast_to((P, 8, 8, 16))
            k = d.tt(tsh, tsh, bc(mx), ALU.subtract, w=[k])
            k = act.act(sc, sc, ACT.Exp, scale=float(np.float32(8.0) ** np.float32(-0.5)), w=[k])
            k = d.red(th(sm), ths, ALU.add, w=[k])
            k = d.rcp(sm, sm, w=[k])
            ks = d.tt(tsh, tsh, bc(sm), ALU.mult, w=[k])
            for t in range(8):
                pr = prod2.rearrange("p (h x s) -> p h x s", h=16, x=8)
                pt = sc[:, t * 128:(t + 1) * 128].rearrange("p (s h) -> p h s", h=16).unsqueeze(2).broadcast_to((P, 16, 8, 8))
                v = rows(2, h).rearrange("p s (h x) -> p h x s", h=16)
                k1 = d.tt(pr, pt, v, ALU.mult, w=[ks, d.now()])
                k = d.red(ctx[:, 2 * t + h, :], prod2.rearrange("p (c s) -> p c s", s=8), ALU.add, w=[k1])
        kT = self.transposed(ctx, lambda q: self.tT[:, q * 512:(q + 1) * 512], [k], w_dst=[pe.now()])
        for t in range(NT):
            i, ps, wb = self.banks.take()
            k = pe.mm(ps[:, 0:128], self.tT[:, t * 128:(t + 1) * 128], self.w0["out"], w=kT + wb)
            k = d.tt(self.t1[:, t, :], ps[:, 0:128], self.xn[:, t, :], ALU.add, w=[k])
            self.banks.give(i, k)
        return d.tt(self.t1[:, :, :], self.t1[:, :, :], grow(self.r0["out_b"], NT), ALU.add, w=[k])

    def mid_gelu(self, F, b1):
        def mid(net, u, ps, ex, k, since):
            d = net.dve
            d.wait([k, since("a")])
            k = d.put(lambda: d.eng.tensor_tensor(net.hm[u][:, 0:F], ps, b1[:, bass.ds(ex * F, F)], ALU.add))
            return net.act.act(net.ha[u][:, 0:F], net.hm[u][:, 0:F], ACT.Gelu, w=[k, since("trm")])
        return mid

    def layer0_mixture(self, k_in):
        d, r0, w0 = self.dve, self.r0, self.w0
        h = self.t1
        k = self.layernorm(self.t1, h, lambda t: [k_in], r0["ln1_g"], r0["ln1_b"])
        kT = self.transposed(h, lambda q: self.tT[:, q * 512:(q + 1) * 512], [k], w_dst=[self.pe.now()])
        lg = self.k8[0][:, :, :]
        k = self.logits(lambda t: self.tT[:, t * 128:(t + 1) * 128], w0["router"], r0["router_b"], lg, kT)
        oh, m, k = self.top2(lg, [k])
        i1, i2 = self.v[6][:, :], self.v[7][:, :]
        io = grow(self.c["iota8"], NT)
        k = self.place(oh[0][:, :, :], io, i1, [k])
        k = self.place(oh[1][:, :, :], io, i2, [k])
        k = d.tt(i1, i1, i2, ALU.max, w=[k])
        k = d.tt(oh[0][:, :, :], io, grow_in(i1, E), ALU.is_equal, w=[k])
        k, kt = self.slots([oh[0]], [k])
        kd = self.dispatch(h, self.xs[0], 1, [self.k_clear[0]], [k])
        ko = self.experts(self.xs[0], self.ys[0], 24, [kd, kt], self.mid_gelu(C, r0["b1"]), ACT.Gelu, C, 1,
                          w0["w1"], w0["w2"], r0["b1"], r0["b2"])
        kc = self.collect([self.t2], self.ys[0], [0], ko + [d.now()])
        k = d.tt(self.t1[:, :, :], self.t1[:, :, :], self.t2[:, :, :], ALU.add, w=[kc])
        return self.layernorm(self.t1, self.g, lambda t: [k], r0["ln2_g"], r0["ln2_b"])

    def layer0(self):
        self.normed(lambda t: [self.k_x])
        ks = self.layer0_linear_attention()
        k = self.layer0_attention()
        k = self.layer0_mixture(k)
        return self.gated(self.s, [k, ks])

    def layer1_attention(self):
        pe, d, act, pool, w1, r1 = self.pe, self.dve, self.act, self.pool, self.w1, self.r1
        start = [e.now() for e in (pe, d, act, pool)]
        k = self.layernorm(self.xn, self.t1, lambda t: [self.k_xn])
        kT = self.transposed(self.t1, lambda q: self.tT[:, q * 512:(q + 1) * 512], [k] + self.k_w1,
                             gain=w1["ln_g"], bias=w1["ln_b"], w_dst=[pe.now()])
        wk = self.work
        for e in (d, act, pool):
            e.wait(start)
        hid = [wk[:, 0:1024].rearrange("p (r n) -> p r n", n=512), wk[:, 1024:2048].rearrange("p (r n) -> p r n", n=512)]
        qk, qT, kk_ = wk[:, 2048:2304], wk[:, 2304:2560], wk[:, 2560:2816]
        at = [wk[:, 2816:3328], wk[:, 3328:3840]]
        rl = wk[:, 3840:4352]
        og, ogT = wk[:, 4352:4864], wk[:, 4864:5376]
        last = {}
        for b in range(NB):
            hb = hid[b % 2]
            for r in range(2):
                t = 2 * b + r
                i, ps, wb = self.banks.take()
                k = pe.mm(ps, self.tT[:, t * 128:(t + 1) * 128], w1["hidden"], w=kT + wb)
                k = d.tt(hb[:, r, :], ps, r1["hidden_b"], ALU.add, w=[k, last.get(("av", b - 2)), last.get(("og", b - 2))])
                self.banks.give(i, k)
            kh = act.act(hb, hb, ACT.Silu, w=[k])
            i, ps, wb = self.banks.take()
            k = pe.mm(ps[:, 0:NS], w1["qk"], self.tT[:, b * NS:(b + 1) * NS], w=kT + wb)
            k = act.act(qk, ps[:, 0:NS], ACT.Silu, bias=w1["qk_b"], w=[k, last.get("qk")])
            self.banks.give(i, k)
            kq = d.ts(qT, qk, w1["osw"][:, 0:1], w1["osb"][:, 0:1], ALU.mult, ALU.add, w=[k, last.get("sim")])
            last["qk"] = kkk = d.ts(kk_, qk, w1["osw"][:, 1:2], w1["osb"][:, 1:2], ALU.mult, ALU.add, w=[k])
            a = at[b % 2]
            i, ps, wb = self.banks.take()
            for r in range(2):
                k = pe.mm(ps[:, r * NS:(r + 1) * NS], kk_[:, r * 128:(r + 1) * 128], qT, w=[kq, kkk] + wb)
            last["sim"] = k
            k = act.act(rl, ps, ACT.Relu, scale=1.0 / NS, w=[k, last.get("a")])
            self.banks.give(i, k)
            last["a"] = ka = pool.tt(a, rl, rl, ALU.mult, w=[k, last.get(("av", b - 2))])
            for r in range(2):
                i, ps, wb = self.banks.take()
                for j in range(2):
                    k = pe.mm(ps[:, 0:256], a[:, j * NS + r * 128:j * NS + r * 128 + 128], hb[:, j, 0:256],
                              first=(j == 0), last=(j == 1), w=[ka, kh] + wb)
                last["av", b] = k
                k = d.tt(og[:, r * 256:(r + 1) * 256], ps[:, 0:256], hb[:, r, 256:512], ALU.mult,
                         w=[k, last.get("ogtr")])
                self.banks.give(i, k)
            last["og", b] = k
            i, ps, wb = self.banks.take()
            for r in range(4):
                k = pe.tr(ps[:, r * 128:(r + 1) * 128], og[:, r * 128:(r + 1) * 128], self.c["ident"], w=[k] + wb if r == 0 else (),
                          inc=(r == 3))
            last["ogtr"] = k
            k = act.act(ogT, ps, ACT.Copy, w=[k, last.get("wout")])
            self.banks.give(i, k)
            i, ps, wb = self.banks.take()
            for r in range(2):
                for f in range(2):
                    kk = pe.mm(ps[:, r * 128:(r + 1) * 128], ogT[:, (2 * r + f) * 128:(2 * r + f + 1) * 128],
                               w1["out"][:, f * 128:(f + 1) * 128], first=(f == 0), last=(f == 1), w=[k] + wb)
            last["wout"] = kk
            k = d.tt(self.s[:, 2 * b:2 * b + 2, :], ps[:, 0:256].rearrange("p (r c) -> p r c", c=C),
                     grow(r1["out_b"], 2), ALU.add, w=[kk])
            self.banks.give(i, k)
        return k

    def pair_softmax(self, m, w1, w2, w):
        d, t = self.dve, self.v[9][:, :]
        k = d.tt(t, m[1], m[0], ALU.subtract, w=w)
        k = self.act.act(t, t, ACT.Exp, w=[k])
        k = d.ts(w1, t, 1.0, op0=ALU.add, w=[k])
        k = d.rcp(w1, w1, w=[k])
        return d.tt(w2, t, w1, ALU.mult, w=[k])

    def layer1_slots(self):
        d, pe, c = self.dve, self.pe, self.c
        CAP = (TOK * 5 + 4 * E - 1) // (4 * E)
        lg = self.k8[0][:, :, :]
        k = self.logits(self.xT_tile, self.w1["router"], self.r1["router_b"], lg, self.k_xT + self.k_w1)
        oh, m, k = self.top2(lg, [k])
        g = [self.gates[:, 0, :], self.gates[:, 1, :]]
        k = self.pair_softmax(m, g[0], g[1], [k])
        val, u = self.k8[0][:, :, :], self.k8[3][:, :, :]
        k1 = d.tt(val, oh[0][:, :, :], grow_in(g[0], E), ALU.mult, w=[k])
        k2 = d.tt(u, oh[1][:, :, :], grow_in(g[1], E), ALU.mult, w=[k])
        k = d.tt(val, val, u, ALU.add, w=[k1, k2])
        thr, cand, step = self.ei, self.p.sbuf("cand", [P, E], I32), self.p.sbuf("step", [P, E], I32)
        part = self.e8[0][:, :]
        bits_i = self.p.sbuf("bits_i", [P, 30], I32)
        k = d.cp(bits_i[:, :], c["bits"], w=[k])
        k = d.fill(thr[:, :], 0, w=[k])
        pe.wait([k])

        def body(i, lp):
            bit_i = bits_i[:, bass.ds(i, 1)]
            bit_f = self.bits_f[:, bass.ds(i, 1)]
            k = d.tt(cand[:, :], thr[:, :], bit_i.broadcast_to((P, E)), ALU.bitwise_or, w=[lp.prev("thr")])
            k = d.tt(u, val, grow(cand[:, :].bitcast(F32), NT), ALU.is_ge, w=[k])
            k = d.red(part, u.rearrange("p t e -> p e t"), ALU.add, w=[k, lp.prev("mm")])
            i0, ps, wb = self.banks.take()
            k = lp.mark("mm", pe.mm(ps[:, 0:E], c["ones"], part, w=[k] + wb))
            d.wait([k])
            k = d.ts(step[:, :], ps[:, 0:E], float(CAP), bit_f, ALU.is_ge, ALU.mult)
            self.banks.give(i0, k)
            lp.mark("thr", d.tt(thr[:, :], thr[:, :], step[:, :], ALU.bitwise_or, w=[k]))

        self.bits_f = c["bits"]
        self.banks.run_loop(30, body)
        k = d.now()
        over, tie, both = self.k8[4], self.p.sbuf("tie", [P, NT, E]), self.p.sbuf("chosen", [P, NT, E])
        tb = grow(thr[:, :].bitcast(F32), NT)
        k1 = d.tt(over[:, :, :], val, tb, ALU.is_gt, w=[k])
        k2 = d.tt(both[:, :, :], oh[0][:, :, :], oh[1][:, :, :], ALU.add, w=[k])
        k3 = d.tt(tie[:, :, :], val, tb, ALU.is_equal, w=[k])
        k3 = d.tt(tie[:, :, :], tie[:, :, :], both[:, :, :], ALU.mult, w=[k2, k3])
        part2 = self.e8[1][:, :]
        k1 = d.red(part, over[:, :, :].rearrange("p t e -> p e t"), ALU.add, w=[k1])
        i0, ps, wb = self.banks.take()
        k1 = pe.mm(ps[:, 0:E], c["ones"], part, w=[k1] + wb)
        k1 = d.ts(part2, ps[:, 0:E], -1.0, float(CAP), ALU.mult, ALU.add, w=[k1])
        self.banks.give(i0, k1)
        rank, incl = self.k8[6], self.k8[7][:, :, :].rearrange("p t e -> p (t e)")
        k = self.prefix(tie, rank[:, :, :], incl, [k3, k1])
        k = d.tt(u, rank[:, :, :], grow(part2, NT), ALU.is_lt, w=[k])
        k = d.tt(u, u, tie[:, :, :], ALU.mult, w=[k])
        k = d.tt(over[:, :, :], over[:, :, :], u, ALU.add, w=[k])
        k = self.prefix(over, rank[:, :, :], incl, [k])
        k = d.tt(rank[:, :, :], rank[:, :, :], grow(c["iota384"], NT), ALU.add, w=[k])
        took, slot, t = self.v[8][:, :], self.v[9][:, :], self.v[0][:, :]
        for n in range(2):
            k = self.place(oh[n][:, :, :], over[:, :, :], took, [k])
            k = self.place(oh[n][:, :, :], rank[:, :, :], slot, [k])
            k = d.tt(t, slot, took, ALU.mult, w=[k])
            k = d.ts(self.idx[:, 2 + n, :], t, float(LEAD * P), op0=ALU.add, w=[k])
            k = d.ts(slot, took, -65536.0, 65536.0, ALU.mult, ALU.add, w=[k])
            k = d.tt(t, t, slot, ALU.add, w=[k])
            k = d.ts(self.idx[:, n, :], t, float(LEAD * P), op0=ALU.add, w=[k])
            k = d.tt(g[n], g[n], took, ALU.mult, w=[k])
        return self.by_eights(c["tile_third"][0:1, :], [k])

    def weighted(self, out, ins, w):
        d = self.dve
        for t in range(NT):
            k = d.stt(out[:, t, :], ins[0][:, t, :], self.gates[:, 0, t:t + 1], out[:, t, :], ALU.mult, ALU.add, w=w)
        w = [k]
        for t in range(NT):
            k = d.stt(out[:, t, :], ins[1][:, t, :], self.gates[:, 1, t:t + 1], out[:, t, :], ALU.mult, ALU.add, w=w)
        return k

    def layer1_mixture(self, k_slots, k_free):
        d, r1 = self.dve, self.r1
        kd = self.dispatch(self.xn, self.xs[1], 2, [self.k_clear[1]], [k_slots], limit=(24 + LEAD) * P - 1)
        ko = self.experts(self.xs[1], self.ys[1], 24, [kd, k_slots] + k_free, self.mid_gelu(512, r1["b1"]), ACT.Gelu, 512, 4,
                          self.w1["w1"], self.w1["w2"], r1["b1"], r1["b2"])
        both = [self.work[:, n * 2048:(n + 1) * 2048].rearrange("p (t c) -> p t c", c=C) for n in range(2)]
        kc = self.collect(both, self.ys[1], [2, 3], ko + [d.now(), self.act.now(), self.pe.now()])
        k = d.cp(self.t1[:, :, :], self.xn[:, :, :])
        k = self.weighted(self.t1, both, [kc, k])
        return self.layernorm(self.t1, self.g, lambda t: [k], r1["gamma"], r1["beta"])

    def layer1(self):
        k = self.dve.now()
        self.normed(lambda t: [k])
        ks = self.layer1_attention()
        kr = self.layer1_slots()
        k = self.layer1_mixture(kr, [ks, self.pe.now(), self.act.now(), self.pool.now()])
        return self.gated(self.s, [k, ks])

    def load_layer3(self):
        w = [e.now() for e in (self.pe, self.dve, self.act, self.pool)] + self.k_w0 + self.k_w1
        self.k_w3 = [self.load(self.sp, self.w3, "w3", w=w), self.load(self.sp, self.r3, "r3", w=w, rows=True)]

    def layer2_attention(self):
        pe, d, act, pool, w2, r2, c = self.pe, self.dve, self.act, self.pool, self.w2, self.r2, self.c
        start = [e.now() for e in (pe, d, act, pool)]
        for e in (d, act, pool):
            e.wait(start)
        wk = self.work
        wq, wkk = wk[:, 0:128], wk[:, 128:256]
        bq = wk[:, 256:258]
        i, ps, wb = self.banks.take()
        pe.mm(ps[:, 0:128], w2["wq"], c["rot2"], w=self.k_w2 + wb, inc=False)
        pe.mm(ps[:, 128:256], w2["wk"], c["rot2"], inc=False)
        pe.mm(ps[:, 256:257], c["rot2"], w2["bq"], inc=False)
        k = pe.mm(ps[:, 257:258], c["rot2"], w2["bk"])
        k0 = d.cp(wk[:, 0:258], ps[:, 0:258], w=[k])
        self.banks.give(i, k0)
        last = {}
        for b in range(NB):
            X = self.xT[:, b, 1:1 + NS]
            o = 512 + (b % 2) * 2304
            qT, kT = wk[:, o:o + 256], wk[:, o + 256:o + 512]
            v = wk[:, o + 512:o + 768]
            pr, pT = wk[:, o + 768:o + 1280], wk[:, o + 1280:o + 1792]
            st = wk[:, o + 1792:o + 1800]
            old = [last.get(("pv", b - 2))]
            for dst, w, bb in ((qT, wq, 0), (kT, wkk, 1)):
                i, ps, wb = self.banks.take()
                k = pe.mm(ps[:, 0:NS], w, X, w=self.k_xT + [k0] + wb)
                k = d.stt(dst, ps[:, 0:NS], bq[:, bb:bb + 1], c["rope2"], ALU.add, ALU.mult, w=[k] + old)
                self.banks.give(i, k)
            kqk = k
            i, ps, wb = self.banks.take()
            for r in range(2):
                k = pe.mm(ps[:, r * 128:(r + 1) * 128], self.xT_tile(2 * b + r), w2["wv"], w=wb)
            kv = d.tt(v.rearrange("p (r c) -> p r c", c=C), ps[:, 0:256].rearrange("p (r c) -> p r c", c=C),
                      grow(r2["bv"], 2), ALU.add, w=[k] + old)
            self.banks.give(i, kv)
            i, ps, wb = self.banks.take()
            for r in range(2):
                k = pe.mm(ps[:, r * NS:(r + 1) * NS], qT[:, r * 128:(r + 1) * 128], kT, w=[kqk] + wb)
            k1 = d.red(st[:, 0:2], ps.rearrange("p (r n) -> p r n", n=NS), ALU.max, w=[k] + old)
            k1 = d.ts(st[:, 2:4], st[:, 0:2], -0.125, w=[k1])
            for r in range(2):
                k = act.act(pr[:, r * NS:(r + 1) * NS], ps[:, r * NS:(r + 1) * NS], ACT.Exp, bias=st[:, 2 + r:3 + r],
                            scale=0.125, acc=st[:, 4 + r:5 + r], w=[k1])
            self.banks.give(i, k)
            kr = d.rcp(st[:, 6:8], st[:, 4:6], w=[k])
            i, ps, wb = self.banks.take()
            for r in range(2):
                for q in range(2):
                    kk = pe.tr(ps[:, r * NS + q * 128:r * NS + (q + 1) * 128], pr[:, q * NS + r * 128:q * NS + (r + 1) * 128],
                               c["ident"], w=[k] + wb, inc=(r + q == 2))
            k = act.act(pT, ps, ACT.Copy, w=[kk] + old)
            self.banks.give(i, k)
            i, ps, wb = self.banks.take()
            for q in range(2):
                for r in range(2):
                    kk = pe.mm(ps[:, q * 128:(q + 1) * 128], pT[:, r * NS + q * 128:r * NS + (q + 1) * 128],
                               v[:, r * 128:(r + 1) * 128], first=(r == 0), last=(r == 1), w=[k, kv] + wb)
            last["pv", b] = kk
            for q in range(2):
                k = d.ts(self.s[:, 2 * b + q, :], ps[:, q * 128:(q + 1) * 128], st[:, 6 + q:7 + q], w=[kk, kr])
            self.banks.give(i, k)
            last["s"] = k
        return k

    def layer2_recurrence(self):
        pe, d, act, pool, w2, r2 = self.pe, self.dve, self.act, self.pool, self.w2, self.r2
        wk = self.work
        base = 512 + 2 * 2304
        cc = [wk[:, base:base + 256], wk[:, base + 256:base + 512]]
        f, ig, g = (wk[:, base + 512 + 256 * n:base + 768 + 256 * n] for n in range(3))
        k = pool.ts(cc[0], grow(w2["c0"], 1)[:, 0, :].broadcast_to((P, 256)), 1.0, w=self.k_w2)
        for t in range(8):
            X = self.xT[:, t, 1:1 + NS]
            c, cn = cc[t % 2], cc[(t + 1) % 2]
            ks = []
            for dst, w, u, b, fn in ((f, "wf", "uf", "bf", ACT.Sigmoid), (ig, "wi", "ui", "bi", ACT.Sigmoid), (g, "wc", "uc", "bc", ACT.Tanh)):
                i, ps, wb = self.banks.take()
                pe.mm(ps[:, 0:NS], w2[w], X, last=False, w=self.k_xT + wb)
                kk = pe.mm(ps[:, 0:NS], w2[u], c, first=False, w=[k])
                kk = act.act(dst, ps[:, 0:NS], fn, bias=w2[b], w=[kk, k])
                self.banks.give(i, kk)
                ks.append(kk)
            k1 = d.tt(cn, f, c, ALU.mult, w=[ks[0]])
            k2 = d.tt(g, ig, g, ALU.mult, w=[ks[2]])
            k = d.tt(cn, cn, g, ALU.add, w=[k1, k2])
        cT = cc[0]
        for t in range(NT):
            i, ps, wb = self.banks.take()
            pe.mm(ps[:, 0:128], self.xT_tile(t), w2["wo"], last=False, w=wb)
            kk = pe.mm(ps[:, 0:128], cT[:, 128 * (t % 2):128 * (t % 2) + 128], w2["uo"], first=False, w=[k])
            kk = d.tt(self.g[:, t, :], ps[:, 0:128], r2["bo"], ALU.add, w=[kk])
            self.banks.give(i, kk)
        return act.act(self.g[:, :, :], self.g[:, :, :], ACT.Tanh, w=[kk])

    def layer2(self):
        k = self.dve.now()
        self.normed(lambda t: [k])
        ks = self.layer2_attention()
        k = self.layer2_recurrence()
        return self.gated(self.s, [k, ks])

    def layer3_parts(self):
        pe, d, act, pool, sp, w3 = self.pe, self.dve, self.act, self.pool, self.sp, self.w3
        start = [e.now() for e in (pe, d, act, pool)]
        for e in (d, act, pool):
            e.wait(start)
        wk = self.work
        self.qs = [wk[:, 2048 * n:2048 * n + 2048].bitcast(BF16) for n in range(2)]
        self.ks = [wk[:, 2048 * n:2048 * n + 2048].bitcast(BF16) for n in (2, 3)]
        self.k_fill = [e.fill(x[n], v) for n in range(2) for e, x, v in ((pool, self.ks, 1.0), (pool, self.qs, 0.0))]
        k = self.layernorm(self.xn, self.t1, lambda t: [self.k_xn])
        kT = self.transposed(self.t1, lambda q: self.tT[:, q * 512:(q + 1) * 512], [k] + self.k_w3,
                             gain=w3["ln_g"], bias=w3["ln_b"], w_dst=start)
        self.k_nT = kT
        xt, w2s = self.xT[:, :, :].rearrange("p b n -> p (b n)"), self.w2.tensor
        self.parts = [self.nc.dram_tensor(f"{n}_parts", (3 * 8, NB, 16 * NS), BF16, kind="Internal").ap() for n in "qk"]
        three = [a.bitcast(BF16).rearrange("p (q n) -> p q n", q=3) for a in (xt[:, 0:768], xt[:, 768:1536], w2s[:, 0:768])]
        beyond = self.r3.start + self.r3.width
        res = [w2s[:, 768:1280], self.w3.tensor[:, beyond:beyond + 512]]
        ch_put = [self.p.channel(f"ch_parts{n}", sp) for n in range(3)]
        put = self.k_put = {}
        for u in range(8):
            j, x = u // 2, u % 2
            q3, rs = three[u % 3], res[x]
            i, ps, wb = self.banks.take()
            k = pe.mm(ps, w3["qk"[x]], self.tT[:, j * 512:(j + 1) * 512], w=kT + wb)
            k = act.act(q3[:, 0, :], ps, ACT.Copy, w=[k, put.get(u - 3)])
            k = d.tt(rs, ps, q3[:, 0, :], ALU.subtract, w=[k, put.get(("res", x))])
            self.banks.give(i, k)
            k = act.act(q3[:, 1, :], rs, ACT.Copy, w=[k])
            k = put["res", x] = d.tt(q3[:, 2, :], rs, q3[:, 1, :], ALU.subtract, w=[k])
            for q in range(3):
                for bb in range(2):
                    dst = self.parts[x][8 * q:8 * q + 8, 2 * j + bb, :].rearrange("d (h n) -> h d n", h=16)
                    put[u] = sp.dma(dst, q3[:, q, bb * NS:(bb + 1) * NS], ch_put[u % 3], w=[k])
        self.k_values = []
        for j in range(4):
            i, ps, wb = self.banks.take()
            for q in range(4):
                t = 4 * j + q
                k = pe.mm(ps[:, q * 128:(q + 1) * 128], self.tT[:, t * 128:(t + 1) * 128], w3["v"], w=wb)
            k = act.act(self.t1[:, 4 * j:4 * j + 4, :], ps.rearrange("p (r c) -> p r c", c=C), ACT.Copy, w=[k])
            self.banks.give(i, k)
            self.k_values.append(k)

    def layer3_gates(self):
        pe, d, act, pool, w3, r3 = self.pe, self.dve, self.act, self.pool, self.w3, self.r3
        kT = self.k_nT
        tile = lambda t: self.tT[:, t * 128:(t + 1) * 128]
        hl = self.stats[:, :, 0:2]
        k = self.logits(tile, w3["halt"], r3["halt_b"], hl, kT)
        alpha, rem, wsum, h = (self.v[i][:, :] for i in (11, 6, 12, 8))
        self.alpha, self.wsum = alpha, wsum
        ka = act.act(alpha, hl[:, :, 0], ACT.Sigmoid, w=[k])
        for step in range(3):
            if step < 2:
                k = act.act(h, hl[:, :, 1], ACT.Sigmoid, bias=r3["step_b"][:, step:step + 1], w=[k])
                if step == 0:
                    k1 = d.cp(wsum, h, w=[k])
                    k2 = d.ts(rem, h, -1.0, 1.0, ALU.mult, ALU.add, w=[k])
                    k = d.ts(rem, rem, 0.0, op0=ALU.max, w=[k1, k2])
                else:
                    k = d.tt(h, h, rem, ALU.mult, w=[k])
                    k1 = d.tt(wsum, wsum, h, ALU.add, w=[k])
                    k = d.tt(rem, rem, h, ALU.subtract, w=[k1])
                    k = d.ts(rem, rem, 0.0, op0=ALU.max, w=[k])
            else:
                k = d.tt(wsum, wsum, rem, ALU.add, w=[k])
        xp = self.xT[:, :, :].rearrange("p b n -> p (b n)")[:, 1536:2054]
        y, sg, z, xc = (self.work[:, 8192 + 512 * n:8704 + 512 * n] for n in range(4))
        two = lambda a: a.rearrange("p (b n) -> p b n", n=NS)
        kf = pool.fill(xp, 0.0)
        xp = xp.rearrange("p (b n) -> p b n", b=2)
        last = {}
        for j in range(4):
            X = self.tT[:, j * 512:(j + 1) * 512]
            i, ps, wb = self.banks.take()
            k = pe.mm(ps, w3["ssm"][:, 0:128], X, w=kT + wb)
            k = act.act(xp[:, :, 3:3 + NS], two(ps), ACT.Copy, w=[k, kf, last.get("y")])
            self.banks.give(i, k)
            cw = w3["conv_w"]
            k = d.ts(two(y), xp[:, :, 0:NS], cw[:, 0:1], w3["conv_b"], ALU.mult, ALU.add, w=[k, last.get("sg")])
            for m in range(1, 4):
                k = d.stt(two(y), xp[:, :, m:m + NS], cw[:, m:m + 1], two(y), ALU.mult, ALU.add, w=[k])
            last["y"] = k
            last["sg"] = k1 = act.act(sg, y, ACT.Sigmoid, w=[k, last.get("xc")])
            i, ps, wb = self.banks.take()
            k = pe.mm(ps, w3["ssm"][:, 128:256], X, w=wb)
            k2 = act.act(z, ps, ACT.Sigmoid, w=[k])
            self.banks.give(i, k2)
            k = pool.tt(xc, y, sg, ALU.mult, w=[k1, last.get("out")])
            k = last["xc"] = d.tt(xc, xc, z, ALU.mult, w=[k, k2])
            last["sg"] = k
            i, ps, wb = self.banks.take()
            for q in range(4):
                kk = pe.mm(ps[:, q * 128:(q + 1) * 128], xc[:, q * 128:(q + 1) * 128], w3["ssm_out"], w=[k] + wb)
            last["out"] = kk
            k = d.cp(self.s[:, 4 * j:4 * j + 4, :], ps.rearrange("p (r c) -> p r c", c=C), w=[kk])
            self.banks.give(i, k)
            i, ps, wb = self.banks.take()
            for q in range(4):
                kk = pe.mm(ps[:, q * 128:(q + 1) * 128], tile(4 * j + q), w3["gate"], w=wb)
            k = act.act(self.g[:, 4 * j:4 * j + 4, :], ps.rearrange("p (r c) -> p r c", c=C), ACT.Sigmoid, w=[kk])
            self.banks.give(i, k)

    def layer3_attention(self):
        pe, d, act, pool, sp, w3, c = self.pe, self.dve, self.act, self.pool, self.sp, self.w3, self.c
        p = self.p
        ROWS = 96
        PAIRS_Q, PAIRS_K = (0, 0, 0, 1, 1, 2), (0, 1, 2, 0, 1, 0)
        HALF = 8 * NS
        start = [e.now() for e in (pe, d, act, pool)]
        for e in (d, act, pool):
            e.wait(start)
        wk, qs, ks, parts, put = self.work, self.qs, self.ks, self.parts, self.k_put
        w2s, beyond = self.w2.tensor, self.r3.start + self.r3.width
        free = [self.tT[:, 512 * n:512 * n + 512] for n in range(4)] + [w2s[:, 512 * n:512 * n + 512] for n in range(3)]
        PT = free + [self.w3.tensor[:, beyond:beyond + 512]]
        Vs = [wk[:, 8192 + 1024 * n:9216 + 1024 * n].rearrange("p (r h x) -> p r h x", r=2, h=16) for n in range(2)]
        spare = wk[:, 10240:10496]
        resid, mx, den = spare[0:16, 0:128], spare[:, 128:160], spare[:, 160:176]
        xt = self.xT[:, :, :].rearrange("p b n -> p (b n)")
        oT = [xt[:, 512 * n:512 * n + 512] for n in range(2)]
        ot = xt[:, 1024:1280].rearrange("p (r c) -> p r c", r=2)
        otT = xt[:, 1280:1536]
        mparts = [xt[0:16, 1536 + 192 * n:1728 + 192 * n].bitcast(BF16).rearrange("p (q n) -> p q n", q=3) for n in range(2)]
        scale = float(np.float32(8.0) ** np.float32(-0.5))
        ch_ld = [[p.channel(f"ch_heads{b}{h}", sp) for h in range(2)] for b in range(2)]
        ch_max = [[p.channel(f"ch_max{b}{h}", sp) for h in range(2)] for b in range(2)]

        for V in Vs:
            k1 = pool.fill(V, 0.0)
            k1 = pool.fill(V[:, :, :, 8], 1.0, w=[k1])
        last = {}

        def since(name):
            lp = p.loop
            if lp is None:
                return last.get(name)
            t = last.get(name)
            return t if t is not None and t.loop is lp else lp.prev(str(name))

        def did(name, k):
            last[name] = k
            if p.loop is not None:
                p.loop.mark(str(name), k)
            return k

        def load_heads(b, par, half):
            cols = slice(half * HALF, (half + 1) * HALF)
            w = [since(("pass2", par, half))] + self.k_fill
            for x, side, dst in ((0, PAIRS_Q, qs[par]), (1, PAIRS_K, ks[par])):
                runs, at = ((3, 2, 1), 0)
                for n in runs:
                    out = dst[8 * at:8 * (at + n), cols]
                    first = side[at]
                    if x == 0:
                        src = parts[0][8 * first:8 * first + 8, bass.ds(b, 1), cols].rearrange("d b n -> d (b n)")
                        src = src.unsqueeze(0).broadcast_to((n, 8, HALF))
                    else:
                        src = parts[1][0:8 * n, bass.ds(b, 1), cols].rearrange("d b n -> d (b n)")
                    k = sp.dma(out, src, ch_ld[par][half], w=w)
                    at += n
            did(("load", par, half), k)

        def pass1(par, h):
            half = h // 8
            i, ps, wb = self.banks.take()
            for r in range(2):
                k = pe.mm(ps[:, r * NS:(r + 1) * NS], qs[par][0:ROWS, h * NS + r * 128:h * NS + r * 128 + 128],
                          ks[par][0:ROWS, h * NS:(h + 1) * NS], w=[since(("load", par, half))] + wb, inc=(r == 1))
            did(("pass1", par, half), k)
            src = ps.rearrange("p (r n) -> p r n", r=2)
            a = (h % 8) * 2
            d.wait([k, since(("mxT", half))])
            k = d.put(lambda: d.eng.tensor_reduce(mx[:, 16 * half + a:16 * half + a + 2], src, AX, ALU.max, negate=True))
            self.banks.give(i, k)
            did(("mx", half), k)

        def maxima(par, half):
            mp = mparts[half]
            i, ps, wb = self.banks.take()
            m = ps[0:16, 0:128]
            k = did(("mxT", half), pe.tr(m, mx[:, 16 * half:16 * half + 16], c["ident"], w=[since(("mx", half))] + wb))
            k = d.cp(mp[:, 0, :], m, w=[k, since(("max", 0, half)), since(("max", 1, half))])
            k = d.tt(resid, m, mp[:, 0, :], ALU.subtract, w=[k])
            self.banks.give(i, k)
            k = d.cp(mp[:, 1, :], resid, w=[k])
            k = d.tt(mp[:, 2, :], resid, mp[:, 1, :], ALU.subtract, w=[k])
            for q in range(3):
                kk = sp.dma(qs[par][ROWS + q:ROWS + q + 1, half * HALF:(half + 1) * HALF], mp[:, q, :], ch_max[par][half], w=[k])
            did(("max", par, half), kk)

        def values(b, par):
            src = self.t1[:, bass.ds(2 * b, 2), :].rearrange("p r (h x) -> p r h x", h=16)
            did(("V", par), pool.cp(Vs[par][:, :, :, 0:8], src, w=self.k_values + [since(("pv", par))]))

        def pass2(par, h):
            half, u = h // 8, h % 8
            i, ps, wb = self.banks.take()
            for kt in range(2):
                k = pe.mm(ps[:, kt * NS:(kt + 1) * NS], ks[par][0:ROWS + 3, h * NS + kt * 128:h * NS + kt * 128 + 128],
                          qs[par][0:ROWS + 3, h * NS:(h + 1) * NS], w=[since(("load", par, half)), since(("max", par, half))] + wb,
                          inc=(kt == 1))
            did(("pass2", par, half), k)
            k = act.act(PT[u], ps, ACT.Exp, scale=scale, w=[k, since(("used", u))])
            self.banks.give(i, k)
            did(("exp", u), k)

        def product(par, g4):
            po = self.banks.ps[:, 7 * 512:8 * 512]
            o = po[:, (g4 % 2) * NS:(g4 % 2 + 1) * NS]
            for g in range(4):
                u = (4 * g4 + g) % 8
                for kt in range(2):
                    k = pe.mm(o[32 * g:32 * g + 32, :], Vs[par][:, kt, 4 * g4 + g, :], PT[u][:, kt * NS:(kt + 1) * NS],
                              first=(kt == 0), last=(kt == 1), w=[since(("exp", u)), since(("V", par)), since("po")])
                did(("used", u), k)
            did(("pv", par), k)
            if g4 % 2:
                half = g4 // 2
                k = act.act(oT[half], po, ACT.Copy, w=[k, since(("oTtr", half))])
                did("po", k)
                did(("oT", half), k)

        def divide(half):
            i, ps, wb = self.banks.take()
            for a in range(2):
                for r in range(2):
                    x = (2 * a + r) * 128
                    k = pe.tr(ps[:, x:x + 128], oT[half][:, a * NS + r * 128:a * NS + r * 128 + 128], c["ident"],
                              w=[since(("oT", half))] + wb, inc=(x == 384))
            did(("oTtr", half), k)
            s4 = ps.rearrange("p (a r g x) -> p a r g x", a=2, r=2, g=4)
            dn = den.rearrange("p (a r g) -> p a r g", a=2, r=2)
            k = d.rcp(dn, s4[:, :, :, :, 8], w=[k, since("ot")])
            for a in range(2):
                g4 = 2 * half + a
                dst = ot.rearrange("p r (h x) -> p r h x", h=16)[:, :, 4 * g4:4 * g4 + 4, :]
                kk = did("ot", d.tt(dst, s4[:, a, :, :, 0:8], dn[:, a].unsqueeze(3).broadcast_to((P, 2, 4, 8)), ALU.mult,
                                    w=[k, since("ottr")]))
            self.banks.give(i, kk)

        def turn_out():
            i, ps, wb = self.banks.take()
            for r in range(2):
                k = pe.tr(ps[:, r * 128:(r + 1) * 128], ot[:, r, :], c["ident"], w=[since("ot")] + wb, inc=(r == 1))
            did("ottr", k)
            k = did("otT", act.act(otT, ps[:, 0:256], ACT.Copy, w=[k, since("wout")]))
            self.banks.give(i, k)

        def project_out(b):
            i, ps, wb = self.banks.take()
            for r in range(2):
                k = pe.mm(ps[:, r * 128:(r + 1) * 128], otT[:, r * 128:(r + 1) * 128], w3["attn_out"],
                          w=[since("otT")] + wb, inc=(r == 1))
            did("wout", k)
            k = d.cp(self.t1[:, bass.ds(2 * b, 2), :], ps[:, 0:256].rearrange("p (r c) -> p r c", r=2),
                     w=[k, since(("V", 0)), since(("V", 1))])
            self.banks.give(i, k)

        def heads(b, par, queue, ahead=None, load=True, this=True):
            def later(n, step):
                queue.append([n, step])

            if this:
                values(b, par)
            for h in range(16):
                if ahead is not None:
                    pass1(1 - par, h)
                if this:
                    pass2(par, h)
                for q in queue:
                    q[0] -= 1
                while queue and min(q[0] for q in queue) <= 0:
                    due = next(q for q in queue if q[0] <= 0)
                    queue.remove(due)
                    due[1]()
                half = h // 8
                if h % 8 == 7:
                    if ahead is not None:
                        later(1, lambda half=half: maxima(1 - par, half))
                    if this and load:
                        load_heads(b + 2, par, half)
                if this and h % 4 == 3:
                    later(2, lambda g4=h // 4: product(par, g4))
                    if h % 8 == 7:
                        later(4, lambda half=half: divide(half))
                    if h == 15:
                        later(6, turn_out)
                        later(8, lambda: project_out(b))

        def flush(queue):
            for q in sorted(queue, key=lambda q: q[0]):
                q[1]()
            queue.clear()

        sp.wait([put[u] for u in range(2)])
        for b in range(2):
            for half in range(2):
                load_heads(b, b, half)
        self.banks.only(7)
        pe.wait(self.banks.free[7])
        queue = []
        heads(-1, 1, queue, ahead=0, load=False, this=False)
        flush(queue)
        every = [e.now() for e in (pe, d, act, pool)] + [last[n, b, h] for n, b, h in
                 [(n, b, h) for n in ("load",) for b in range(2) for h in range(2)] + [("max", 0, 0), ("max", 0, 1)]]
        for e in (pe, d, act, pool, sp):
            e.wait(every + [put[u] for u in range(5, 8)])

        def body(i, lp):
            queue = []
            last.clear()
            for par in range(2):
                heads(2 * i + par, par, queue, ahead=2 * i + par + 1)
            flush(queue)

        self.banks.run_loop(3, body)
        for par in range(2):
            heads(6 + par, par, queue, ahead=7 if par == 0 else None, load=False)
        flush(queue)
        self.banks.free[7] = [last["po"]]
        self.banks.only(8)
        return d.now()

    def layer3_mixture(self, k):
        d, act, pool, r3, w3 = self.dve, self.act, self.pool, self.r3, self.w3
        s, t1, g = self.s, self.t1, self.g
        A = lambda t: t[:, :, :]
        k = d.tt(A(t1), A(t1), A(g), ALU.mult, w=[k, act.now()])
        k = d.tt(A(t1), A(t1), A(s), ALU.subtract, w=[k])
        k = d.tt(A(t1), A(t1), grow_in(self.alpha, C), ALU.mult, w=[k])
        k = d.tt(A(s), A(s), A(t1), ALU.add, w=[k])
        k = d.tt(A(s), A(s), grow(r3["ls1"], NT), ALU.mult, w=[k])
        k = d.tt(A(s), A(s), A(self.xn), ALU.add, w=[k])
        k = self.layernorm(s, t1, lambda t: [k], r3["ln2_g"], r3["ln2_b"])
        kT = self.transposed(t1, lambda q: self.tT[:, q * 512:(q + 1) * 512], [k], w_dst=[self.pe.now()])
        lg = self.k8[0][:, :, :]
        zero8 = self.zero[:, 0:8]
        k = self.logits(lambda t: self.tT[:, t * 128:(t + 1) * 128], w3["router"], zero8, lg, kT)
        oh, m, k = self.top2(lg, [k])
        Z, p2, sm = self.v[0][:, :], self.v[1][:, :], self.v[2][:, :]
        k1 = d.tt(lg, lg, grow_in(m[0], E), ALU.subtract, w=[k])
        k2 = d.tt(p2, m[1], m[0], ALU.subtract, w=[k])
        k1 = act.act(lg, lg, ACT.Exp, w=[k1])
        k2 = act.act(p2, p2, ACT.Exp, w=[k2])
        k = d.red(Z, lg, ALU.add, w=[k1])
        k = d.rcp(Z, Z, w=[k])
        k = d.tt(p2, p2, Z, ALU.mult, w=[k, k2])
        k = d.tt(sm, p2, Z, ALU.add, w=[k])
        k = d.ts(sm, sm, 1e-8, op0=ALU.add, w=[k])
        k = d.rcp(sm, sm, w=[k])
        k1 = d.tt(self.gates[:, 0, :], Z, sm, ALU.mult, w=[k])
        k2 = d.tt(self.gates[:, 1, :], p2, sm, ALU.mult, w=[k])
        k, kt = self.slots(oh, [k1, k2])
        kd = self.dispatch(t1, self.xs[2], 2, [self.k_clear[2]], [k])

        def mid(net, u, ps, ex, k, since):
            return act.act(net.hm[u][:, 0:256], ps[:, 0:256], ACT.Silu, w=[k, since("a")])

        def mid_end(net, u, ps, k, since):
            return d.tt(net.ha[u][:, 0:256], net.hm[u][:, 0:256], ps[:, 256:512], ALU.mult, w=[k, since("trm")])

        ko = self.experts(self.xs[2], self.ys[2], 40, [kd, kt, k] + [e.now() for e in (self.pe, d, act, pool)], mid,
                          ACT.Silu, 512, 2, w3["w13"], w3["w2"], mid_end=mid_end)
        both = [self.work[:, n * 2048:(n + 1) * 2048].rearrange("p (t c) -> p t c", c=C) for n in range(2)]
        kc = self.collect(both, self.ys[2], [0, 1], ko + [d.now(), act.now(), self.pe.now(), pool.now()])
        k = d.fill(A(t1), 0.0)
        k = self.weighted(t1, both, [kc, k])
        k = d.tt(A(t1), A(t1), grow(r3["ls2"], NT), ALU.mult, w=[k])
        k = d.tt(A(s), A(s), A(t1), ALU.add, w=[k])
        k = d.tt(A(s), A(s), grow_in(self.wsum, C), ALU.mult, w=[k])
        return d.tt(A(s), A(s), A(self.xn), ALU.add, w=[k])

    def layer3_ffn(self):
        d, act, pool, r3, w3 = self.dve, self.act, self.pool, self.r3, self.w3
        t1 = self.t1
        A = lambda t: t[:, :, :]
        ms, rs = self.v[0][:, :], self.v[1][:, :]
        start = [d.now(), self.pe.now(), pool.now()]
        for t in range(NT):
            k = act.act(t1[:, t, :], self.xn[:, t, :], ACT.Square, w=start, acc=ms[:, t:t + 1])
        k = d.ts(ms, ms, 1.0 / C, EPS, ALU.mult, ALU.add, w=[k])
        k = self.rsqrt(rs, ms, [k])
        for t in range(NT):
            kk = d.stt(t1[:, t, :], self.xn[:, t, :], rs[:, t:t + 1], r3["norm"], ALU.mult, ALU.mult, w=[k])
        kT = self.transposed(t1, lambda q: self.tT[:, q * 512:(q + 1) * 512], [kk], w_dst=[self.pe.now()])
        lg = self.k8[0][:, :, :]
        k = self.logits(lambda t: self.tT[:, t * 128:(t + 1) * 128], w3["gate_w"], r3["gate_b"], lg, kT)
        oh, m, k = self.top2(lg, [k])
        k = self.pair_softmax(m, self.gates[:, 0, :], self.gates[:, 1, :], [k])
        k, kt = self.slots(oh, [k])
        kd = self.dispatch(t1, self.xs[3], 2, [self.k_clear[3]], [k])
        b1 = r3["mlp1_b"]
        ALPHA = 1.702

        def mid(net, u, ps, ex, k, since):
            d.wait([k, since("a")])
            k = d.put(lambda: d.eng.tensor_tensor(net.hm[u], ps, b1[:, bass.ds(ex * 512, 512)], ALU.add))
            k1 = d.ts(net.hm[u][:, 0:256], net.hm[u][:, 0:256], 7.0, op0=ALU.min, w=[k])
            k2 = d.ts(net.hm[u][:, 256:512], net.hm[u][:, 256:512], 7.0, -7.0, ALU.min, ALU.max, w=[k])
            return act.act(net.ha[u][:, 256:512], net.hm[u][:, 0:256], ACT.Silu, scale=ALPHA, w=[k1, k2, since("a")])

        def mid_end(net, u, ps, k, since):
            return d.stt(net.ha[u][:, 0:256], net.hm[u][:, 256:512], 1.0, net.ha[u][:, 256:512], ALU.add, ALU.mult,
                         w=[k, since("trm")])

        ko = self.experts(self.xs[3], self.ys[3], 40, [kd, kt, k] + [e.now() for e in (self.pe, d, act, pool)], mid,
                          ACT.Silu, 512, 2, w3["mlp1"], w3["mlp2"], b1, r3["mlp2_b"], yscale=1.0 / ALPHA, mid_end=mid_end)
        both = [self.work[:, n * 2048:(n + 1) * 2048].rearrange("p (t c) -> p t c", c=C) for n in range(2)]
        kc = self.collect(both, self.ys[3], [0, 1], ko + [d.now(), act.now(), self.pe.now(), pool.now()])
        k = d.cp(A(self.g), A(self.xn))
        return self.weighted(self.g, both, [kc, k])

    def layer3(self):
        k = self.dve.now()
        self.normed(lambda t: [k], turned=False)
        self.layer3_parts()
        self.layer3_gates()
        k = self.layer3_attention()
        ks = self.layer3_mixture(k)
        k = self.layer3_ffn()
        return self.gated(self.s, [k, ks])


def build(nc, ins, out, upto=4):
    n = Net(nc, ins)
    n.start()
    n.layer0()
    if upto > 1:
        n.layer1()
    n.load_layer3()
    if upto > 2:
        n.layer2()
    if upto > 3:
        n.layer3()
    src = n.x
    k = n.sp.dma(out.rearrange("(t p) c -> p t c", p=P), src[:, :, :], n.ch_out_x, [n.dve.now()])
    n.sp.wait([k])
    for e in n.p.engines[:4]:
        n.sp.wait([e.now()])
    return n


def constants():
    f = np.float32
    i = np.arange(P)
    t = {"ident": np.eye(P), "ones": np.ones((P, P)), "before": (i[:, None] < i[None, :]),
         "swap": (i[:, None] == (i[None, :] + 64) % P)}
    channel = np.where(i < 64, 2 * i, 2 * (i - 64) + 1)
    t["heads"] = (channel[:, None] // 16 == np.arange(8)[None, :]) / f(NS)
    t["kv_mask"] = (i[:, None] // 16 == i[None, :] // 16) / np.sqrt(f(NS))
    n = np.arange(NS, dtype=f)
    theta = f(1.0) / f(10000.0) ** (np.arange(64, dtype=f) / f(64))
    ang = (n[:, None] * theta).T
    t["rope_cos"] = np.concatenate([np.cos(ang)] * 2)
    t["rope_sin"] = np.concatenate([-np.sin(ang), np.sin(ang)])
    rot = np.eye(P)
    rot[2 * np.arange(64) + 1, 2 * np.arange(64)] = -1
    rot[2 * np.arange(64), 2 * np.arange(64) + 1] = 1
    t["rot2"] = rot
    inv = f(10000.0) ** (np.arange(0, 64, 2, dtype=f) / f(64))
    rad = n[:, None] / inv
    t["rope2"] = np.repeat(np.stack((np.sin(rad), np.cos(rad)), axis=-1).reshape(NS, -1), 2, axis=-1).T
    t["iota8"] = np.tile(np.arange(8), (P, 1))
    t["iota384"] = np.tile(np.arange(8) * 384, (P, 1))
    t["tile_start"] = np.tile((np.arange(TILES) - LEAD) * P, (P, 1))
    t["tile_third"] = np.tile(np.clip((np.arange(TILES) - LEAD) // 3, 0, 7), (P, 1))
    t["octal"] = np.tile(8 ** np.arange(4), (P, 1))
    t["scan_mask"] = np.tile(i % NT != 0, (P, 1))
    t["bits"] = np.tile(2.0 ** np.arange(29, -1, -1), (P, 1))
    return t


def packed(fields, values):
    return np.ascontiguousarray(np.concatenate([np.asarray(values[n], np.float32).reshape(-1, w) for n, w in fields], axis=1))


def lay_out(a):
    T = np.transpose
    even_first = np.r_[0:C:2, 1:C:2]
    o = {"x": a["L0_attn_x"].reshape(TOK, C), "consts": packed(CONSTS, constants())}
    g = lambda p: (lambda n: np.asarray(a[p + n]))
    A, B = g("L0_attn_"), g("L0_ffn_")
    o["w0"] = packed(W0, {
        "q": A("qk_w")[:, :C][:, even_first], "k": A("qk_w")[:, C:][:, even_first],
        "lepe": T(A("lepe_w"), (1, 0, 2)).reshape(C, 384), "qkv": B("in_proj_w").T, "out": B("out_w").T,
        "router": B("router_w").T, "q_b": A("qk_b")[:C][even_first][:, None], "k_b": A("qk_b")[C:][even_first][:, None],
        "w1": T(B("w1"), (2, 0, 1)).reshape(C, 1024), "w2": T(B("w2"), (2, 0, 1)).reshape(C, 1024)})
    o["r0"] = packed(R0, {"lepe_b": A("lepe_b"), "qkv_b": B("in_proj_b"), "out_b": B("out_b"), "ln1_g": B("ln1_g"),
                          "ln1_b": B("ln1_b"), "ln2_g": B("ln2_g"), "ln2_b": B("ln2_b"), "router_b": B("router_b"),
                          "b1": B("b1"), "b2": B("b2")})
    A, B = g("L1_attn_"), g("L1_ffn_")
    o["w1"] = packed(W1, {
        "hidden": A("W_hidden"), "qk": A("W_qk"), "out": T(A("W_out").reshape(2, C, C), (1, 0, 2)).reshape(C, 256),
        "router": B("Wr"), "ln_g": A("ln_scale")[:, None], "ln_b": A("ln_bias")[:, None], "qk_b": A("b_qk")[:, None],
        "osw": A("os_weight").T, "osb": A("os_bias").T, "w1": T(B("W1"), (1, 0, 2)).reshape(C, 4096),
        "w2": T(B("W2").reshape(E, 4, C, C), (2, 0, 1, 3)).reshape(C, 4096)})
    o["r1"] = packed(R1, {"hidden_b": A("b_hidden"), "out_b": A("b_out"), "router_b": B("br"), "gamma": B("gamma"),
                          "beta": B("beta"), "b1": B("b1"), "b2": B("b2")})
    A, B = g("L2_attn_"), g("L2_ffn_")
    o["w2"] = packed(W2, {
        "wq": A("Wq"), "wk": A("Wk"), "wv": A("Wv").T, "wf": B("wf").T, "wi": B("wi").T, "wc": B("wc").T,
        "uf": B("uf").T, "ui": B("ui").T, "uc": B("uc").T, "wo": B("wo").T, "uo": B("uo").T,
        "bq": A("bq")[:, None], "bk": A("bk")[:, None], "bf": B("bf")[:, None], "bi": B("bi")[:, None],
        "bc": B("bc")[:, None], "c0": B("in_c")[:, None]})
    o["r2"] = packed(R2, {"bv": A("bv"), "bo": B("bo")})
    A, B = g("L3_attn_"), g("L3_ffn_")

    qkv = A("Wqkv")
    w13 = np.stack([T(A("W1"), (1, 0, 2)), T(A("W3"), (1, 0, 2))], axis=2).reshape(C, 4096)
    halves = np.r_[0:512:2, 1:512:2]
    o["w3"] = packed(W3, {
        "q": qkv[:, 0:C], "k": qkv[:, C:2 * C], "v": qkv[:, 2 * C:], "gate": A("Wgate"),
        "ssm": A("Win_ssm"), "ssm_out": A("Wout_ssm"), "attn_out": A("Wout"), "halt": A("Wr"), "router": A("Wg"),
        "gate_w": B("gate_w"), "ln_g": A("ln1_g")[:, None], "ln_b": A("ln1_b")[:, None],
        "conv_w": A("conv_w").reshape(C, 4), "conv_b": A("conv_b")[:, None], "w13": w13,
        "w2": T(A("W2").reshape(E, 2, C, C), (2, 0, 1, 3)).reshape(C, 2048),
        "mlp1": T(B("mlp1_w")[:, :, halves], (1, 0, 2)).reshape(C, 4096),
        "mlp2": T(B("mlp2_w").reshape(E, 2, C, C), (2, 0, 1, 3)).reshape(C, 2048)})
    o["r3"] = packed(R3, {"ln2_g": A("ln2_g"), "ln2_b": A("ln2_b"), "ls1": A("ls1"), "ls2": A("ls2"),
                          "halt_b": A("br"), "step_b": A("step_bias"), "norm": B("norm_scale"), "gate_b": B("gate_b"),
                          "mlp1_b": B("mlp1_b")[:, halves], "mlp2_b": B("mlp2_b")})
    return o


def kernel(**inputs):
    import concourse.bacc as bacc
    from concourse.bass_utils import run_bass_kernel_spmd

    nc = bacc.Bacc("TRN2", target_bir_lowering=False, num_devices=1)
    arrays = {f"in_{k}": np.ascontiguousarray(v) for k, v in lay_out({k: np.asarray(v) for k, v in inputs.items()}).items()}
    ins = {k[3:]: nc.dram_tensor(k, v.shape, F32, kind="ExternalInput").ap() for k, v in arrays.items()}
    out = nc.dram_tensor("out", (TOK, C), F32, kind="ExternalOutput").ap()
    build(nc, ins, out)
    r = run_bass_kernel_spmd(nc, [arrays], core_ids=[0])
    return r.results[0]["out"].reshape(NB, NS, C)
```

```python
import numpy as np
import concourse.bass as bass
from concourse import mybir
from concourse.alu_op_type import AluOpType as ALU

F32 = mybir.dt.float32
BF16 = mybir.dt.bfloat16
I32 = mybir.dt.int32
ACT = mybir.ActivationFunctionType
AX = mybir.AxisListType.X

P = 128
C = 128
NB, NS = 8, 256
NT = NB * NS // P
TOK = NB * NS
E = 8
EPS = 1e-5
LEAD = 4
PAIRS_Q, PAIRS_K = (0, 0, 0, 1, 1, 2), (0, 1, 2, 0, 1, 0)
TILES = 52
PAD = 1000


class Token:

    def __init__(self, src, off, loop, back=0):
        self.src, self.off, self.loop, self.back = src, off, loop, back


class Loop:

    def __init__(self, count):
        self.count, self.i, self.base, self.per, self.marks = count, 0, {}, {}, {}

    def mark(self, name, tok):
        self.marks[name] = tok
        return tok

    def prev(self, name, back=1):
        t = self.marks.get(name)
        return None if t is None else Token(t.src, t.off, self, back)


class Source:

    def __init__(self, prog, name, step):
        self.prog, self.step, self.n, self.pad = prog, step, 0, PAD
        self.sem = prog.nc.alloc_semaphore(name)
        prog.sources.append(self)

    def took(self):
        self.n += self.step
        lp = self.prog.loop
        return Token(self, self.n if lp is None else self.n - lp.base.get(self, 0), lp)

    def value(self, t):
        lp = t.loop
        if lp is None:
            return self.pad + t.off
        k = lp.per.get(self, 0)
        if lp is self.prog.loop:
            return lp.i * k + (self.pad + lp.base.get(self, 0) + t.off - k * t.back)
        return self.pad + lp.base.get(self, 0) + (lp.count - 1) * k + t.off


class Engine(Source):
    def __init__(self, prog, name, eng):
        super().__init__(prog, "done_" + name, 1)
        self.eng = eng
        self.seen = {}

    def wait(self, toks):
        for t in toks:
            if t is None or self.prog.dry:
                continue
            key = (t.src, t.loop if t.loop is self.prog.loop else None)
            rank = (-t.back, t.off) if key[1] is not None else (0, t.src.value(t))
            if key in self.seen and self.seen[key] >= rank:
                continue
            self.seen[key] = rank
            self.eng.wait_ge(t.src.sem, t.src.value(t))

    def put(self, build, w=(), inc=True):
        self.wait(w)
        if not self.prog.dry:
            ins = build()
            if inc:
                ins.then_inc(self.sem, 1)
        return self.took() if inc else None

    def now(self):
        lp = self.prog.loop
        return Token(self, self.n if lp is None else self.n - lp.base.get(self, 0), lp)

    def tt(self, out, a, b, op, w=()):
        return self.put(lambda: self.eng.tensor_tensor(out, a, b, op), w)

    def ts(self, out, a, s1, s2=None, op0=ALU.mult, op1=None, w=()):
        if op1 is None:
            return self.put(lambda: self.eng.tensor_scalar(out, a, s1, None, op0), w)
        return self.put(lambda: self.eng.tensor_scalar(out, a, s1, s2, op0, op1), w)

    def stt(self, out, a, s, b, op0, op1, w=(), acc=None):
        return self.put(lambda: self.eng.scalar_tensor_tensor(out=out, in0=a, scalar=s, in1=b, op0=op0, op1=op1,
                                                              accum_out=acc), w)

    def cp(self, out, a, w=()):
        return self.put(lambda: self.eng.tensor_copy(out, a), w)

    def red(self, out, a, op, w=()):
        return self.put(lambda: self.eng.tensor_reduce(out, a, AX, op), w)

    def rcp(self, out, a, w=()):
        return self.put(lambda: self.eng.reciprocal(out, a), w)

    def fill(self, out, val, w=()):
        return self.put(lambda: self.eng.memset(out, val), w)

    def act(self, out, a, func, w=(), bias=0.0, scale=1.0, acc=None):
        return self.put(lambda: self.eng.activation(out, a, func, bias=bias, scale=scale, accum_out=acc), w)

    def mm(self, out, lhsT, rhs, first=True, last=True, w=(), inc=None, shared=False):
        inc = last if inc is None else inc
        return self.put(lambda: self.eng.matmul(out, lhsT, rhs, start=first, stop=last, skip_group_check=shared), w, inc)

    def tr(self, out, a, ident, w=(), inc=True):
        return self.put(lambda: self.eng.transpose(out, a, ident), w, inc)

    def dma(self, out, a, ch, w=()):
        self.wait(w)
        if not self.prog.dry:
            self.eng.dma_start(out, a).then_inc(ch.sem, 16)
        return ch.took()

    def scatter_rows(self, table, idx, rows, ch, limit=None):
        extra = {} if limit is None else {"bounds_check": limit, "oob_is_err": False}
        self.eng.indirect_dma_start(table, bass.IndirectOffsetOnAxis(ap=idx, axis=0), rows, None, **extra).then_inc(ch.sem, 16)
        return ch.took()

    def gather_rows(self, rows, table, idx, ch, w=()):
        self.wait(w)
        if not self.prog.dry:
            self.eng.indirect_dma_start(rows, None, table, bass.IndirectOffsetOnAxis(ap=idx, axis=0)).then_inc(ch.sem, 16)
        return ch.took()


class Program:

    def __init__(self, nc):
        self.nc, self.sources, self.loop, self.dry = nc, [], None, False
        self.pe = Engine(self, "pe", nc.tensor)
        self.dve = Engine(self, "dve", nc.vector)
        self.act = Engine(self, "act", nc.scalar)
        self.pool = Engine(self, "pool", nc.gpsimd)
        self.sp = Engine(self, "sp", nc.sync)
        self.engines = [self.pe, self.dve, self.act, self.pool, self.sp]
        for e in self.engines:
            e.eng.sem_inc(e.sem, PAD)
        self.n_sb = 0

    def channel(self, name, issuer):
        ch = Source(self, name, 16)
        if issuer is self.pool:
            ch.pad = 0
        else:
            issuer.eng.sem_inc(ch.sem, PAD)
        return ch

    def run_loop(self, count, body):
        lp = Loop(count)
        lp.base = {s: s.n for s in self.sources}
        kept = {s: s.n for s in self.sources}
        self.loop, self.dry = lp, True
        body(0, lp)
        lp.per = {s: s.n - kept[s] for s in self.sources}
        for s in self.sources:
            s.n = kept[s]
        self.dry = False
        for e in self.engines:
            e.seen = {}
        with self.nc.Fori(0, count) as i:
            lp.i = i
            body(i, lp)
        lp.i = 0
        self.loop = None
        for s in self.sources:
            s.n = kept[s] + count * lp.per[s]
        for e in self.engines:
            e.seen = {}

    def sbuf(self, name, shape, dt=F32):
        return self.nc.alloc_sbuf_tensor(name, shape, dt)


class Steps:

    def __init__(self, prog):
        self.prog, self.last = prog, {}

    def did(self, name, k):
        self.last[name] = k
        if self.prog.loop is not None:
            self.prog.loop.mark(name, k)
        return k

    def since(self, name):
        lp, t = self.prog.loop, self.last.get(name)
        return t if lp is None or (t is not None and t.loop is lp) else lp.prev(name)


def weave(*lanes, first=1):
    lanes = [list(lane) for lane in lanes]
    while any(lanes):
        for lane in [lanes[0]] * (first - 1) + lanes:
            if lane:
                try:
                    next(lane[0])
                except StopIteration:
                    lane.pop(0)


def until(chain, mark):
    for at in chain:
        if at == mark:
            return
        yield


class Banks:

    def __init__(self, prog, nc):
        self.prog = prog
        self.ps = nc.alloc_psum_tensor("banks", [P, 8 * 512], F32)
        self.k, self.n, self.free, self.local, self.held = 0, 8, [[] for _ in range(8)], set(), set()

    def take(self, width=512):
        while self.k % self.n in self.held:
            self.k += 1
        i = self.k % self.n
        self.k += 1
        self.held.add(i)
        lp = self.prog.loop
        w = self.free[i]
        if lp is not None and i not in self.local:
            w = [lp.prev(f"bank{i}.{n}") for n in range(2)]
        return i, self.ps[:, i * 512:i * 512 + width], w

    def only(self, n):
        self.k, self.n = 0, n

    def give(self, i, *toks):
        self.free[i] = list(toks)
        self.held.discard(i)
        lp = self.prog.loop
        if lp is not None:
            self.local.add(i)
            for n, t in enumerate(toks):
                lp.mark(f"bank{i}.{n}", t)

    def run_loop(self, count, body):
        self.prog.pe.wait([t for f in self.free for t in f])

        def whole(i, lp):
            self.k, self.local = 0, set()
            self.free = [[] for _ in range(8)]
            body(i, lp)

        self.prog.run_loop(count, whole)
        self.k = 0


def grow(ap, n):
    return ap.unsqueeze(1).broadcast_to((ap.shape[0], n, ap.shape[1]))


def grow_in(ap, n):
    return ap.unsqueeze(2).broadcast_to((ap.shape[0], ap.shape[1], n))


class Pack:

    def __init__(self, fields):
        self.at, n = {}, 0
        for name, width in fields:
            self.at[name] = (n, n + width)
            n += width
        self.width = n

    def on(self, tensor, start=0):
        self.tensor, self.start = tensor, start
        return self

    def __getitem__(self, name):
        a, b = self.at[name]
        return self.tensor[:, self.start + a:self.start + b]


CONSTS = [("ident", 128), ("ones", 128), ("before", 128), ("swap", 128), ("heads", 8), ("kv_mask", 128),
          ("rope_cos", 256), ("rope_sin", 256), ("rot2", 128), ("rope2", 256), ("iota8", 8), ("iota384", 8),
          ("tile_start", 52), ("tile_third", 52), ("octal", 4), ("scan_mask", 128), ("quarters", 45)]
W0 = [("q", 128), ("k", 128), ("lepe", 384), ("qkv", 384), ("out", 128), ("router", 8), ("q_b", 1), ("k_b", 1),
      ("w1", 1024), ("w2", 1024)]
R0 = [("lepe_b", 128), ("qkv_b", 384), ("out_b", 128), ("ln1_g", 128), ("ln1_b", 128), ("ln2_g", 128),
      ("ln2_b", 128), ("router_b", 8), ("b1", 1024), ("b2", 1024)]
W1 = [("hidden", 512), ("qk", 128), ("out", 256), ("router", 8), ("ln_g", 1), ("ln_b", 1), ("qk_b", 1),
      ("osw", 2), ("osb", 2), ("w1", 4096), ("w2", 4096)]
R1 = [("hidden_b", 512), ("out_b", 128), ("router_b", 8), ("gamma", 128), ("beta", 128), ("b1", 4096), ("b2", 1024)]
W2 = [("wq", 128), ("wk", 128), ("wv", 128), ("wf", 128), ("wi", 128), ("wc", 128), ("uf", 128), ("ui", 128),
      ("uc", 128), ("wo", 128), ("uo", 128), ("bq", 1), ("bk", 1), ("bf", 1), ("bi", 1), ("bc", 1), ("c0", 1)]
R2 = [("bv", 128), ("bo", 128)]
W3 = [("q", 128), ("k", 128), ("v", 128), ("gate", 128), ("ssm", 256), ("ssm_out", 128), ("attn_out", 128),
      ("halt", 2), ("router", 8), ("gate_w", 8), ("ln_g", 1), ("ln_b", 1), ("conv_w", 4), ("conv_b", 1),
      ("w13", 4096), ("w2", 2048), ("mlp1", 4096), ("mlp2", 2048)]
R3 = [("ln2_g", 128), ("ln2_b", 128), ("ls1", 128), ("ls2", 128), ("halt_b", 2), ("step_b", 3), ("norm", 128),
      ("gate_b", 8), ("mlp1_b", 4096), ("mlp2_b", 1024)]


class Net:

    def __init__(self, nc, ins):
        self.nc = nc
        p = self.p = Program(nc)
        self.pe, self.dve, self.act, self.pool, self.sp = p.engines
        self.banks = Banks(p, nc)
        self.ins = ins
        sb = p.sbuf
        self.x = sb("x", [P, NT, C])
        self.xn = sb("xn", [P, NT, C])
        self.xT = sb("xT", [P, NB, NS + 2])
        self.s = sb("s", [P, NT, C])
        self.g = sb("g", [P, NT, C])
        self.t1 = sb("t1", [P, NT, C])
        self.t2 = self.g
        self.tT = sb("tT", [P, TOK])
        self.work = sb("work", [P, 10496])
        self.arena = self.work[:, 0:4352]
        self.qkv = self.work[:, 4352:10496].rearrange("p (t c) -> p t c", c=3 * C)
        self.c = Pack(CONSTS).on(sb("consts", [P, Pack(CONSTS).width]))
        w0, r0, w1, r1, w2, r2, w3, r3 = (Pack(f) for f in (W0, R0, W1, R1, W2, R2, W3, R3))
        room = max(w0.width + r0.width + w1.width + r1.width, w3.width + r3.width)
        wts = sb("weights", [P, room])
        self.w0, self.r0 = w0.on(wts, 0), r0.on(wts, w0.width)
        a = w0.width + r0.width
        self.w1, self.r1 = w1.on(wts, a), r1.on(wts, a + w1.width)
        self.w3, self.r3 = w3.on(wts, 0), r3.on(wts, w3.width)
        w2s = sb("weights2", [P, w2.width + r2.width])
        self.w2, self.r2 = w2.on(w2s, 0), r2.on(w2s, w2.width)
        self.stats = sb("stats", [P, NT, 6])
        self.v = [sb(f"small{i}", [P, NT]) for i in range(15)]
        self.k8 = [sb(f"byexpert{i}", [P, NT, E]) for i in range(8)]
        self.e8 = [sb(f"experts{i}", [P, E]) for i in range(6)]
        self.routes = [(sb(f"idx{n}", [P, 4, NT], I32), sb(f"gates{n}", [P, 2, NT]),
                        sb(f"eight{n}", [1, TILES // 4 - 1], I32)) for n in range(2)]
        self.use_route(0)
        self.scrap = sb("scrap", [P, 1])
        self.joint = sb("joint", [P, 1])
        self.tile_f = sb("tile_f", [1, 52, E])
        self.tile_n = sb("tile_n", [1, 52])
        self.ei = sb("ei", [P, E], I32)
        self.vi = sb("vi", [P, NT], I32)
        U = self.R = 4
        at = [0]

        def part(n):
            at[0] += n
            return self.work[:, at[0] - n:at[0]]

        self.hs = [part(C) for _ in range(U)]
        self.hT = [part(C) for _ in range(U)]
        self.hm = [part(512) for _ in range(U)]
        self.ha = [part(512) for _ in range(U)]
        self.aT = [part(512) for _ in range(U)]
        self.y = [part(C) for _ in range(U)]
        self.ch_in = [p.channel(f"ch_in{u}", self.act) for u in range(U)]
        self.ch_out = [p.channel(f"ch_out{u}", self.sp) for u in range(U)]
        self.ch_got, self.ch_got2 = ([p.channel(f"ch_got{t}{n}", self.pool) for t in range(NT)] for n in "ab")

    def use_route(self, n):
        self.idx, self.gates, self.eight = self.routes[n]

    def load(self, eng, pack, name, w=(), rows=False):
        ch = self.p.channel("ch_" + name, eng)
        dst = pack.tensor[:, pack.start:pack.start + pack.width]
        src = self.ins[name]
        if rows:
            src = src.broadcast_to((P, pack.width))
        return eng.dma(dst, src, ch, w)

    def rsqrt(self, out, v, w):
        d, t = self.dve, self.v[10]
        k = d.ts(self.vi[:, :], v.bitcast(I32), 1, op0=ALU.logical_shift_right, w=w)
        k = d.ts(out.bitcast(I32), self.vi[:, :], -1.0, float(0x5F3759DF), ALU.mult, ALU.add, w=[k])
        for _ in range(3):
            k = d.tt(t[:, :], out, out, ALU.mult, w=[k])
            k = d.stt(t[:, :], t[:, :], -0.5, v, ALU.mult, ALU.mult, w=[k])
            k = d.stt(out, t[:, :], 1.5, out, ALU.add, ALU.mult, w=[k])
        return k

    def layernorm(self, src, dst, w, gain=None, bias=None, w_dst=()):
        d, st = self.dve, self.stats
        diff, both, q, var, rstd, nmr = (self.v[i][:, :] for i in range(6))
        made = [None] * NT
        for t in range(NT):
            made[t] = w(t)
            k = d.put(lambda: d.eng.bn_stats(st[:, t, :], src[:, t, :]), made[t])
        k1 = d.tt(diff, st[:, :, 1], st[:, :, 4], ALU.subtract, w=[k])
        d.tt(both, st[:, :, 1], st[:, :, 4], ALU.add, w=[k])
        k3 = d.tt(q, st[:, :, 2], st[:, :, 5], ALU.add, w=[k])
        k4 = d.tt(diff, diff, diff, ALU.mult, w=[k1])
        k5 = d.ts(q, q, 1.0 / C, EPS, ALU.mult, ALU.add, w=[k3])
        k6 = d.stt(var, diff, 0.25, q, ALU.mult, ALU.add, w=[k4, k5])
        k7 = self.rsqrt(rstd, var, [k6])
        k8 = d.stt(nmr, both, -0.5, rstd, ALU.mult, ALU.mult, w=[k7])
        d.wait(w_dst)
        self.act.wait(w_dst)
        for t in range(2, NT, 3):
            self.act.wait(made[t])
        for t in range(NT):
            s, b = rstd[:, t:t + 1], nmr[:, t:t + 1]
            if t % 3 == 2:
                ka = self.act.act(dst[:, t, :], src[:, t, :], ACT.Identity, bias=b, scale=s, w=[k8])
            else:
                k = d.ts(dst[:, t, :], src[:, t, :], s, b, ALU.mult, ALU.add, w=[k8])
        if gain is None:
            return self.join([k, ka])

        def scaled(e, a, b):
            k1 = e.tt(dst[:, a:b, :], dst[:, a:b, :], grow(gain, b - a), ALU.mult, w=[k, ka])
            return e.tt(dst[:, a:b, :], dst[:, a:b, :], grow(bias, b - a), ALU.add, w=[k1])

        return self.split(scaled)

    def join(self, toks):
        return self.dve.cp(self.joint[:, :], self.joint[:, :], w=list(toks) + [self.dve.now()])

    def split(self, step):
        return self.join([step(self.dve, 0, 11), step(self.pool, 11, NT)])

    def transposed(self, src, dst4, w, gain=None, bias=None, w_dst=()):
        out = []
        for q in range(4):
            i, ps, wb = self.banks.take()
            for r in range(4):
                k = self.pe.tr(ps[:, r * 128:(r + 1) * 128], src[:, 4 * q + r, :], self.c["ident"],
                               w=list(w) + wb, inc=(r == 3))
            d = dst4(q)
            a = ps if len(d.shape) == 2 else ps.rearrange("p (b n) -> p b n", n=NS)
            if gain is not None:
                k = self.act.act(d, a, ACT.Identity, bias=bias, scale=gain, w=[k] + list(w_dst))
            else:
                eng = self.act if q % 2 else self.dve
                k = eng.act(d, a, ACT.Copy, w=[k] + list(w_dst)) if eng is self.act else eng.cp(d, a, w=[k] + list(w_dst))
            self.banks.give(i, k)
            out.append(k)
        return out

    def xT_tile(self, t):
        return self.xT[:, t // 2, 1 + 128 * (t % 2):129 + 128 * (t % 2)]

    def logits(self, tileT, weight, bias, out, w):
        n = weight.shape[1]
        i, ps, wb = self.banks.take()
        for t in range(NT):
            k = self.pe.mm(ps[:, t * n:(t + 1) * n], tileT(t), weight, w=list(w) + wb, inc=(t == NT - 1))
        k = self.dve.tt(out, ps[:, 0:NT * n].rearrange("p (t n) -> p t n", n=n), grow(bias, NT), ALU.add, w=[k])
        self.banks.give(i, k)
        return k

    def preset(self, func):
        one = self.scrap[:, 0:1]
        return self.act.act(one, one, func, w=[self.act.now()])

    def top2(self, lg, w):
        d = self.dve
        io = grow(self.c["iota8"], NT)
        m = [self.v[6][:, :], self.v[7][:, :]]
        oh = [self.k8[1], self.k8[2]]
        u, low, l2 = self.k8[3][:, :, :], self.v[8][:, :], self.k8[4][:, :, :]
        cur, k = lg, None
        for n in range(2):
            k = d.red(m[n], cur, ALU.max, w=list(w) if k is None else [k])
            k = d.tt(u, cur, grow_in(m[n], E), ALU.is_equal, w=[k])
            k = d.stt(u, u, -8.0, io, ALU.mult, ALU.add, w=[k])
            k = d.red(low, u, ALU.min, w=[k])
            k = d.tt(oh[n][:, :, :], u, grow_in(low, E), ALU.is_equal, w=[k])
            if n == 0:
                k = d.stt(l2, oh[0][:, :, :], -3.0e38, lg, ALU.mult, ALU.add, w=[k])
                cur = l2
        return oh, m, k

    def prefix(self, a, out, incl, w):
        d = self.dve
        i, ps, wb = self.banks.take()
        flat = a[:, :, :].rearrange("p t e -> p (t e)")
        self.pe.mm(ps[:, 0:128], self.c["before"], flat, w=list(w) + wb, inc=False)
        k = self.pe.mm(ps[:, 128:256], self.c["ones"], flat)
        tot = self.k8[5][:, :, :].rearrange("p t e -> p (t e)")
        tot3 = tot.rearrange("p (e t) -> p e t", t=NT)
        k = d.cp(tot3, ps[:, 128:256].rearrange("p (t e) -> p e t", e=E), w=[k])
        k = d.put(lambda: d.eng.tensor_tensor_scan(incl, self.c["scan_mask"], tot, 0.0, ALU.mult, ALU.add), [k])
        k = d.tt(tot, incl, tot, ALU.subtract, w=[k])
        k = d.tt(out, ps[:, 0:128].rearrange("p (t e) -> p t e", e=E),
                 tot.rearrange("p (e t) -> p t e", t=NT), ALU.add, w=[k])
        self.banks.give(i, k)
        return k

    def place(self, oh, D, out, w):
        d = self.dve
        u = self.k8[3][:, :, :]
        k = d.tt(u, oh, D, ALU.mult, w=w)
        return d.red(out, u, ALU.add, w=[k])

    def slots(self, ohs, w):
        d = self.dve
        a, k = ohs[0], None
        if len(ohs) == 2:
            a = self.k8[4]
            k = d.tt(a[:, :, :], ohs[0][:, :, :], ohs[1][:, :, :], ALU.add, w=w)
        D, incl = self.k8[6], self.k8[7][:, :, :].rearrange("p t e -> p (t e)")
        k = self.prefix(a, D[:, :, :], incl, list(w) + [k])
        cnt = incl.rearrange("p (e t) -> p e t", t=NT)[:, :, NT - 1]
        rounded, end, base = (self.e8[i][:, :] for i in range(3))
        k = d.ts(self.ei[:, :], cnt, 127.0, op0=ALU.add, w=[k])
        k = d.ts(self.ei[:, :], self.ei[:, :], 7, 7, ALU.logical_shift_right, ALU.logical_shift_left, w=[k])
        k = d.cp(rounded, self.ei[:, :], w=[k])
        k = d.put(lambda: d.eng.tensor_tensor_scan(end, self.c["ones"][:, 0:E], rounded, 0.0, ALU.mult, ALU.add), [k])
        k = d.tt(base, end, rounded, ALU.subtract, w=[k])
        kd = d.tt(D[:, :, :], D[:, :, :], grow(base, NT), ALU.add, w=[k])
        tf = self.tile_f[:, :, :]
        k = d.tt(tf, end[0:1, :].unsqueeze(1).broadcast_to((1, TILES, E)),
                 self.c["tile_start"][0:1, :].unsqueeze(2).broadcast_to((1, TILES, E)), ALU.is_le, w=[k])
        k = d.red(self.tile_n[:, :], tf, ALU.add, w=[k])
        k = d.ts(self.tile_n[:, :], self.tile_n[:, :], float(E - 1), op0=ALU.min, w=[k])
        kt = self.by_eights(self.tile_n[:, :], [k])
        for n, oh in enumerate(ohs):
            k = self.place(oh[:, :, :], D[:, :, :], self.v[9][:, :], [kd, kt])
            k = d.ts(self.idx[:, n, :], self.v[9][:, :], float(LEAD * P), op0=ALU.add, w=[k])
        return k, kt

    def by_eights(self, experts, w):
        d = self.dve
        v = self.tile_f[:, :, 0].rearrange("o (g u) -> o g u", u=4)
        k = d.tt(v, experts.rearrange("o (g u) -> o g u", u=4),
                 self.c["octal"][0:1, :].unsqueeze(1).broadcast_to((1, TILES // 4, 4)), ALU.mult, w=w)
        total = self.tile_f[:, 0:TILES // 4, 1]
        k = d.red(total, v, ALU.add, w=[k])
        return d.stt(self.eight[:, :], total[:, 1:], 4096.0, total[:, 0:TILES // 4 - 1], ALU.mult, ALU.add, w=[k])

    def experts(self, xs, ys, ntile, w, mid, func, F, NF, wa, wb_, b1=None, b2=None, yscale=1.0, mid_end=None):
        pe, d, act, sp = self.pe, self.dve, self.act, self.sp
        R = self.R
        steps = self.steps = Steps(self.p)
        since, did = steps.since, steps.did
        pe.wait([t for f in self.banks.free for t in f])
        for e in self.p.engines:
            e.wait(w)

        def bank(i, n=512):
            return self.banks.ps[:, i * 512:i * 512 + n]

        def rows_in(n, u):
            did(f"in{u}", act.dma(self.hs[u], xs[bass.ds((n + LEAD) * P, P), :], self.ch_in[u], w=[since(f"tr{u}")]))

        def turn(u):
            ps = bank(u % 2, 128)
            k = did(f"tr{u}", pe.tr(ps, self.hs[u], self.c["ident"], w=[since(f"in{u}"), since(f"hT{(u - 2) % R}")]))
            did(f"hT{u}", act.act(self.hT[u], ps, ACT.Copy, w=[k, since(f"m1{u}")]))

        def product1(u, ex_pe, ex_dve):
            ps = bank(2 + u, F)
            k = did(f"m1{u}", pe.mm(ps, self.hT[u], wa[:, bass.ds(ex_pe * F, F)], w=[since(f"hT{u}"), since(f"aT{u}")]))
            did(f"mid{u}", mid(self, u, ps, ex_dve, k, lambda n: since(f"{n}{u}")))

        def end_mid(u):
            k = since(f"mid{u}")
            did(f"a{u}", k if mid_end is None else mid_end(self, u, bank(2 + u, F), k, lambda n: since(f"{n}{u}")))

        def turn_mid(u):
            ps = bank(2 + u, 128 * NF)
            for f in range(NF):
                k = pe.tr(ps[:, 128 * f:128 * f + 128], self.ha[u][:, f * 128:(f + 1) * 128], self.c["ident"],
                          w=[since(f"a{u}")], inc=(f == NF - 1))
            did(f"trm{u}", k)
            dst, w = self.aT[u][:, 0:128 * NF], [k, since(f"m2{u}")]
            on_act = NF == 2 or (NF == 4 and u % 2)
            did(f"aT{u}", act.act(dst, ps, ACT.Copy, w=w) if on_act else d.cp(dst, ps, w=w))

        def product2(n, u, ex_pe, ex_dve):
            ps = bank(6 + u % 2, 128)
            for f in range(NF):
                k = pe.mm(ps, self.aT[u][:, f * 128:(f + 1) * 128], wb_[:, bass.ds(ex_pe * (128 * NF) + 128 * f, 128)],
                          first=(f == 0), last=(f == NF - 1), w=[since(f"aT{u}"), since(f"y{(u - 2) % R}")])
            did(f"m2{u}", k)
            d.wait([k, since(f"out{u}")])
            if b2 is None:
                k = d.cp(self.y[u], ps)
            else:
                k = d.stt(self.y[u], ps, yscale, b2[:, bass.ds(ex_dve * C, C)], ALU.mult, ALU.add)
            did(f"y{u}", k)
            did(f"out{u}", sp.dma(ys[bass.ds(n * P, P), :], self.y[u], self.ch_out[u], w=[k]))

        def body(i, lp):
            steps.last.clear()
            ex = {}
            for eng in (pe, d) if b2 is not None else (pe,):
                v = 0 if self.p.dry else eng.eng.value_load(self.eight[0:1, bass.ds(i, 1)], min_val=0, max_val=8 ** 8 - 1)
                for u in range(-R, R):
                    ex[eng, u] = (v >> (3 * (u + R))) & 7
            for u in range(R):
                for (eng, tile), e in ex.items():
                    if tile in (u, u - R) and not self.p.dry:
                        eng.eng.compute_val(e)
                end_mid((u - 2) % R)
                turn_mid((u - 3) % R)
                turn((u + 1) % R)
                rows_in(i * R + u + 1 + R, (u + 1) % R)
                product2(i * R + u, u, ex[pe, u - 4], ex.get((d, u - 4)))
                product1(u, ex[pe, u], ex.get((d, u)))

        for u in range(R):
            rows_in(u, u)
        turn(0)
        rows_in(R, 0)
        self.preset(func)
        self.p.run_loop(ntile // R + 1, body)
        act.wait([Token(c, c.n, None) for c in self.ch_in])
        done = [self.dve.now(), self.preset(func)]
        self.banks.free = [list(done) for _ in range(8)]
        return [Token(c, c.n, None) for c in self.ch_out]

    def dispatch(self, rows, xs, n, filled, w, limit=None):
        self.n_sent = self.n_sent + 1
        ch = self.p.channel(f"ch_sent{self.n_sent}", self.pool)
        self.pool.wait(list(w) + list(filled))
        for t in range(NT):
            for j in range(n):
                k = self.pool.scatter_rows(xs[:, :], self.idx[:, j, t:t + 1], rows[:, t, :], ch, limit)
        return k

    def collect(self, outs, ys, idxs, w, chs=None):
        got = []
        for t in range(NT):
            for o, j in zip(outs, idxs):
                k = self.pool.gather_rows(o[:, t, :], ys[:, :], self.idx[:, j, t:t + 1], (chs or self.ch_got)[t], w=w)
            got.append(k)
        return got

    def clear_rows(self, xs, ntile):
        ch = self.p.channel(f"ch_zero{self.p.n_sb}", self.sp)
        self.p.n_sb += 1
        return self.sp.dma(xs[0:ntile * P, :].rearrange("(t p) c -> p t c", p=P),
                           self.zero[:, :].unsqueeze(1).broadcast_to((P, ntile, C)), ch, [self.k_zero])

    def start(self):
        sp, d, pool = self.sp, self.dve, self.pool
        quarter = lambda q: self.ins["x"].rearrange("(t p) c -> p t c", p=P)[:, 4 * q:4 * q + 4, :]
        k_in = [sp.dma(self.x[:, 4 * q:4 * q + 4, :], quarter(q), self.p.channel(f"ch_x{q}", sp)) for q in range(4)]
        self.k_x = lambda t: [k_in[t // 4]]
        self.k_c = self.load(sp, self.c, "consts")
        self.k_w0 = [self.load(sp, self.w0, "w0"), self.load(sp, self.r0, "r0", rows=True)]
        self.n_sent, self.lane_done = 0, {}
        self.zero = self.p.sbuf("zero", [P, C])
        self.k_zero = pool.fill(self.zero[:, :], 0.0)
        pool.fill(self.scrap[:, :], 0.0)
        d.fill(self.joint[:, :], 0.0)
        self.k_edge = pool.fill(self.xT[:, :, :], 0.0)
        dt = self.nc.dram_tensor
        self.xs = [dt(f"xs{n}", ((t + 3 * LEAD + 1) * P, C), F32, kind="Internal").ap() for n, t in enumerate((24, 24, 40, 40))]
        self.ys = [dt(f"ys{n}", ((t + LEAD) * P, C), F32, kind="Internal").ap() for n, t in enumerate((24, 24, 40, 40))]
        self.k_clear = [self.clear_rows(x, t + 3 * LEAD + 1) for x, t in zip(self.xs, (24, 24, 40, 40))]
        self.k_w1 = [self.load(sp, self.w1, "w1"), self.load(sp, self.r1, "r1", rows=True)]
        self.k_w2 = [self.load(sp, self.w2, "w2"), self.load(sp, self.r2, "r2", rows=True)]

    def normed(self, turned=True):
        k = self.layernorm(self.x, self.xn, self.k_x)
        self.k_xn = k
        if not turned:
            return k
        self.k_xT = self.transposed(self.xn, lambda q: self.xT[:, 2 * q:2 * q + 2, 1:1 + NS], [k, self.k_c],
                                    w_dst=[self.k_edge, self.pe.now()])
        return k

    def gated(self, s, w):
        k = self.act.act(self.g[:, :, :], self.g[:, :, :], ACT.Silu, w=w)

        def add(e, a, b):
            k1 = e.tt(self.g[:, a:b, :], self.g[:, a:b, :], s[:, a:b, :], ALU.mult, w=[k] + list(w))
            return e.tt(self.x[:, a:b, :], self.x[:, a:b, :], self.g[:, a:b, :], ALU.add, w=[k1])

        kd, kp = add(self.dve, 0, 11), add(self.pool, 11, NT)
        self.k_x = lambda t: [kd if t < 11 else kp]

    def layer0_linear(self, j, ar, br):
        pe, d, act, pool, c, w0 = self.pe, self.dve, self.act, self.pool, self.c, self.w0
        e, r = ar[:, 0:512], ar[:, 512:1024]
        ue = [ar[:, 1024:1536], ar[:, 1536:2048]]
        t1 = br[:, 0:512]
        ro = [br[:, 512:1024], br[:, 1024:1536]]
        kt = br[:, 1536:1792].rearrange("p (r c) -> p r c", c=C)
        kvm, mz, zz = br[:, 1792:1920], br[:, 1920:1928], br[:, 1928:1936]
        km = self.v[11]
        last = self.lin_last
        two = lambda a: a.rearrange("p (b n) -> p b n", n=NS)
        X = self.xT[:, 2 * j:2 * j + 2, 1:1 + NS]
        kin = [self.k_xT[j]] + self.k_w0
        for n, (w, b) in enumerate((("q", "q_b"), ("k", "k_b"))):
            i, ps, wb = self.banks.take()
            k = pe.mm(ps, w0[w], X, w=kin + wb)
            yield
            ke = act.act(e, ps, ACT.Exp, bias=w0[b], w=[k, last.get("u")])
            kr = act.act(r, ps, ACT.Relu, bias=w0[b], w=[k, last.get("u")])
            self.banks.give(i, kr)
            yield
            for h in range(2):
                sl = slice(h * NS, (h + 1) * NS)
                k = d.stt(ue[n][:, sl], e[:, sl], 1.0, r[:, sl], ALU.min, ALU.add,
                          w=[ke, kr, last.get("o")], acc=km[:, h:h + 1] if n else None)
            last["u"] = ku = k
            last["u", n] = ku
            i, ps, wb = self.banks.take()
            k = pe.mm(ps, c["swap"], ue[n], w=[ku] + wb)
            k1 = pool.tt(two(t1), two(ue[n]), grow(c["rope_cos"], 2), ALU.mult, w=[ku, last.get("t1"), self.k_c])
            yield
            k2 = d.tt(two(ro[n]), two(ps), grow(c["rope_sin"], 2), ALU.mult, w=[k, last.get("o")])
            self.banks.give(i, k2)
            last["t1"] = k = d.tt(ro[n], ro[n], t1, ALU.add, w=[k1, k2])
            last["r", n] = k
        for h in range(2):
            i, ps, wb = self.banks.take()
            for q in range(2):
                k = pe.tr(ps[:, q * 128:(q + 1) * 128], ro[1][:, (2 * h + q) * 128:(2 * h + q + 1) * 128],
                          c["ident"], w=[last["r", 1]] + wb)
            yield
            k = act.act(kt[:, 0:2, :], ps[:, 0:256].rearrange("p (r c) -> p r c", c=C), ACT.Copy,
                        w=[k, last.get("kv")])
            self.banks.give(i, k)
            yield
            i, ps, wb = self.banks.take()
            for q in range(2):
                kk = pe.mm(ps[:, 0:128], kt[:, q, :], self.xn[:, 4 * j + 2 * h + q, :], first=(q == 0),
                           last=(q == 1), w=[k, self.k_xn] + wb)
            last["kv"] = kk
            yield
            k = d.tt(kvm, ps[:, 0:128], c["kv_mask"], ALU.mult, w=[kk, last.get("o")])
            self.banks.give(i, k)
            kz = d.ts(mz, c["heads"], km[:, h:h + 1], w=[last["u", 1], last.get("o")])
            yield
            outs = []
            for q in range(2):
                sl = slice((2 * h + q) * 128, (2 * h + q + 1) * 128)
                i, ps, wb = self.banks.take()
                pe.mm(ps[:, 0:128], ro[0][:, sl], kvm, w=[k, last["r", 0]] + wb)
                pe.mm(ps[:, 128:136], ue[0][:, sl], mz, w=[kz])
                for m in range(3):
                    b = 2 * j + h
                    kk = pe.mm(ps[:, 256:384], self.xT[:, b, m + 128 * q:m + 128 * q + 128],
                               w0["lepe"][:, m * 128:(m + 1) * 128], first=(m == 0), last=(m == 2))
                last["o"] = kk
                outs.append((i, ps, kk))
            yield
            for q, (i, ps, kk) in enumerate(outs):
                k1 = d.ts(zz, ps[:, 128:136], 1e-6, op0=ALU.add, w=[kk, last.get("zz")])
                k1 = d.rcp(zz, zz, w=[k1])
                st = self.s[:, 4 * j + 2 * h + q, :]
                k1 = last["zz"] = d.tt(st.rearrange("p (h e) -> p h e", e=16), ps[:, 0:128].rearrange("p (h e) -> p h e", e=16),
                                       grow_in(zz, 16), ALU.mult, w=[k1])
                k1 = d.tt(st, st, ps[:, 256:384], ALU.add, w=[k1])
                self.banks.give(i, k1)
        q4 = self.s[:, 4 * j:4 * j + 4, :]
        self.k_lin = d.tt(q4, q4, grow(self.r0["lepe_b"], 4), ALU.add, w=[k1])

    def layer0_attention(self):
        pe, d, act, pool, c = self.pe, self.dve, self.act, self.pool, self.c
        qkv = self.qkv
        kq = [None, None]

        def project(t):
            i, ps, wb = self.banks.take()
            k = pe.mm(ps[:, 0:384], self.xT_tile(t), self.w0["qkv"], w=self.k_w0 + self.k_xT + wb)
            yield
            kq[t % 2] = d.tt(qkv[:, t, :], ps[:, 0:384], self.r0["qkv_b"], ALU.add, w=[k])
            self.banks.give(i, kq[t % 2])

        for t in range(0, NT, 2):
            yield from project(t)
        prods = [self.arena[:, 1024 * n:1024 * n + 1024] for n in range(3)]
        sc = self.arena[:, 3072:4096]
        mx, sm = self.arena[:, 4096:4224], self.arena[:, 4224:4352]
        ctx = self.t2
        read, k_sc = {}, None

        def rows(part, h):
            return qkv[:, :, :].rearrange("p (s h) c -> p h s c", h=2)[:, h, :, part * 128:(part + 1) * 128]

        def pipelined(product, reduce, on_pool, extra=()):
            made = {}
            for t in range(8 + 2):
                if t < 8:
                    made[t] = product(t, pool if t in on_pool else d, prods[t % 3], read.get(t % 3))
                if t >= 2:
                    read[(t - 2) % 3] = reduce(t - 2, prods[(t - 2) % 3], made[t - 2])
                if t < len(extra):
                    yield from extra[t]
                yield
            return read[7 % 3]

        for h in range(2):
            def score_product(t, eng, buf, old):
                return eng.tt(buf.rearrange("p (s c) -> p s c", c=C), rows(1, h), grow(qkv[:, 2 * t + h, 0:128], 8),
                              ALU.mult, w=[kq[h], old])

            def score_sum(t, buf, k):
                return d.red(sc[:, t * 128:(t + 1) * 128], buf.rearrange("p (a x) -> p a x", x=8), ALU.add, w=[k, k_sc])

            k = yield from pipelined(score_product, score_sum, (1, 3, 5, 7), [] if h else [project(t) for t in range(1, NT, 2)])
            ths = sc.rearrange("p (t s h) -> p t h s", s=8, h=16)
            th = lambda a: a.rearrange("p (t h) -> p t h", h=16)
            k = d.red(th(mx), ths, ALU.max, w=[k])
            tsh = sc.rearrange("p (t s h) -> p t s h", s=8, h=16)
            bc = lambda a: th(a).unsqueeze(2).broadcast_to((P, 8, 8, 16))
            k = d.tt(tsh, tsh, bc(mx), ALU.subtract, w=[k])
            k = act.act(sc, sc, ACT.Exp, scale=float(np.float32(8.0) ** np.float32(-0.5)), w=[k])
            yield
            k = d.red(th(sm), ths, ALU.add, w=[k])
            k = d.rcp(sm, sm, w=[k])
            ks = d.tt(tsh, tsh, bc(sm), ALU.mult, w=[k])
            yield

            def value_product(t, eng, buf, old):
                pr = buf.rearrange("p (h x s) -> p h x s", h=16, x=8)
                pt = sc[:, t * 128:(t + 1) * 128].rearrange("p (s h) -> p h s", h=16).unsqueeze(2).broadcast_to((P, 16, 8, 8))
                return eng.tt(pr, pt, rows(2, h).rearrange("p s (h x) -> p h x s", h=16), ALU.mult, w=[ks, old])

            def value_sum(t, buf, k):
                return d.red(ctx[:, 2 * t + h, :], buf.rearrange("p (c s) -> p c s", s=8), ALU.add, w=[k])

            k = k_sc = yield from pipelined(value_product, value_sum, (1, 3, 5, 7))
        self.k_ctx = k

    def layer0_attention_out(self):
        pe, d = self.pe, self.dve
        kT = self.transposed(self.t2, lambda q: self.tT[:, q * 512:(q + 1) * 512], [self.k_ctx],
                             w_dst=[pe.now(), d.now(), self.pool.now()])
        for t in range(NT):
            i, ps, wb = self.banks.take()
            k = pe.mm(ps[:, 0:128], self.tT[:, t * 128:(t + 1) * 128], self.w0["out"], w=kT + wb)
            k = d.tt(self.t1[:, t, :], ps[:, 0:128], self.xn[:, t, :], ALU.add, w=[k])
            self.banks.give(i, k)
        return d.tt(self.t1[:, :, :], self.t1[:, :, :], grow(self.r0["out_b"], NT), ALU.add, w=[k])

    def mid_gelu(self, F, b1):
        def mid(net, u, ps, ex, k, since):
            d = net.dve
            d.wait([k, since("a")])
            k = d.put(lambda: d.eng.tensor_tensor(net.hm[u][:, 0:F], ps, b1[:, bass.ds(ex * F, F)], ALU.add))
            return net.act.act(net.ha[u][:, 0:F], net.hm[u][:, 0:F], ACT.Gelu, w=[k, since("trm")])
        return mid

    def layer0_mixture(self, k_in):
        d, r0, w0 = self.dve, self.r0, self.w0
        h = self.t1
        k = self.layernorm(self.t1, h, lambda t: [k_in], r0["ln1_g"], r0["ln1_b"])
        kT = self.transposed(h, lambda q: self.tT[:, q * 512:(q + 1) * 512], [k], w_dst=[self.pe.now()])
        lg = self.k8[0][:, :, :]
        k = self.logits(lambda t: self.tT[:, t * 128:(t + 1) * 128], w0["router"], r0["router_b"], lg, kT)
        oh, m, k = self.top2(lg, [k])
        i1, i2 = self.v[6][:, :], self.v[7][:, :]
        io = grow(self.c["iota8"], NT)
        k = self.place(oh[0][:, :, :], io, i1, [k])
        k = self.place(oh[1][:, :, :], io, i2, [k])
        k = d.tt(i1, i1, i2, ALU.max, w=[k])
        k = d.tt(oh[0][:, :, :], io, grow_in(i1, E), ALU.is_equal, w=[k])
        k, kt = self.slots([oh[0]], [k])
        kd = self.dispatch(h, self.xs[0], 1, [self.k_clear[0]], [k])
        ko = self.experts(self.xs[0], self.ys[0], 24, [kd] + [e.now() for e in (self.pe, d, self.act)],
                          self.mid_gelu(C, r0["b1"]), ACT.Gelu, C, 1,
                          w0["w1"], w0["w2"], r0["b1"], r0["b2"])
        kc = self.collect([self.t2], self.ys[0], [0], ko + [d.now()])

        def summed(t):
            return [d.tt(self.t1[:, t, :], self.t1[:, t, :], self.t2[:, t, :], ALU.add, w=[kc[t]])]

        return self.layernorm(self.t1, self.g, summed, r0["ln2_g"], r0["ln2_b"])

    def layer0(self):
        self.normed()
        self.lin_last = {}
        t1 = self.t1[:, :, :].rearrange("p t c -> p (t c)")
        weave([self.layer0_attention()], [self.layer0_linear(j, self.tT, t1) for j in range(4)])
        k = self.layer0_attention_out()
        k = self.layer0_mixture(k)
        return self.gated(self.s, [k, self.k_lin])

    def layer1_attention(self):
        pe, d, act, pool, w1 = self.pe, self.dve, self.act, self.pool, self.w1
        start = [e.now() for e in (pe, d, act, pool)]
        k = self.layernorm(self.xn, self.t1, lambda t: [self.k_xn])
        kT = self.transposed(self.t1, lambda q: self.tT[:, q * 512:(q + 1) * 512], [k] + self.k_w1,
                             gain=w1["ln_g"], bias=w1["ln_b"], w_dst=[pe.now()])
        for e in (d, act, pool):
            e.wait(start)
        return lambda b, lane: self.layer1_batch(b, lane, kT)

    def layer1_batch(self, b, lane, kT):
        pe, d, act, w1, r1 = self.pe, self.dve, self.act, self.w1, self.r1
        wk = self.work[:, 3328 * lane:3328 * lane + 3328]
        hb = wk[:, 0:1024].rearrange("p (r n) -> p r n", n=512)
        qk, qT, kk_ = wk[:, 1024:1280], wk[:, 1280:1536], wk[:, 1536:1792]
        a, og, ogT = wk[:, 1792:2304], wk[:, 2304:2816], wk[:, 2816:3328]
        old = self.lane_done.get(lane, [])
        for r in range(2):
            t = 2 * b + r
            i, ps, wb = self.banks.take()
            k = pe.mm(ps, self.tT[:, t * 128:(t + 1) * 128], w1["hidden"], w=kT + wb)
            k = d.tt(hb[:, r, :], ps, r1["hidden_b"], ALU.add, w=[k] + old)
            self.banks.give(i, k)
        i, ps, wb = self.banks.take()
        kp = pe.mm(ps[:, 0:NS], w1["qk"], self.tT[:, b * NS:(b + 1) * NS], w=kT + wb)
        yield
        k = act.act(qk, ps[:, 0:NS], ACT.Silu, bias=w1["qk_b"], w=[kp] + old)
        self.banks.give(i, k)
        kh = act.act(hb, hb, ACT.Silu, w=[d.now()])
        kq = d.ts(qT, qk, w1["osw"][:, 0:1], w1["osb"][:, 0:1], ALU.mult, ALU.add, w=[k] + old)
        kkk = d.ts(kk_, qk, w1["osw"][:, 1:2], w1["osb"][:, 1:2], ALU.mult, ALU.add, w=[k])
        yield
        i, ps, wb = self.banks.take()
        for r in range(2):
            k = pe.mm(ps[:, r * NS:(r + 1) * NS], kk_[:, r * 128:(r + 1) * 128], qT, w=[kq, kkk] + wb)
        yield
        k = act.act(a, ps, ACT.Relu, scale=1.0 / NS, w=[k] + old)
        self.banks.give(i, k)
        ka = d.tt(a, a, a, ALU.mult, w=[k])
        yield
        for r in range(2):
            i, ps, wb = self.banks.take()
            for j in range(2):
                k = pe.mm(ps[:, 0:256], a[:, j * NS + r * 128:j * NS + r * 128 + 128], hb[:, j, 0:256],
                          first=(j == 0), last=(j == 1), w=[ka, kh] + wb)
            k = d.tt(og[:, r * 256:(r + 1) * 256], ps[:, 0:256], hb[:, r, 256:512], ALU.mult, w=[k] + old)
            self.banks.give(i, k)
        yield
        i, ps, wb = self.banks.take()
        for r in range(4):
            kt = pe.tr(ps[:, r * 128:(r + 1) * 128], og[:, r * 128:(r + 1) * 128], self.c["ident"], w=[k] + wb, inc=(r == 3))
        yield
        k = act.act(ogT, ps, ACT.Copy, w=[kt] + old)
        self.banks.give(i, k)
        yield
        i, ps, wb = self.banks.take()
        for r in range(2):
            for f in range(2):
                kk = pe.mm(ps[:, r * 128:(r + 1) * 128], ogT[:, (2 * r + f) * 128:(2 * r + f + 1) * 128],
                           w1["out"][:, f * 128:(f + 1) * 128], first=(f == 0), last=(f == 1), w=[k] + wb)
        yield
        k = d.tt(self.s[:, 2 * b:2 * b + 2, :], ps[:, 0:256].rearrange("p (r c) -> p r c", c=C), grow(r1["out_b"], 2), ALU.add,
                 w=[kk])
        self.banks.give(i, k)
        self.lane_done[lane] = [kk, k]

    def pair_softmax(self, m, w1, w2, w):
        d, t = self.dve, self.v[9][:, :]
        k = d.tt(t, m[1], m[0], ALU.subtract, w=w)
        k = self.act.act(t, t, ACT.Exp, w=[k])
        k = d.ts(w1, t, 1.0, op0=ALU.add, w=[k])
        k = d.rcp(w1, w1, w=[k])
        return d.tt(w2, t, w1, ALU.mult, w=[k])

    def layer1_slots(self):
        d, pe, c = self.dve, self.pe, self.c
        CAP = (TOK * 5 + 4 * E - 1) // (4 * E)
        lg = self.k8[0][:, :, :]
        k = self.logits(self.xT_tile, self.w1["router"], self.r1["router_b"], lg, self.k_xT + self.k_w1)
        yield
        oh, m, k = self.top2(lg, [k])
        yield
        g = [self.gates[:, 0, :], self.gates[:, 1, :]]
        k = self.pair_softmax(m, g[0], g[1], [k])
        yield
        val, u = self.k8[0][:, :, :], self.k8[3][:, :, :]
        k1 = d.tt(val, oh[0][:, :, :], grow_in(g[0], E), ALU.mult, w=[k])
        k2 = d.tt(u, oh[1][:, :, :], grow_in(g[1], E), ALU.mult, w=[k])
        k = d.tt(val, val, u, ALU.add, w=[k1, k2])
        thr, spare = self.ei, self.work[:, 9984:10496]
        reach = spare[:, 0:3 * NT * E]
        cand, part, hit, step = (spare[:, 384 + 24 * n:408 + 24 * n] for n in range(4))
        cand_i, step_i = cand.bitcast(I32), spare[:, 480:488].bitcast(I32)
        step = step[:, 0:E]
        by = lambda a: a.rearrange("p (m e) -> p m e", e=E)
        quarters = self.p.sbuf("quarters", [P, 45], I32)
        k = d.cp(quarters[:, :], c["quarters"], w=[k])
        k = d.fill(thr[:, :], 0, w=[k])
        for s in range(15):
            k = d.tt(by(cand_i), grow(thr[:, :], 3), grow_in(quarters[:, 3 * s:3 * s + 3], E), ALU.bitwise_or, w=[k])
            k = d.tt(reach.rearrange("p (m t e) -> p m t e", m=3, e=E), val.unsqueeze(1).broadcast_to((P, 3, NT, E)),
                     by(cand).unsqueeze(2).broadcast_to((P, 3, NT, E)), ALU.is_ge, w=[k])
            k = d.red(by(part), reach.rearrange("p (m t e) -> p m e t", m=3, e=E), ALU.add, w=[k])
            yield
            i0, ps, wb = self.banks.take()
            k = pe.mm(ps[:, 0:24], c["ones"], part, w=[k] + wb)
            yield
            k = d.ts(hit, ps[:, 0:24], float(CAP), c["quarters"][:, 3 * s:3 * s + 1], ALU.is_ge, ALU.mult, w=[k])
            self.banks.give(i0, k)
            k = d.red(step, hit.rearrange("p (m e) -> p e m", e=E), ALU.add, w=[k])
            k = d.cp(step_i, step, w=[k])
            k = d.tt(thr[:, :], thr[:, :], step_i, ALU.bitwise_or, w=[k])
        part, part2 = self.e8[0][:, :], self.e8[1][:, :]
        over, tie, both = self.k8[4], self.p.sbuf("tie", [P, NT, E]), self.p.sbuf("chosen", [P, NT, E])
        tb = grow(thr[:, :].bitcast(F32), NT)
        k1 = d.tt(over[:, :, :], val, tb, ALU.is_gt, w=[k])
        k2 = d.tt(both[:, :, :], oh[0][:, :, :], oh[1][:, :, :], ALU.add, w=[k])
        k3 = d.tt(tie[:, :, :], val, tb, ALU.is_equal, w=[k])
        k3 = d.tt(tie[:, :, :], tie[:, :, :], both[:, :, :], ALU.mult, w=[k2, k3])
        k1 = d.red(part, over[:, :, :].rearrange("p t e -> p e t"), ALU.add, w=[k1])
        i0, ps, wb = self.banks.take()
        k1 = pe.mm(ps[:, 0:E], c["ones"], part, w=[k1] + wb)
        yield
        k1 = d.ts(part2, ps[:, 0:E], -1.0, float(CAP), ALU.mult, ALU.add, w=[k1])
        self.banks.give(i0, k1)
        rank, incl = self.k8[6], self.k8[7][:, :, :].rearrange("p t e -> p (t e)")
        k = self.prefix(tie, rank[:, :, :], incl, [k3, k1])
        k = d.tt(u, rank[:, :, :], grow(part2, NT), ALU.is_lt, w=[k])
        k = d.tt(u, u, tie[:, :, :], ALU.mult, w=[k])
        k = d.tt(over[:, :, :], over[:, :, :], u, ALU.add, w=[k])
        yield
        k = self.prefix(over, rank[:, :, :], incl, [k])
        k = d.tt(rank[:, :, :], rank[:, :, :], grow(c["iota384"], NT), ALU.add, w=[k])
        took, slot, t = self.v[8][:, :], self.v[9][:, :], self.v[0][:, :]
        for n in range(2):
            k = self.place(oh[n][:, :, :], over[:, :, :], took, [k])
            k = self.place(oh[n][:, :, :], rank[:, :, :], slot, [k])
            k = d.tt(t, slot, took, ALU.mult, w=[k])
            k = d.ts(self.idx[:, 2 + n, :], t, float(LEAD * P), op0=ALU.add, w=[k])
            k = d.ts(slot, took, -65536.0, 65536.0, ALU.mult, ALU.add, w=[k])
            k = d.tt(t, t, slot, ALU.add, w=[k])
            k = d.ts(self.idx[:, n, :], t, float(LEAD * P), op0=ALU.add, w=[k])
            k = d.tt(g[n], g[n], took, ALU.mult, w=[k])
            yield
        kt = self.by_eights(c["tile_third"][0:1, :], [k])
        self.k_sent = self.dispatch(self.xn, self.xs[1], 2, [self.k_clear[1]], [k, kt], limit=(24 + LEAD) * P - 1)

    def weighted_tile(self, t, out, ins, got, base):
        d, g = self.dve, [self.gates[:, n, t:t + 1] for n in range(2)]
        if base is None:
            k = d.ts(out[:, t, :], ins[0][:, t, :], g[0], w=[got[t]])
        else:
            k = d.stt(out[:, t, :], ins[0][:, t, :], g[0], base[:, t, :], ALU.mult, ALU.add, w=[got[t]])
        return d.stt(out[:, t, :], ins[1][:, t, :], g[1], out[:, t, :], ALU.mult, ALU.add, w=[k])

    def weighted(self, out, ins, got, base=None, then=None):
        for t in range(NT):
            k = self.weighted_tile(t, out, ins, got, base)
            if then is not None and t % 4 == 3:
                k = then(t // 4, k)
        return k

    def layer1_mixture(self, batch):
        d, r1 = self.dve, self.r1
        ko = self.experts(self.xs[1], self.ys[1], 24, [self.k_sent] + [e.now() for e in (self.pe, d, self.act)], self.mid_gelu(512, r1["b1"]), ACT.Gelu, 512, 4,
                          self.w1["w1"], self.w1["w2"], r1["b1"], r1["b2"])
        done = [d.now(), self.act.now(), self.pe.now()]
        both = [self.t1, self.g]
        kc = self.collect(both, self.ys[1], [2, 3], ko + done)
        self.lane_done = {lane: done for lane in range(2)}
        weave(*[[batch(6 + lane, lane)] for lane in range(2)])
        return self.layernorm(self.t1, self.g, lambda t: [self.weighted_tile(t, self.t1, both, kc, self.xn)],
                              r1["gamma"], r1["beta"])

    def layer1(self):
        self.normed()
        slots = self.layer1_slots()
        next(slots)
        batch = self.layer1_attention()
        weave([slots], [batch(b, 0) for b in (0, 1)], [batch(b, 1) for b in (2, 3)])
        weave(*[[batch(4 + lane, lane)] for lane in range(2)])
        return self.gated(self.s, [self.layer1_mixture(batch)])

    def load_layer3(self):
        w = [e.now() for e in (self.pe, self.dve, self.act, self.pool)] + self.k_w0 + self.k_w1
        self.k_w3 = [self.load(self.sp, self.w3, "w3", w=w), self.load(self.sp, self.r3, "r3", w=w, rows=True)]

    def layer2_attention(self):
        pe, d, w2, c = self.pe, self.dve, self.w2, self.c
        start = [e.now() for e in (pe, d, self.act, self.pool)]
        for e in (d, self.act, self.pool):
            e.wait(start)
        wk = self.work
        i, ps, wb = self.banks.take()
        pe.mm(ps[:, 0:128], w2["wq"], c["rot2"], w=self.k_w2 + wb, inc=False)
        pe.mm(ps[:, 128:256], w2["wk"], c["rot2"], inc=False)
        pe.mm(ps[:, 256:257], c["rot2"], w2["bq"], inc=False)
        k = pe.mm(ps[:, 257:258], c["rot2"], w2["bk"])
        k0 = d.cp(wk[:, 0:258], ps[:, 0:258], w=[k])
        self.banks.give(i, k0)
        self.lane_done = {}
        return lambda b, lane: self.layer2_batch(b, lane, k0)

    def layer2_batch(self, b, lane, k0):
        pe, d, act, w2, r2, c = self.pe, self.dve, self.act, self.w2, self.r2, self.c
        wq, wkk, bq = self.work[:, 0:128], self.work[:, 128:256], self.work[:, 256:258]
        X = self.xT[:, b, 1:1 + NS]
        wk = self.work[:, 512 + 2304 * lane:512 + 2304 * (lane + 1)]
        qT, kT, v = wk[:, 0:256], wk[:, 256:512], wk[:, 512:768]
        pr, pT, st = wk[:, 768:1280], wk[:, 1280:1792], wk[:, 1792:1800]
        old = self.lane_done.get(lane, [])
        for dst, w, bb in ((qT, wq, 0), (kT, wkk, 1)):
            i, ps, wb = self.banks.take()
            k = pe.mm(ps[:, 0:NS], w, X, w=self.k_xT + [k0] + wb)
            k = d.stt(dst, ps[:, 0:NS], bq[:, bb:bb + 1], c["rope2"], ALU.add, ALU.mult, w=[k] + old)
            self.banks.give(i, k)
        kqk = k
        i, ps, wb = self.banks.take()
        for r in range(2):
            k = pe.mm(ps[:, r * 128:(r + 1) * 128], self.xT_tile(2 * b + r), w2["wv"], w=wb)
        kv = d.tt(v.rearrange("p (r c) -> p r c", c=C), ps[:, 0:256].rearrange("p (r c) -> p r c", c=C),
                  grow(r2["bv"], 2), ALU.add, w=[k] + old)
        self.banks.give(i, kv)
        yield
        i, ps, wb = self.banks.take()
        for r in range(2):
            k = pe.mm(ps[:, r * NS:(r + 1) * NS], qT[:, r * 128:(r + 1) * 128], kT, w=[kqk] + wb)
        yield
        k1 = d.red(st[:, 0:2], ps.rearrange("p (r n) -> p r n", n=NS), ALU.max, w=[k] + old)
        k1 = d.ts(st[:, 2:4], st[:, 0:2], -0.125, w=[k1])
        yield
        for r in range(2):
            k = act.act(pr[:, r * NS:(r + 1) * NS], ps[:, r * NS:(r + 1) * NS], ACT.Exp, bias=st[:, 2 + r:3 + r],
                        scale=0.125, acc=st[:, 4 + r:5 + r], w=[k1])
        self.banks.give(i, k)
        yield
        kr = d.rcp(st[:, 6:8], st[:, 4:6], w=[k])
        i, ps, wb = self.banks.take()
        for r in range(2):
            for q in range(2):
                kk = pe.tr(ps[:, r * NS + q * 128:r * NS + (q + 1) * 128], pr[:, q * NS + r * 128:q * NS + (r + 1) * 128],
                           c["ident"], w=[k] + wb, inc=(r + q == 2))
        yield
        k = act.act(pT, ps, ACT.Copy, w=[kk] + old)
        self.banks.give(i, k)
        yield
        i, ps, wb = self.banks.take()
        for q in range(2):
            for r in range(2):
                kk = pe.mm(ps[:, q * 128:(q + 1) * 128], pT[:, r * NS + q * 128:r * NS + (q + 1) * 128],
                           v[:, r * 128:(r + 1) * 128], first=(r == 0), last=(r == 1), w=[k, kv] + wb)
        yield
        for q in range(2):
            k = d.ts(self.s[:, 2 * b + q, :], ps[:, q * 128:(q + 1) * 128], st[:, 6 + q:7 + q], w=[kk, kr])
        self.banks.give(i, k)
        self.lane_done[lane] = [kk, k]

    def layer2_recurrence(self):
        pe, d, act, pool, w2, r2 = self.pe, self.dve, self.act, self.pool, self.w2, self.r2
        wk = self.work
        base = 512 + 3 * 2304
        cc = [wk[:, base:base + 256], wk[:, base + 256:base + 512]]
        f, ig, g = (wk[:, base + 512 + 256 * n:base + 768 + 256 * n] for n in range(3))
        half = wk[:, base + 1280:base + 1282]
        k = d.ts(half[:, 0:1], w2["bf"], 0.5, w=self.k_w2)
        kb = d.ts(half[:, 1:2], w2["bi"], 0.5)
        k = pool.ts(cc[0], w2["c0"].broadcast_to((P, 256)), 1.0, w=self.k_w2)
        gates = ((f, "wf", "uf", half[:, 0:1], 0.5), (ig, "wi", "ui", half[:, 1:2], 0.5), (g, "wc", "uc", w2["bc"], 1.0))
        for t in range(8):
            X = self.xT[:, t, 1:1 + NS]
            c, cn = cc[t % 2], cc[(t + 1) % 2]
            taken, ks = [], []
            for dst, w, u, b, scale in gates:
                i, ps, wb = self.banks.take()
                pe.mm(ps[:, 0:NS], w2[w], X, last=False, w=self.k_xT + wb)
                kk = pe.mm(ps[:, 0:NS], w2[u], c, first=False, w=[k])
                taken.append((i, ps, kk))
            yield
            for (i, ps, kk), (dst, w, u, b, scale) in zip(taken, gates):
                kk = act.act(dst, ps[:, 0:NS], ACT.Tanh, bias=b, scale=scale, w=[kk, k, kb])
                self.banks.give(i, kk)
                ks.append(kk)
            yield
            k1 = d.stt(cn, f, 1.0, c, ALU.add, ALU.mult, w=[ks[0]])
            k2 = d.stt(g, ig, 1.0, g, ALU.add, ALU.mult, w=[ks[2]])
            k = d.tt(cn, cn, g, ALU.add, w=[k1, k2])
            k = d.ts(cn, cn, 0.5, w=[k])
            yield
        cT = cc[0]
        for t in range(NT):
            i, ps, wb = self.banks.take()
            pe.mm(ps[:, 0:128], self.xT_tile(t), w2["wo"], last=False, w=wb)
            kk = pe.mm(ps[:, 0:128], cT[:, 128 * (t % 2):128 * (t % 2) + 128], w2["uo"], first=False, w=[k])
            kk = d.tt(self.g[:, t, :], ps[:, 0:128], r2["bo"], ALU.add, w=[kk])
            self.banks.give(i, kk)
            if t % 2:
                yield
        self.k_g = act.act(self.g[:, :, :], self.g[:, :, :], ACT.Tanh, w=[kk])

    def layer2(self):
        self.normed()
        batch = self.layer2_attention()
        weave([self.layer2_recurrence()], *[[batch(b, lane) for b in range(lane, NB, 3)] for lane in range(3)])
        return self.gated(self.s, [self.k_g, self.dve.now()])

    def layer3_inputs(self):
        pe, d, act, pool, sp, w3 = self.pe, self.dve, self.act, self.pool, self.sp, self.w3
        start = [e.now() for e in (pe, d, act, pool)]
        pool.wait(start)
        wk = self.work
        self.qs = [wk[:, 2048 * n:2048 * n + 2048].bitcast(BF16) for n in range(2)]
        self.ks = [wk[:, 2048 * n:2048 * n + 2048].bitcast(BF16) for n in (2, 3)]
        self.k_fill = [e.fill(x[n], v) for n in range(2) for e, x, v in ((pool, self.ks, 1.0), (pool, self.qs, 0.0))]
        k = self.layernorm(self.xn, self.t1, lambda t: [self.k_xn])
        kT = self.transposed(self.t1, lambda q: self.tT[:, q * 512:(q + 1) * 512], [k] + self.k_w3,
                             gain=w3["ln_g"], bias=w3["ln_b"], w_dst=start)
        self.k_nT = kT
        self.att, self.k_put = Steps(self.p), {}
        self.ch_heads = [[self.p.channel(f"ch_heads{b}{h}", self.sp) for h in range(2)] for b in range(2)]

    def load_heads(self, b, par, half):
        HALF = 8 * NS
        cols = slice(half * HALF, (half + 1) * HALF)
        w = [self.att.since(("pass2", par, half))] + self.k_fill
        for x, side, dst in ((0, PAIRS_Q, self.qs[par]), (1, PAIRS_K, self.ks[par])):
            at = 0
            for n in (3, 2, 1):
                out = dst[8 * at:8 * (at + n), cols]
                first = 8 * side[at]
                if x == 0:
                    src = self.parts[0][first:first + 8, bass.ds(b, 1), cols].rearrange("d b n -> d (b n)")
                    src = src.unsqueeze(0).broadcast_to((n, 8, HALF))
                else:
                    src = self.parts[1][0:8 * n, bass.ds(b, 1), cols].rearrange("d b n -> d (b n)")
                k = self.sp.dma(out, src, self.ch_heads[par][half], w=w)
                at += n
        self.att.did(("load", par, half), k)

    def layer3_parts(self):
        pe, d, act, sp, w3, kT = self.pe, self.dve, self.act, self.sp, self.w3, self.k_nT
        xt, w2s = self.xT[:, :, :].rearrange("p b n -> p (b n)"), self.w2.tensor
        self.parts = [self.nc.dram_tensor(f"{n}_parts", (3 * 8, NB, 16 * NS), BF16, kind="Internal").ap() for n in "qk"]
        three = [a.bitcast(BF16).rearrange("p (q n) -> p q n", q=3) for a in (xt[:, 0:768], xt[:, 768:1536], w2s[:, 0:768])]
        rs = w2s[:, 768:1280]
        ch_put = [self.p.channel(f"ch_parts{n}", sp) for n in range(3)]
        put = self.k_put
        for u in range(8):
            j, x = u // 2, u % 2
            q3 = three[u % 3]
            i, ps, wb = self.banks.take()
            k = pe.mm(ps, w3["qk"[x]], self.tT[:, j * 512:(j + 1) * 512], w=kT + wb)
            yield
            k = act.act(q3[:, 0, :], ps, ACT.Copy, w=[k, put.get(u - 3)])
            yield
            k = d.tt(rs, ps, q3[:, 0, :], ALU.subtract, w=[k, put.get("rest")])
            self.banks.give(i, k)
            yield
            k = act.act(q3[:, 1, :], rs, ACT.Copy, w=[k])
            yield
            k = put["rest"] = d.tt(q3[:, 2, :], rs, q3[:, 1, :], ALU.subtract, w=[k])
            for q in range(3):
                for bb in range(2):
                    dst = self.parts[x][8 * q:8 * q + 8, 2 * j + bb, :].rearrange("d (h n) -> h d n", h=16)
                    put[u] = sp.dma(dst, q3[:, q, bb * NS:(bb + 1) * NS], ch_put[u % 3], w=[k])
            if u == 1:
                sp.wait([put[0], put[1]])
                for b in range(2):
                    for half in range(2):
                        self.load_heads(b, b, half)
        self.k_values = []
        for j in range(4):
            i, ps, wb = self.banks.take()
            for q in range(4):
                t = 4 * j + q
                k = pe.mm(ps[:, q * 128:(q + 1) * 128], self.tT[:, t * 128:(t + 1) * 128], w3["v"], w=wb)
            k = act.act(self.t1[:, 4 * j:4 * j + 4, :], ps.rearrange("p (r c) -> p r c", c=C), ACT.Copy, w=[k])
            self.banks.give(i, k)
            self.k_values.append(k)
            yield

    def layer3_gates(self):
        pe, d, act, pool, w3, r3 = self.pe, self.dve, self.act, self.pool, self.w3, self.r3
        kT = self.k_nT
        tile = lambda t: self.tT[:, t * 128:(t + 1) * 128]
        hl = self.stats[:, :, 0:2]
        k = self.logits(tile, w3["halt"], r3["halt_b"], hl, kT)
        alpha, rem, wsum, h = (self.v[i][:, :] for i in (11, 13, 12, 14))
        self.alpha, self.wsum = alpha, wsum
        ka = act.act(alpha, hl[:, :, 0], ACT.Sigmoid, w=[k])
        for step in range(3):
            if step < 2:
                k = act.act(h, hl[:, :, 1], ACT.Sigmoid, bias=r3["step_b"][:, step:step + 1], w=[k])
                if step == 0:
                    k1 = d.cp(wsum, h, w=[k])
                    k2 = d.ts(rem, h, -1.0, 1.0, ALU.mult, ALU.add, w=[k])
                    k = d.ts(rem, rem, 0.0, op0=ALU.max, w=[k1, k2])
                else:
                    k = d.tt(h, h, rem, ALU.mult, w=[k])
                    k1 = d.tt(wsum, wsum, h, ALU.add, w=[k])
                    k = d.tt(rem, rem, h, ALU.subtract, w=[k1])
                    k = d.ts(rem, rem, 0.0, op0=ALU.max, w=[k])
            else:
                k = d.tt(wsum, wsum, rem, ALU.add, w=[k])
        xp = self.xT[:, :, :].rearrange("p b n -> p (b n)")[:, 1536:2054]
        y, sg, z, xc = (self.work[:, 8192 + 512 * n:8704 + 512 * n] for n in range(4))
        two = lambda a: a.rearrange("p (b n) -> p b n", n=NS)
        kf = pool.fill(xp, 0.0)
        xp = xp.rearrange("p (b n) -> p b n", b=2)
        last = {}
        for j in range(4):
            X = self.tT[:, j * 512:(j + 1) * 512]
            i, ps, wb = self.banks.take()
            k = pe.mm(ps, w3["ssm"][:, 0:128], X, w=kT + wb)
            k = act.act(xp[:, :, 3:3 + NS], two(ps), ACT.Copy, w=[k, kf, last.get("y")])
            self.banks.give(i, k)
            cw = w3["conv_w"]
            yield
            k = d.ts(two(y), xp[:, :, 0:NS], cw[:, 0:1], w3["conv_b"], ALU.mult, ALU.add, w=[k, last.get("sg")])
            for m in range(1, 4):
                k = d.stt(two(y), xp[:, :, m:m + NS], cw[:, m:m + 1], two(y), ALU.mult, ALU.add, w=[k])
            last["y"] = k
            yield
            last["sg"] = k1 = act.act(sg, y, ACT.Sigmoid, w=[k, last.get("xc")])
            i, ps, wb = self.banks.take()
            k = pe.mm(ps, w3["ssm"][:, 128:256], X, w=wb)
            k2 = act.act(z, ps, ACT.Sigmoid, w=[k])
            self.banks.give(i, k2)
            yield
            k = d.tt(xc, y, sg, ALU.mult, w=[k1, last.get("out")])
            k = last["xc"] = d.tt(xc, xc, z, ALU.mult, w=[k, k2])
            last["sg"] = k
            yield
            i, ps, wb = self.banks.take()
            for q in range(4):
                kk = pe.mm(ps[:, q * 128:(q + 1) * 128], xc[:, q * 128:(q + 1) * 128], w3["ssm_out"], w=[k] + wb)
            last["out"] = kk
            yield
            k = d.cp(self.s[:, 4 * j:4 * j + 4, :], ps.rearrange("p (r c) -> p r c", c=C), w=[kk, self.k_ffn_logits])
            self.banks.give(i, k)
            i, ps, wb = self.banks.take()
            for q in range(4):
                kk = pe.mm(ps[:, q * 128:(q + 1) * 128], tile(4 * j + q), w3["gate"], w=wb)
            k = act.act(self.g[:, 4 * j:4 * j + 4, :], ps.rearrange("p (r c) -> p r c", c=C), ACT.Sigmoid, w=[kk])
            self.banks.give(i, k)

    def layer3_attention(self):
        pe, d, act, pool, sp, w3, c = self.pe, self.dve, self.act, self.pool, self.sp, self.w3, self.c
        p = self.p
        ROWS = 96
        HALF = 8 * NS
        wk, qs, ks, put = self.work, self.qs, self.ks, self.k_put
        w2s, beyond = self.w2.tensor, self.r3.start + self.r3.width
        free = [self.tT[:, 512 * n:512 * n + 512] for n in range(4)] + [w2s[:, 512 * n:512 * n + 512] for n in range(3)]
        PT = free + [self.w3.tensor[:, beyond:beyond + 512]]
        Vs = [wk[:, 8192 + 1024 * n:9216 + 1024 * n].rearrange("p (r h x) -> p r h x", r=2, h=16) for n in range(2)]
        spare = wk[:, 10240:10496]
        resid, mx, den = spare[0:16, 0:128], spare[:, 128:160], spare[:, 160:176]
        xt = self.xT[:, :, :].rearrange("p b n -> p (b n)")
        oT = [xt[:, 512 * n:512 * n + 512] for n in range(2)]
        ot = xt[:, 1024:1280].rearrange("p (r c) -> p r c", r=2)
        otT = xt[:, 1280:1536]
        mparts = [xt[0:16, 1536 + 192 * n:1728 + 192 * n].bitcast(BF16).rearrange("p (q n) -> p q n", q=3) for n in range(2)]
        scale = float(np.float32(8.0) ** np.float32(-0.5))
        ch_max = [[p.channel(f"ch_max{b}{h}", sp) for h in range(2)] for b in range(2)]

        steps = self.att
        since, did, last, load_heads = steps.since, steps.did, steps.last, self.load_heads

        def pass1(par, h):
            half = h // 8
            i, ps, wb = self.banks.take()
            for r in range(2):
                k = pe.mm(ps[:, r * NS:(r + 1) * NS], qs[par][0:ROWS, h * NS + r * 128:h * NS + r * 128 + 128],
                          ks[par][0:ROWS, h * NS:(h + 1) * NS], w=[since(("load", par, half))] + wb, inc=(r == 1))
            did(("pass1", par, half), k)
            src = ps.rearrange("p (r n) -> p r n", r=2)
            a = (h % 8) * 2
            d.wait([k, since(("mxT", half))])
            k = d.put(lambda: d.eng.tensor_reduce(mx[:, 16 * half + a:16 * half + a + 2], src, AX, ALU.max, negate=True))
            self.banks.give(i, k)
            did(("mx", half), k)

        def maxima(par, half):
            mp = mparts[half]
            i, ps, wb = self.banks.take()
            m = ps[0:16, 0:128]
            k = did(("mxT", half), pe.tr(m, mx[:, 16 * half:16 * half + 16], c["ident"], w=[since(("mx", half))] + wb))
            k = d.cp(mp[:, 0, :], m, w=[k, since(("max", 0, half)), since(("max", 1, half))])
            k = d.tt(resid, m, mp[:, 0, :], ALU.subtract, w=[k])
            self.banks.give(i, k)
            k = d.cp(mp[:, 1, :], resid, w=[k])
            k = d.tt(mp[:, 2, :], resid, mp[:, 1, :], ALU.subtract, w=[k])
            for q in range(3):
                kk = sp.dma(qs[par][ROWS + q:ROWS + q + 1, half * HALF:(half + 1) * HALF], mp[:, q, :], ch_max[par][half], w=[k])
            did(("max", par, half), kk)

        def values(b, par):
            src = self.t1[:, bass.ds(2 * b, 2), :].rearrange("p r (h x) -> p r h x", h=16)
            did(("V", par), pool.cp(Vs[par][:, :, :, 0:8], src, w=self.k_values + [since(("pv", par))]))

        def pass2(par, h):
            half, u = h // 8, h % 8
            i, ps, wb = self.banks.take()
            for kt in range(2):
                k = pe.mm(ps[:, kt * NS:(kt + 1) * NS], ks[par][0:ROWS + 3, h * NS + kt * 128:h * NS + kt * 128 + 128],
                          qs[par][0:ROWS + 3, h * NS:(h + 1) * NS], w=[since(("load", par, half)), since(("max", par, half))] + wb,
                          inc=(kt == 1))
            did(("pass2", par, half), k)
            k = act.act(PT[u], ps, ACT.Exp, scale=scale, w=[k, since(("used", u))])
            self.banks.give(i, k)
            did(("exp", u), k)

        def product(par, g4):
            po = self.banks.ps[:, 7 * 512:8 * 512]
            o = po[:, (g4 % 2) * NS:(g4 % 2 + 1) * NS]
            for g in range(4):
                u = (4 * g4 + g) % 8
                for kt in range(2):
                    k = pe.mm(o[32 * g:32 * g + 32, :], Vs[par][:, kt, 4 * g4 + g, :], PT[u][:, kt * NS:(kt + 1) * NS],
                              first=(kt == 0), last=(kt == 1), w=[since(("exp", u)), since(("V", par)), since("po")])
                did(("used", u), k)
            did(("pv", par), k)
            if g4 % 2:
                half = g4 // 2
                k = act.act(oT[half], po, ACT.Copy, w=[k, since(("oTtr", half))])
                did("po", k)
                did(("oT", half), k)

        def divide(half):
            i, ps, wb = self.banks.take()
            for a in range(2):
                for r in range(2):
                    x = (2 * a + r) * 128
                    k = pe.tr(ps[:, x:x + 128], oT[half][:, a * NS + r * 128:a * NS + r * 128 + 128], c["ident"],
                              w=[since(("oT", half))] + wb, inc=(x == 384))
            did(("oTtr", half), k)
            s4 = ps.rearrange("p (a r g x) -> p a r g x", a=2, r=2, g=4)
            dn = den.rearrange("p (a r g) -> p a r g", a=2, r=2)
            k = d.rcp(dn, s4[:, :, :, :, 8], w=[k, since("ot")])
            for a in range(2):
                g4 = 2 * half + a
                dst = ot.rearrange("p r (h x) -> p r h x", h=16)[:, :, 4 * g4:4 * g4 + 4, :]
                kk = did("ot", d.tt(dst, s4[:, a, :, :, 0:8], dn[:, a].unsqueeze(3).broadcast_to((P, 2, 4, 8)), ALU.mult,
                                    w=[k, since("ottr")]))
            self.banks.give(i, kk)

        def turn_out():
            i, ps, wb = self.banks.take()
            for r in range(2):
                k = pe.tr(ps[:, r * 128:(r + 1) * 128], ot[:, r, :], c["ident"], w=[since("ot")] + wb, inc=(r == 1))
            did("ottr", k)
            k = did("otT", act.act(otT, ps[:, 0:256], ACT.Copy, w=[k, since("wout")]))
            self.banks.give(i, k)

        def project_out(b):
            i, ps, wb = self.banks.take()
            for r in range(2):
                k = pe.mm(ps[:, r * 128:(r + 1) * 128], otT[:, r * 128:(r + 1) * 128], w3["attn_out"],
                          w=[since("otT")] + wb, inc=(r == 1))
            did("wout", k)
            k = d.cp(self.t1[:, bass.ds(2 * b, 2), :], ps[:, 0:256].rearrange("p (r c) -> p r c", r=2),
                     w=[k, since(("V", 0)), since(("V", 1))])
            self.banks.give(i, k)

        def heads(b, par, queue, ahead=None, load=True):
            def later(n, step):
                queue.append([n, step])

            values(b, par)
            for h in range(16):
                if ahead is not None:
                    pass1(1 - par, h)
                pass2(par, h)
                for q in queue:
                    q[0] -= 1
                while queue and min(q[0] for q in queue) <= 0:
                    due = next(q for q in queue if q[0] <= 0)
                    queue.remove(due)
                    due[1]()
                half = h // 8
                if h % 8 == 7:
                    if ahead is not None:
                        later(1, lambda half=half: maxima(1 - par, half))
                    if load:
                        load_heads(b + 2, par, half)
                if h % 4 == 3:
                    later(2, lambda g4=h // 4: product(par, g4))
                    if h % 8 == 7:
                        later(4, lambda half=half: divide(half))
                    if h == 15:
                        later(6, turn_out)
                        later(8, lambda: project_out(b))

        def flush(queue):
            for q in sorted(queue, key=lambda q: q[0]):
                q[1]()
            queue.clear()

        while 5 not in self.k_put:
            yield
        for h in range(16):
            pass1(0, h)
            yield
        yield "first maxima"
        start = [e.now() for e in (pe, d, act, pool)] + [self.k_ffn_sent]
        for e in (d, act, pool):
            e.wait(start)
        for V in Vs:
            k1 = pool.fill(V, 0.0)
            k1 = pool.fill(V[:, :, :, 8], 1.0, w=[k1])
        maxima(0, 0)
        maxima(0, 1)
        self.banks.only(7)
        pe.wait(self.banks.free[7])
        queue = []
        every = [e.now() for e in (pe, d, act, pool)] + [last[n, b, h] for n, b, h in
                 [(n, b, h) for n in ("load",) for b in range(2) for h in range(2)] + [("max", 0, 0), ("max", 0, 1)]]
        for e in (pe, d, act, pool, sp):
            e.wait(every + [put[u] for u in range(5, 8)])

        def body(i, lp):
            queue = []
            last.clear()
            for par in range(2):
                heads(2 * i + par, par, queue, ahead=2 * i + par + 1)
            flush(queue)

        self.preset(ACT.Exp)
        self.banks.run_loop(3, body)
        for par in range(2):
            heads(6 + par, par, queue, ahead=7 if par == 0 else None, load=False)
        flush(queue)
        self.banks.free[7] = [last["po"]]
        self.banks.only(8)

    def layer3_ffn_route(self):
        d, act, pool, r3, w3 = self.dve, self.act, self.pool, self.r3, self.w3
        beyond = self.r3.start + self.r3.width
        rows = self.w3.tensor[:, beyond:beyond + TOK].rearrange("p (t c) -> p t c", c=C)
        rT = self.s[:, :, :].rearrange("p t c -> p (t c)")
        ms, rs = self.v[0][:, :], self.v[1][:, :]
        start = [d.now(), self.pe.now(), pool.now()]
        for t in range(NT):
            k = act.act(rows[:, t, :], self.xn[:, t, :], ACT.Square, w=start, acc=ms[:, t:t + 1])
        yield
        k = d.ts(ms, ms, 1.0 / C, EPS, ALU.mult, ALU.add, w=[k])
        k = self.rsqrt(rs, ms, [k])
        for t in range(NT):
            kk = d.stt(rows[:, t, :], self.xn[:, t, :], rs[:, t:t + 1], r3["norm"], ALU.mult, ALU.mult, w=[k] + self.k_w3)
        yield
        kT = self.transposed(rows, lambda q: rT[:, q * 512:(q + 1) * 512], [kk], w_dst=start)
        lg = self.k8[0][:, :, :]
        yield
        k = self.logits(lambda t: rT[:, t * 128:(t + 1) * 128], w3["gate_w"], r3["gate_b"], lg, kT)
        self.k_ffn_logits = k
        yield
        oh, m, k = self.top2(lg, [k])
        yield
        self.use_route(1)
        k = self.pair_softmax(m, self.gates[:, 0, :], self.gates[:, 1, :], [k])
        k, kt = self.slots(oh, [k])
        self.k_ffn_sent = self.dispatch(rows, self.xs[3], 2, [self.k_clear[3]], [k])
        self.use_route(0)

    def layer3_route(self, k):
        d, act, r3, w3 = self.dve, self.act, self.r3, self.w3
        s, t1, g = self.s, self.t1, self.g
        k_in = [k, act.now()]

        def blend(e, a, b):
            s_, t_ = s[:, a:b, :], t1[:, a:b, :]
            k = e.tt(t_, t_, g[:, a:b, :], ALU.mult, w=k_in)
            k = e.tt(t_, t_, s_, ALU.subtract, w=[k])
            k = e.tt(t_, t_, grow_in(self.alpha[:, a:b], C), ALU.mult, w=[k])
            k = e.tt(s_, s_, t_, ALU.add, w=[k])
            k = e.tt(s_, s_, grow(r3["ls1"], b - a), ALU.mult, w=[k])
            return e.tt(s_, s_, self.xn[:, a:b, :], ALU.add, w=[k])

        k = self.split(blend)
        k = self.layernorm(s, t1, lambda t: [k], r3["ln2_g"], r3["ln2_b"])
        kT = self.transposed(t1, lambda q: self.tT[:, q * 512:(q + 1) * 512], [k], w_dst=[self.pe.now()])
        lg = self.k8[0][:, :, :]
        zero8 = self.zero[:, 0:8]
        k = self.logits(lambda t: self.tT[:, t * 128:(t + 1) * 128], w3["router"], zero8, lg, kT)
        oh, m, k = self.top2(lg, [k])
        Z, p2, sm = self.v[0][:, :], self.v[1][:, :], self.v[2][:, :]
        k1 = d.tt(lg, lg, grow_in(m[0], E), ALU.subtract, w=[k])
        k2 = d.tt(p2, m[1], m[0], ALU.subtract, w=[k])
        k1 = act.act(lg, lg, ACT.Exp, w=[k1])
        k2 = act.act(p2, p2, ACT.Exp, w=[k2])
        k = d.red(Z, lg, ALU.add, w=[k1])
        k = d.rcp(Z, Z, w=[k])
        k = d.tt(p2, p2, Z, ALU.mult, w=[k, k2])
        k = d.tt(sm, p2, Z, ALU.add, w=[k])
        k = d.ts(sm, sm, 1e-8, op0=ALU.add, w=[k])
        k = d.rcp(sm, sm, w=[k])
        k1 = d.tt(self.gates[:, 0, :], Z, sm, ALU.mult, w=[k])
        k2 = d.tt(self.gates[:, 1, :], p2, sm, ALU.mult, w=[k])
        k, kt = self.slots(oh, [k1, k2])
        self.k_mix_sent = self.dispatch(t1, self.xs[2], 2, [self.k_clear[2]], [k])

    def layer3_ffn_experts(self):
        d, act, r3, w3 = self.dve, self.act, self.r3, self.w3
        b1 = r3["mlp1_b"]
        ALPHA = 1.702

        def mid(net, u, ps, ex, k, since):
            d.wait([k, since("a")])
            k = d.put(lambda: d.eng.tensor_tensor(net.hm[u], ps, b1[:, bass.ds(ex * 512, 512)], ALU.add))
            k1 = d.ts(net.hm[u][:, 0:256], net.hm[u][:, 0:256], 7.0, op0=ALU.min, w=[k])
            k2 = d.ts(net.hm[u][:, 256:512], net.hm[u][:, 256:512], 7.0, -7.0, ALU.min, ALU.max, w=[k])
            return act.act(net.ha[u][:, 256:512], net.hm[u][:, 0:256], ACT.Silu, scale=ALPHA, w=[k1, k2, since("a")])

        def mid_end(net, u, ps, k, since):
            return d.stt(net.ha[u][:, 0:256], net.hm[u][:, 256:512], 1.0, net.ha[u][:, 256:512], ALU.add, ALU.mult,
                         w=[k, since("trm")])

        self.use_route(1)
        ko = self.experts(self.xs[3], self.ys[3], 40, [self.k_ffn_sent] + [e.now() for e in (self.pe, d, act)], mid,
                          ACT.Silu, 512, 2, w3["mlp1"], w3["mlp2"], b1, r3["mlp2_b"], yscale=1.0 / ALPHA, mid_end=mid_end)
        xt = self.xT[:, :, :].rearrange("p b n -> p (b n)")[:, 0:NT * C]
        self.ffn_rows = [a.rearrange("p (t c) -> p t c", c=C) for a in (xt, self.tT[:, :])]
        self.k_ffn_got = self.collect(self.ffn_rows, self.ys[3], [0, 1], ko + [d.now(), act.now(), self.pe.now()],
                                      self.ch_got2)
        self.use_route(0)

    def layer3_experts(self):
        d, act, r3, w3 = self.dve, self.act, self.r3, self.w3
        s, t1 = self.s, self.t1

        def mid(net, u, ps, ex, k, since):
            return act.act(net.hm[u][:, 0:256], ps[:, 0:256], ACT.Silu, w=[k, since("a")])

        def mid_end(net, u, ps, k, since):
            return d.tt(net.ha[u][:, 0:256], net.hm[u][:, 0:256], ps[:, 256:512], ALU.mult, w=[k, since("trm")])

        ko = self.experts(self.xs[2], self.ys[2], 40, [self.k_mix_sent] + [e.now() for e in (self.pe, d, act)], mid,
                          ACT.Silu, 512, 2, w3["w13"], w3["w2"], mid_end=mid_end)
        both = [self.work[:, n * 2048:(n + 1) * 2048].rearrange("p (t c) -> p t c", c=C) for n in range(2)]
        kc = self.collect(both, self.ys[2], [0, 1], ko + [d.now(), act.now(), self.pe.now()])
        self.use_route(1)
        k = self.weighted(self.g, self.ffn_rows, self.k_ffn_got, self.xn)
        k_silu = act.act(self.g[:, :, :], self.g[:, :, :], ACT.Silu, w=[k])
        self.use_route(0)

        def end(q, k):
            a = lambda x: x[:, 4 * q:4 * q + 4, :]
            k = d.tt(a(t1), a(t1), grow(r3["ls2"], 4), ALU.mult, w=[k])
            k = d.tt(a(s), a(s), a(t1), ALU.add, w=[k])
            k = d.tt(a(s), a(s), grow_in(self.wsum[:, 4 * q:4 * q + 4], C), ALU.mult, w=[k])
            k = d.tt(a(s), a(s), a(self.xn), ALU.add, w=[k])
            k = d.tt(a(s), a(s), a(self.g), ALU.mult, w=[k, k_silu])
            k = d.tt(a(self.x), a(self.x), a(s), ALU.add, w=[k])
            self.k_out.append(self.sp.dma(self.out[:, 4 * q:4 * q + 4, :], a(self.x), self.p.channel(f"ch_out_x{q}", self.sp),
                                          w=[k]))
            return k

        self.k_out = []
        return self.weighted(t1, both, kc, then=end)

    def layer3(self):
        self.normed(turned=False)
        self.layer3_inputs()
        attention = self.layer3_attention()
        weave([self.layer3_ffn_route()], [self.layer3_parts()], [self.layer3_gates()], [until(attention, "first maxima")])
        weave([attention])
        self.layer3_route(self.dve.now())
        self.layer3_ffn_experts()
        return self.layer3_experts()


def build(nc, ins, out):
    n = Net(nc, ins)
    n.out = out.rearrange("(t p) c -> p t c", p=P)
    n.start()
    n.layer0()
    n.layer1()
    n.load_layer3()
    n.layer2()
    n.layer3()
    n.sp.wait(n.k_out + [e.now() for e in n.p.engines[:4]])
    return n


def constants():
    f = np.float32
    i = np.arange(P)
    t = {"ident": np.eye(P), "ones": np.ones((P, P)), "before": (i[:, None] < i[None, :]),
         "swap": (i[:, None] == (i[None, :] + 64) % P)}
    channel = np.where(i < 64, 2 * i, 2 * (i - 64) + 1)
    t["heads"] = (channel[:, None] // 16 == np.arange(8)[None, :]) / f(NS)
    t["kv_mask"] = (i[:, None] // 16 == i[None, :] // 16) / np.sqrt(f(NS))
    n = np.arange(NS, dtype=f)
    theta = f(1.0) / f(10000.0) ** (np.arange(64, dtype=f) / f(64))
    ang = (n[:, None] * theta).T
    t["rope_cos"] = np.concatenate([np.cos(ang)] * 2)
    t["rope_sin"] = np.concatenate([-np.sin(ang), np.sin(ang)])
    rot = np.eye(P)
    rot[2 * np.arange(64) + 1, 2 * np.arange(64)] = -1
    rot[2 * np.arange(64), 2 * np.arange(64) + 1] = 1
    t["rot2"] = rot
    inv = f(10000.0) ** (np.arange(0, 64, 2, dtype=f) / f(64))
    rad = n[:, None] / inv
    t["rope2"] = np.repeat(np.stack((np.sin(rad), np.cos(rad)), axis=-1).reshape(NS, -1), 2, axis=-1).T
    t["iota8"] = np.tile(np.arange(8), (P, 1))
    t["iota384"] = np.tile(np.arange(8) * 384, (P, 1))
    t["tile_start"] = np.tile((np.arange(TILES) - LEAD) * P, (P, 1))
    t["tile_third"] = np.tile(np.clip((np.arange(TILES) - LEAD) // 3, 0, 7), (P, 1))
    t["octal"] = np.tile(8 ** np.arange(4), (P, 1))
    t["scan_mask"] = np.tile(i % NT != 0, (P, 1))
    t["quarters"] = np.tile((4.0 ** np.arange(14, -1, -1)[:, None] * np.array([1, 2, 3])).reshape(-1), (P, 1))
    return t


def packed(fields, values):
    return np.ascontiguousarray(np.concatenate([np.asarray(values[n], np.float32).reshape(-1, w) for n, w in fields], axis=1))


def lay_out(a):
    T = np.transpose
    even_first = np.r_[0:C:2, 1:C:2]
    o = {"x": a["L0_attn_x"].reshape(TOK, C), "consts": packed(CONSTS, constants())}
    g = lambda p: (lambda n: np.asarray(a[p + n]))
    A, B = g("L0_attn_"), g("L0_ffn_")
    o["w0"] = packed(W0, {
        "q": A("qk_w")[:, :C][:, even_first], "k": A("qk_w")[:, C:][:, even_first],
        "lepe": T(A("lepe_w"), (1, 0, 2)).reshape(C, 384), "qkv": B("in_proj_w").T, "out": B("out_w").T,
        "router": B("router_w").T, "q_b": A("qk_b")[:C][even_first][:, None], "k_b": A("qk_b")[C:][even_first][:, None],
        "w1": T(B("w1"), (2, 0, 1)).reshape(C, 1024), "w2": T(B("w2"), (2, 0, 1)).reshape(C, 1024)})
    o["r0"] = packed(R0, {"lepe_b": A("lepe_b"), "qkv_b": B("in_proj_b"), "out_b": B("out_b"), "ln1_g": B("ln1_g"),
                          "ln1_b": B("ln1_b"), "ln2_g": B("ln2_g"), "ln2_b": B("ln2_b"), "router_b": B("router_b"),
                          "b1": B("b1"), "b2": B("b2")})
    A, B = g("L1_attn_"), g("L1_ffn_")
    o["w1"] = packed(W1, {
        "hidden": A("W_hidden"), "qk": A("W_qk"), "out": T(A("W_out").reshape(2, C, C), (1, 0, 2)).reshape(C, 256),
        "router": B("Wr"), "ln_g": A("ln_scale")[:, None], "ln_b": A("ln_bias")[:, None], "qk_b": A("b_qk")[:, None],
        "osw": A("os_weight").T, "osb": A("os_bias").T, "w1": T(B("W1"), (1, 0, 2)).reshape(C, 4096),
        "w2": T(B("W2").reshape(E, 4, C, C), (2, 0, 1, 3)).reshape(C, 4096)})
    o["r1"] = packed(R1, {"hidden_b": A("b_hidden"), "out_b": A("b_out"), "router_b": B("br"), "gamma": B("gamma"),
                          "beta": B("beta"), "b1": B("b1"), "b2": B("b2")})
    A, B = g("L2_attn_"), g("L2_ffn_")
    o["w2"] = packed(W2, {
        "wq": A("Wq"), "wk": A("Wk"), "wv": A("Wv").T, "wf": B("wf").T, "wi": B("wi").T, "wc": B("wc").T,
        "uf": B("uf").T, "ui": B("ui").T, "uc": B("uc").T, "wo": B("wo").T, "uo": B("uo").T,
        "bq": A("bq")[:, None], "bk": A("bk")[:, None], "bf": B("bf")[:, None], "bi": B("bi")[:, None],
        "bc": B("bc")[:, None], "c0": B("in_c")[:, None]})
    o["r2"] = packed(R2, {"bv": A("bv"), "bo": B("bo")})
    A, B = g("L3_attn_"), g("L3_ffn_")

    qkv = A("Wqkv")
    w13 = np.stack([T(A("W1"), (1, 0, 2)), T(A("W3"), (1, 0, 2))], axis=2).reshape(C, 4096)
    halves = np.r_[0:512:2, 1:512:2]
    o["w3"] = packed(W3, {
        "q": qkv[:, 0:C], "k": qkv[:, C:2 * C], "v": qkv[:, 2 * C:], "gate": A("Wgate"),
        "ssm": A("Win_ssm"), "ssm_out": A("Wout_ssm"), "attn_out": A("Wout"), "halt": A("Wr"), "router": A("Wg"),
        "gate_w": B("gate_w"), "ln_g": A("ln1_g")[:, None], "ln_b": A("ln1_b")[:, None],
        "conv_w": A("conv_w").reshape(C, 4), "conv_b": A("conv_b")[:, None], "w13": w13,
        "w2": T(A("W2").reshape(E, 2, C, C), (2, 0, 1, 3)).reshape(C, 2048),
        "mlp1": T(B("mlp1_w")[:, :, halves], (1, 0, 2)).reshape(C, 4096),
        "mlp2": T(B("mlp2_w").reshape(E, 2, C, C), (2, 0, 1, 3)).reshape(C, 2048)})
    o["r3"] = packed(R3, {"ln2_g": A("ln2_g"), "ln2_b": A("ln2_b"), "ls1": A("ls1"), "ls2": A("ls2"),
                          "halt_b": A("br"), "step_b": A("step_bias"), "norm": B("norm_scale"), "gate_b": B("gate_b"),
                          "mlp1_b": B("mlp1_b")[:, halves], "mlp2_b": B("mlp2_b")})
    return o


def kernel(**inputs):
    import concourse.bacc as bacc
    from concourse.bass_utils import run_bass_kernel_spmd

    nc = bacc.Bacc("TRN2", target_bir_lowering=False, num_devices=1)
    arrays = {f"in_{k}": np.ascontiguousarray(v) for k, v in lay_out({k: np.asarray(v) for k, v in inputs.items()}).items()}
    ins = {k[3:]: nc.dram_tensor(k, v.shape, F32, kind="ExternalInput").ap() for k, v in arrays.items()}
    out = nc.dram_tensor("out", (TOK, C), F32, kind="ExternalOutput").ap()
    build(nc, ins, out)
    r = run_bass_kernel_spmd(nc, [arrays], core_ids=[0])
    return r.results[0]["out"].reshape(NB, NS, C)
```
